# Optimizing a Trainium2 kernel written in Bass

```python
import numpy as np
import jax
import jax.numpy as jnp

def _softmax(x, axis=-1):
    return jax.nn.softmax(x, axis=axis)

def _gelu(x):
    return jax.nn.gelu(x, approximate=True)

def _silu(x):
    return jax.nn.silu(x)

def _sigmoid(x):
    return jax.nn.sigmoid(x)

def _layernorm(x, axis=-1, eps=1e-05):
    m = jnp.mean(x, axis=axis, keepdims=True)
    v = jnp.var(x, axis=axis, keepdims=True)
    return (x - m) / jnp.sqrt(v + eps)

def _scatter_add(tgt, idx, src, axis=0):
    return tgt.at[idx].add(src)

def _segment_sum(src, seg, n):
    return jax.ops.segment_sum(src, seg, n)
kernel_name = 'mk_gnn_resnorm_d2_gnn_r8_b1e5bc'

def setup_inputs(seed: int=0):
    np.random.seed(seed)
    _w = jnp.asarray

    def _rec_inputs():
        import jax
        import jax.numpy as jnp
        _gk = jax.random.key(seed)
        x = -0.000202 + 1 * jax.random.normal(jax.random.fold_in(_gk, 1), (6250, 128), jnp.float32)
        _s = jax.random.randint(jax.random.fold_in(_gk, 2), (50000,), 0, 6250, jnp.int32)
        _d = jax.random.randint(jax.random.fold_in(_gk, 3), (50000,), 0, 6250, jnp.int32)
        _loop = jnp.arange(6250, dtype=jnp.int32)
        src = jnp.concatenate([_s, _d, _loop])
        dst = jnp.concatenate([_d, _s, _loop])
        _o = jnp.argsort(dst, stable=True)
        src = src[_o]
        dst = dst[_o]
        edge_attr_64 = 0.000102155 + 1.00015 * jax.random.normal(jax.random.fold_in(_gk, 12), (106250, 64), jnp.float32)
        edge_weight = jax.random.uniform(jax.random.fold_in(_gk, 14), (106250,), jnp.float32, 0.0, 0.999999)
        return (x, src, dst, edge_attr_64, edge_weight)
    x, src, dst, edge_attr_64, edge_weight = _rec_inputs()

    def _L0_gnn_setup():
        import jax, jax.numpy as jnp
        import numpy as np
        N_NODES = 6250
        N_EDGES = 200000
        IN_CH = 128
        HEAD = 8
        OUT_CH = 16
        LEAKY_ALPHA = 0.3
        key = jax.random.key(seed)
        k1, k2, k3, k4, k5, k6 = jax.random.split(key, 6)
        x = jax.random.normal(k1, (N_NODES, IN_CH), dtype=jnp.float32)
        w1 = jax.random.normal(k2, (IN_CH, HEAD * OUT_CH), dtype=jnp.float32) * (1.0 / np.sqrt(IN_CH))
        w2 = jax.random.normal(k3, (IN_CH, HEAD * OUT_CH), dtype=jnp.float32) * (1.0 / np.sqrt(IN_CH))
        a = jax.random.normal(k4, (1, HEAD * OUT_CH), dtype=jnp.float32) * 0.1
        src = jax.random.randint(k5, (N_EDGES,), 0, N_NODES, dtype=jnp.int32)
        tgt = jax.random.randint(k6, (N_EDGES,), 0, N_NODES, dtype=jnp.int32)
        return {'x': x, 'w1': w1, 'w2': w2, 'a': a, 'src': src, 'tgt': tgt}
    _L0_gnn_all = _L0_gnn_setup()
    _L0_gnn_in = {k: v for k, v in _L0_gnn_all.items() if k in ('w1', 'w2', 'a')}
    del _L0_gnn_all

    def _L1_gnn_setup():
        import jax, jax.numpy as jnp
        import numpy as np
        N_NODES = 12500
        N_EDGES = 62500
        IN_CH = 128
        EDGE_CH = 64

        def _glorot(key, shape):
            fan_in, fan_out = (shape[0], shape[1])
            lim = (6.0 / (fan_in + fan_out)) ** 0.5
            return jax.random.uniform(key, shape, jnp.float32, -lim, lim)
        key = jax.random.key(seed)
        ks = jax.random.split(key, 14)
        x = jax.random.normal(ks[0], (N_NODES, IN_CH), jnp.float32)
        edge_index = jax.random.randint(ks[1], (2, N_EDGES), 0, N_NODES, jnp.int64)
        edge_attr = jax.random.normal(ks[2], (N_EDGES, EDGE_CH), jnp.float32)
        timestamps = jax.random.uniform(ks[3], (N_EDGES,), jnp.float32)
        We1 = _glorot(ks[4], (EDGE_CH, 2 * EDGE_CH))
        be1 = jnp.zeros((2 * EDGE_CH,), jnp.float32)
        We2 = _glorot(ks[5], (2 * EDGE_CH, IN_CH))
        be2 = jnp.zeros((IN_CH,), jnp.float32)
        Wt = _glorot(ks[6], (1, IN_CH))
        bt = jnp.zeros((IN_CH,), jnp.float32)
        Wn1 = _glorot(ks[7], (2 * IN_CH, IN_CH))
        bn1 = jnp.zeros((IN_CH,), jnp.float32)
        Wn2 = _glorot(ks[8], (IN_CH, IN_CH))
        bn2 = jnp.zeros((IN_CH,), jnp.float32)
        return {'x': x, 'edge_index': edge_index, 'edge_attr': edge_attr, 'timestamps': timestamps, 'We1': We1, 'be1': be1, 'We2': We2, 'be2': be2, 'Wt': Wt, 'bt': bt, 'Wn1': Wn1, 'bn1': bn1, 'Wn2': Wn2, 'bn2': bn2}
    _L1_gnn_all = _L1_gnn_setup()
    _L1_gnn_in = {k: v for k, v in _L1_gnn_all.items() if k in ('We1', 'be1', 'We2', 'be2', 'Wt', 'bt', 'Wn1', 'bn1', 'Wn2', 'bn2')}
    del _L1_gnn_all
    return {'x': x, 'src': src, 'dst': dst, 'edge_attr_64': edge_attr_64, 'edge_weight': edge_weight, 'L0_gnn_w1': _L0_gnn_in['w1'], 'L0_gnn_w2': _L0_gnn_in['w2'], 'L0_gnn_a': _L0_gnn_in['a'], 'L1_gnn_We1': _L1_gnn_in['We1'], 'L1_gnn_be1': _L1_gnn_in['be1'], 'L1_gnn_We2': _L1_gnn_in['We2'], 'L1_gnn_be2': _L1_gnn_in['be2'], 'L1_gnn_Wt': _L1_gnn_in['Wt'], 'L1_gnn_bt': _L1_gnn_in['bt'], 'L1_gnn_Wn1': _L1_gnn_in['Wn1'], 'L1_gnn_bn1': _L1_gnn_in['bn1'], 'L1_gnn_Wn2': _L1_gnn_in['Wn2'], 'L1_gnn_bn2': _L1_gnn_in['bn2']}

def reference(x, src, dst, edge_attr_64, edge_weight, L0_gnn_w1, L0_gnn_w2, L0_gnn_a, L1_gnn_We1, L1_gnn_be1, L1_gnn_We2, L1_gnn_be2, L1_gnn_Wt, L1_gnn_bt, L1_gnn_Wn1, L1_gnn_bn1, L1_gnn_Wn2, L1_gnn_bn2):
    import jax
    import jax.numpy as jnp

    def _L0_gnn_ref(x, w1, w2, a, src, tgt):
        import jax, jax.numpy as jnp
        import numpy as np
        N_NODES = 6250
        N_EDGES = 200000
        IN_CH = 128
        HEAD = 8
        OUT_CH = 16
        LEAKY_ALPHA = 0.3
        hi = x[src] @ w1
        hj = x[tgt] @ w2
        e = jax.nn.leaky_relu(hi + hj, negative_slope=LEAKY_ALPHA)
        e = e * a
        logits = e.reshape(-1, HEAD, OUT_CH).sum(axis=-1)
        seg_max = jax.ops.segment_max(logits, tgt, num_segments=N_NODES)
        seg_max = jnp.where(jnp.isfinite(seg_max), seg_max, 0.0)
        exp = jnp.exp(logits - seg_max[tgt])
        seg_sum = jax.ops.segment_sum(exp, tgt, num_segments=N_NODES)
        attn = exp / seg_sum[tgt]
        msg = hi.reshape(-1, HEAD, OUT_CH) * attn[:, :, None]
        out = jax.ops.segment_sum(msg, tgt, num_segments=N_NODES)
        return out.reshape(N_NODES, HEAD * OUT_CH)

    def _L1_gnn_ref(x, edge_index, edge_attr, timestamps, We1, be1, We2, be2, Wt, bt, Wn1, bn1, Wn2, bn2):
        import jax, jax.numpy as jnp
        import numpy as np
        N_NODES = 12500
        N_EDGES = 62500
        IN_CH = 128
        EDGE_CH = 64

        def _glorot(key, shape):
            fan_in, fan_out = (shape[0], shape[1])
            lim = (6.0 / (fan_in + fan_out)) ** 0.5
            return jax.random.uniform(key, shape, jnp.float32, -lim, lim)
        ts = timestamps[:, None]
        ef = jax.nn.relu(edge_attr @ We1 + be1) @ We2 + be2
        tw = jax.nn.sigmoid(ts @ Wt + bt)
        ef = ef * tw
        row, col = (edge_index[0], edge_index[1])
        combined = jnp.concatenate([x[row], ef], axis=1)
        msg = jax.nn.relu(combined @ Wn1 + bn1) @ Wn2 + bn2
        out = jax.ops.segment_sum(msg, col, num_segments=x.shape[0])
        return out + x
    edge_index = jnp.stack([src, dst])
    x = _layernorm(x + _L0_gnn_ref(x, L0_gnn_w1, L0_gnn_w2, L0_gnn_a, src, dst), axis=-1)
    x = _layernorm(x + _L1_gnn_ref(x, edge_index, edge_attr_64, edge_weight, L1_gnn_We1, L1_gnn_be1, L1_gnn_We2, L1_gnn_be2, L1_gnn_Wt, L1_gnn_bt, L1_gnn_Wn1, L1_gnn_bn1, L1_gnn_Wn2, L1_gnn_bn2), axis=-1)
    return x

_drawn_inputs = setup_inputs


def setup_inputs(seed=0):
    import zlib

    import numpy as np

    out = dict(_drawn_inputs(seed))
    spreads = {'L1_gnn_be1': (0.0, 0.369),
     'L1_gnn_be2': (0.0, 0.1),
     'L1_gnn_bt': (0.0, 0.735),
     'L1_gnn_bn1': (0.0, 0.1),
     'L1_gnn_bn2': (0.0, 0.1)}
    factors = {'edge_weight': 8.0, 'L0_gnn_w2': 11.285, 'L1_gnn_Wt': 7.94}
    for name, (base, spread) in spreads.items():
        noise = np.random.default_rng([zlib.crc32(name.encode()), seed]).standard_normal(out[name].shape)
        drawn = base * np.exp(spread * noise) if base else spread * noise
        out[name] = jnp.asarray(drawn.astype(out[name].dtype))
    for name, factor in factors.items():
        out[name] = (out[name] * factor).astype(out[name].dtype)
    return out
```

```python
from contextlib import ExitStack

import concourse.bass as bass
from concourse import mybir

ALU = mybir.AluOpType
ACT = mybir.ActivationFunctionType
F32 = mybir.dt.float32
BF16 = mybir.dt.bfloat16
I32 = mybir.dt.int32

P = 128
C = 128
NODES = 6250
EDGES = 106250
HEADS = 8
HC = C // HEADS
EC = 64
NB = -(-NODES // P)
NCH = 7
NC = NB // NCH
QE = 512
NQ = -(-EDGES // QE)
QP = NQ // 2
TAIL = EDGES - (NQ - 1) * QE
GQ, GT = 3, 12
NG = -(-NQ // GQ)
LASTQ = NQ - (NG - 1) * GQ
W = 64
NP = 6400
HALO = 2
BT = GT + 2 * HALO
LT_TILES = (NG - 1) * GT + BT
NO_NODE = 30000
BIG = float(2 ** 100)
EPS = 1e-5
RB = 4
assert NCH * NC == NB and 2 * QP == NQ and NQ % RB == 0


def is_int(v):
    return isinstance(v, int)


def need(eng, sem, value):
    if is_int(value) and value <= 0:
        return
    eng.wait_ge(sem, value)


def build(nc, x, src, dst, attr, ew, w1, w2, a, We1, be1, We2, be2, Wt, bt, Wn1, bn1, Wn2, bn2,
          hi_d, y_d, rel_d, scan_d, out):
    with ExitStack() as ctx:
        def sb(name, shape, dt=F32):
            return ctx.enter_context(nc.sbuf_tensor(name, shape, dt))

        def sem(name):
            return ctx.enter_context(nc.semaphore(name))

        T = sb("T", [P, 2 * NB, 3, C], BF16)
        acc = sb("acc", [P, 2, NP])
        L = sb("L", [P, 3, BT * HEADS])
        G = sb("G", [P, 3, GT * C])
        Dbc = sb("Dbc", [P, 3, GT * P], BF16)
        ohT = sb("ohT", [P, GQ, QE], BF16)
        oh = sb("oh", [P, GT * W])
        msg = sb("msg", [P, GT * C])
        V = sb("V", [P, GQ, QE])
        E = sb("E", [P, GQ, QE])
        Dsc = sb("Dsc", [BT, 3, P + 1])
        X16 = sb("X16", [BT, P])
        XH = sb("XH", [HEADS, P])
        link = sb("link", [P, P + 1])
        R1 = sb("R1", [P, P])
        R2 = sb("R2", [P, P])
        R3 = sb("R3", [P, P])
        R4 = sb("R4", [P, P])
        XM = sb("XM", [P, P])
        EXT = sb("EXT", [P, P])
        EXs = sb("EXs", [P, GT * HEADS])
        R64 = sb("R64", [P, NQ * 4])
        IDX = sb("IDX", [P, NQ * 4], I32)
        idx = sb("idx", [P, 4, GT], I32)
        baseR = sb("baseR", [1, NQ], I32)
        tabR = sb("tabR", [1, NQ], I32)
        ident = sb("ident", [P, P])
        down = sb("down", [P, P])
        up = sb("up", [P, P])
        iotaI = sb("iotaI", [P, W], I32)
        iotaF = sb("iotaF", [P, W])
        pI = sb("pI", [P, 1], I32)
        pF = sb("pF", [P, 1])
        ones = sb("ones", [P, 1])
        Aw = sb("Aw", [P, HEADS])
        cols = sb("cols", [P, 8])
        W12 = sb("W12", [P, 2 * C])
        wE1 = sb("wE1", [EC, C])
        wE2 = sb("wE2", [P, C])
        wN1 = sb("wN1", [P, 2, C])
        wN2 = sb("wN2", [P, C])
        bn1B = sb("bn1B", [P, C])
        bn2R = sb("bn2R", [1, C])
        mv = sb("mv", [P, NCH, 2])
        st = sb("st", [P, NCH, 6])
        ve = sb("ve", [P, NCH])
        sd = sb("sd", [P, NCH])
        rs = sb("rs", [P, NCH])

        TF = T[:, :, :, :].rearrange("p b k c -> p (b k c)").bitcast(F32)
        xN = TF[:, 0:NB * C].rearrange("p (b c) -> p b c", b=NB)
        xT = acc[:, 0, :]
        oh2 = acc[:, 1, 0:2 * QE]
        hjr = acc[:, 1, 2 * QE:2 * QE + 4 * 2 * C].rearrange("p (r b c) -> p r b c", r=4, b=2)
        D4i = G[0:QP, 0, 0:2 * QE].bitcast(I32).rearrange("p (k e) -> p k e", k=2)
        S4i = G[0:QP, 1, 0:2 * QE].bitcast(I32).rearrange("p (k e) -> p k e", k=2)
        D4 = G[0:QP, 2, 0:2 * QE].rearrange("p (k e) -> p k e", k=2)
        S4 = msg[0:QP, 0:2 * QE].rearrange("p (k e) -> p k e", k=2)
        DR = V[0:QP, 0:2, :]
        DS = oh2[0:QP, 0:2 * QE].rearrange("p (k e) -> p k e", k=2)
        P4i = E[0:QP, 0:2, :].bitcast(I32)
        D128 = Dbc[0:QP, 0, 0:2 * QE].rearrange("p (k e) -> p k e", k=2)
        B64i = sb("B64i", [QP, 2], I32)
        B64 = sb("B64", [QP, 2])
        front = sb("front", [HALO, P])
        back = sb("back", [16, P])
        hiS = sb("hiS", [P, 4, 2, C])

        X1 = TF[:, 0:NB * C]
        T2 = TF[:, NB * C:3 * NB * C]
        CW = NCH * C
        rec = T2[:, 0:CW]
        gat = T2[:, CW:2 * CW]
        xc = T2[:, 2 * CW:3 * CW].rearrange("p (b c) -> p b c", b=NCH)
        xs = T2[:, 3 * CW:4 * CW].rearrange("p (b c) -> p b c", b=NCH)
        x1T = T2[:, 4 * CW:5 * CW]
        yS = T2[:, 5 * CW:6 * CW].rearrange("p (b c) -> p b c", b=NCH)
        x1S = T2[:, 6 * CW:7 * CW].rearrange("p (b c) -> p b c", b=NCH)
        T3 = T2[:, 7 * CW:2 * NB * C]
        Yb = T3[:, 0:RB * QE].rearrange("p (r c) -> p r c", r=RB)
        ewB = T3[:, RB * QE:2 * RB * QE].rearrange("p (r c) -> p r c", r=RB)
        atB = T3[:, 2 * RB * QE:2 * RB * QE + RB * 4 * EC].rearrange("p (r c) -> p r c", r=RB)
        atS = msg[0:EC, 0:QE]
        r1S = msg[:, QE:2 * QE]
        twS = G[:, 0, 0:QE]
        efS = G[:, 0, QE:2 * QE]
        zS = G[:, 1, 0:QE]
        hS = G[:, 1, QE:2 * QE]
        ohB = G[:, 2, 0:4 * W]
        accH = acc[:, 0, :]
        accD = acc[0:HEADS, 1, :]
        accN = acc[0:1, 1, :]

        ps = [ctx.enter_context(nc.psum_tensor(f"ps{i}", [P, 512], F32)) for i in range(8)]

        s_w = sem("weights_loaded")
        s_col = sem("columns_loaded")
        s_x = sem("x_loaded")
        s_fill = sem("fills_done")
        s_e = sem("edge_lists_loaded")
        s_row = sem("base_row_loaded")
        s_own = sem("vector_steps")
        s_tab = sem("block_columns_made")
        s_c = sem("constants_made")
        s_c2 = sem("constants_step")
        s_p = sem("prologue_vector_steps")
        s_xt = sem("x_transposed")
        s_xtc = sem("x_transposed_copied")
        s_hh = sem("projections_ready")
        s_hic = sem("hi_copied")
        s_h1 = sem("hj_first_parts")
        s_hr = sem("hj_remainders")
        s_h2 = sem("hj_second_parts")
        s_h3 = sem("hj_third_parts")
        s_odd = sem("odd_blocks_copied")
        s_hw = [sem(f"hi_written_{i}") for i in range(4)]
        s_et = sem("edge_lists_transposed")
        s_etc = sem("edge_lists_copied")
        s_sw = sem("scan_lists_written")
        s_zero = sem("accumulators_cleared")
        s_idx = sem("indices_staged")
        s_g = [sem(f"rows_gathered_{i}") for i in range(3)]
        s_db = [sem(f"block_destinations_loaded_{i}") for i in range(3)]
        s_ds = [sem(f"scan_destinations_loaded_{i}") for i in range(3)]
        s_ohT = sem("block_onehots_ready")
        s_u = sem("sums_ready")
        s_v = sem("scaled_sums_ready")
        s_lk = sem("leaky_ready")
        s_log = sem("logits_ready")
        s_lc = sem("logits_copied")
        s_lt = sem("logits_transposed")
        s_lx = sem("links_spread")
        s_mask = sem("links_ready")
        s_r1 = sem("first_scan_done")
        s_sh1 = sem("carry_down_ready")
        s_r2 = sem("second_scan_done")
        s_r3 = sem("third_scan_done")
        s_sh2 = sem("carry_up_ready")
        s_r4 = sem("fourth_scan_done")
        s_xm = sem("max_subtracted")
        s_exp = sem("exponentials_ready")
        s_ext = sem("exponentials_transposed")
        s_exs = sem("exponentials_copied")
        s_oh = sem("window_onehots_ready")
        s_msg = sem("messages_ready")
        s_agg = sem("aggregates_ready")
        s_acc = sem("aggregates_added")
        s_m = {n: sem("mid_" + n) for n in ("dx", "den", "rec", "gat", "gT", "xs", "st", "mv", "ve", "sd", "rs", "x1",
                                            "xT", "xTc", "x1c", "y", "ys", "cl")}
        s_mx = sem("mid_x_loaded")
        s_mr = sem("mid_last_rows_loaded")
        s_yw = sem("y_written")
        s_gy = [sem(f"y_gathered_{i}") for i in range(RB)]
        s_at = [sem(f"attributes_loaded_{i}") for i in range(RB)]
        s_ew = [sem(f"edge_weights_loaded_{i}") for i in range(RB)]
        s_b = {n: sem("edge_" + n) for n in ("at", "atc", "h1", "r1", "ef", "tw", "efs", "z", "zs", "h", "oh",
                                             "agg", "acc", "idx", "cl")}
        s_f = {n: sem("last_" + n) for n in ("ac", "o", "xs", "st", "mv", "ve", "sd", "rs", "x2")}
        s_out = sem("output_written")
        s_passed = {n: sem("waits_passed_" + n) for n in ("sp", "pool", "pe", "dve")}

        ctx.enter_context(nc.allow_non_contiguous_dma(reason="a few hundred words in all"))
        block = ctx.enter_context(nc.Block())

        def pair_of(pair, part, blocks):
            flat = T[:, :, :, :].rearrange("p b k c -> p b (k c)")
            if is_int(pair):
                return flat[:, 4 * pair:4 * pair + 2 * blocks:2, part * C:(part + 1) * C]
            return flat[:, bass.ds(4 * pair, blocks, 2), part * C:(part + 1) * C]

        def passed(eng, name):
            eng.sem_inc(s_passed[name], 1)

        def quads(g):
            return LASTQ if is_int(g) and g == NG - 1 else GQ

        def run_steps(eng, step):
            for g in range(3):
                step(g, g % 3, g // 3)
            turns = (NG - 1 - 3) // 3 - 1
            with_loop = 3 + 3 * turns
            with eng.Fori(0, turns) as k:
                for i in range(3):
                    step(3 * k + 3 + i, i, k + 1)
            for g in range(with_loop, NG + 2):
                step(g, g % 3, g // 3)

        def stage(g, lag):
            if is_int(g):
                return g - lag if 0 <= g - lag < NG else None
            return g - lag

        def run_chunks(eng, chunk, count):
            chunk(0)
            with eng.Fori(1, count) as c:
                chunk(c)

        def later(q, lag):
            if is_int(q):
                return q - lag if 0 <= q - lag < NQ else None
            return q - lag

        def slot(r, k, lag):
            d = r - lag
            return d % RB, k + d // RB

        def run_edges(eng, edge):
            for q in range(2 * RB):
                edge(q, q % RB, q // RB)
            with eng.Fori(2, NQ // RB - 1) as k:
                for r in range(RB):
                    edge(k * RB + r, r, k)
            for q in range(NQ - RB, NQ + 4):
                edge(q, q % RB, q // RB)

        @block.sync
        def _(sp):
            sp.dma_start(W12[:, 0:C], w1).then_inc(s_w, 16)
            sp.dma_start(W12[:, C:2 * C], w2).then_inc(s_w, 16)
            FB = NB - 1
            for c in range(NC):
                b1 = min((c + 1) * NCH, FB)
                sp.dma_start(xN[:, c * NCH:b1, :],
                             x[c * NCH * P:b1 * P, :].rearrange("(b p) c -> p b c", p=P)).then_inc(s_x, 16)
            sp.wait_ge(s_fill, 9)
            sp.dma_start(xN[0:NODES - FB * P, FB, :], x[FB * P:NODES, :]).then_inc(s_x, 16)
            for lst, t in ((dst, D4i), (src, S4i)):
                sp.dma_start(t[:, 0, :], lst[0:QP * QE].rearrange("(p e) -> p e", e=QE)).then_inc(s_e, 16)
                sp.dma_start(t[0:QP - 1, 1, :],
                             lst[QP * QE:(NQ - 1) * QE].rearrange("(p e) -> p e", e=QE)).then_inc(s_e, 16)
                sp.dma_start(t[QP - 1:QP, 1, 0:TAIL],
                             lst[(NQ - 1) * QE:EDGES].rearrange("(p e) -> p e", p=1)).then_inc(s_e, 16)
            sp.dma_start(P4i[0:1, 0, 1:QE], dst[0:QE - 1].rearrange("(p e) -> p e", p=1)).then_inc(s_e, 16)
            sp.dma_start(P4i[1:QP, 0, :],
                         dst[QE - 1:QP * QE - 1].rearrange("(p e) -> p e", e=QE)).then_inc(s_e, 16)
            sp.dma_start(P4i[0:QP - 1, 1, :],
                         dst[QP * QE - 1:(NQ - 1) * QE - 1].rearrange("(p e) -> p e", e=QE)).then_inc(s_e, 16)
            sp.dma_start(P4i[QP - 1:QP, 1, 0:TAIL + 1],
                         dst[(NQ - 1) * QE - 1:EDGES].rearrange("(p e) -> p e", p=1)).then_inc(s_e, 16)
            sp.dma_start(baseR[:, :], dst[0:(NQ - 1) * QE + 1:QE].rearrange("(p q) -> p q", p=1)).then_inc(s_row, 16)
            for i, v in enumerate((a.rearrange("o c -> (o c)"), be1, be2, Wt.rearrange("o c -> (o c)"), bt)):
                sp.dma_start(cols[:, i:i + 1], v.rearrange("(c o) -> c o", o=1)).then_inc(s_col, 16)
            sp.dma_start(wE1[:, :], We1).then_inc(s_col, 16)
            sp.dma_start(wE2[:, :], We2).then_inc(s_col, 16)
            sp.dma_start(wN1[:, :, :], Wn1.rearrange("(k p) c -> p k c", p=P)).then_inc(s_col, 16)
            sp.dma_start(wN2[:, :], Wn2).then_inc(s_col, 16)
            sp.dma_start(bn1B[:, :], bn1.rearrange("(o c) -> o c", o=1).to_broadcast([P, C])).then_inc(s_col, 16)
            sp.dma_start(bn2R[:, :], bn2.rearrange("(o c) -> o c", o=1)).then_inc(s_col, 16)
            sp.wait_ge(s_p, 1)
            H0 = HALO * P
            sp.dma_start(scan_d[0:H0].rearrange("(p e) -> p e", e=P), front[:, :]).then_inc(s_sw, 16)
            sp.dma_start(scan_d[H0 + NQ * QE:H0 + NQ * QE + 16 * P].rearrange("(p e) -> p e", e=P),
                         back[:, :]).then_inc(s_sw, 16)
            for k in range(2):
                at = k * QP * QE
                sp.dma_start(scan_d[H0 + at:H0 + at + QP * QE].rearrange("(p e) -> p e", e=QE),
                             DS[:, k, :]).then_inc(s_sw, 16)
                sp.dma_start(rel_d[at:at + QP * QE].rearrange("(p e) -> p e", e=QE),
                             D128[:, k, :]).then_inc(s_sw, 16)

            with sp.Fori(0, NB // 8) as k:
                for r in range(4):
                    sp.wait_ge(s_hic, 4 * k + r + 1)
                    sp.dma_start(hi_d[bass.ds((k * 8 + r * 2) * P, 2 * P), :].rearrange("(b p) c -> p b c", p=P),
                                 hiS[:, r, :, :]).then_inc(s_hw[r], 16)
            sp.wait_ge(s_hic, NB // 2 + 1)
            sp.dma_start(hi_d[(NB - 1) * P:NB * P, :], hiS[:, 0, 0, :]).then_inc(s_hw[0], 16)
            sp.wait_ge(s_h3, NB // 2 + 1)
            sp.dma_start(T[0:W, 1:2 * NB:2, :, :], T[W:P, 0:2 * NB:2, :, :]).then_inc(s_odd, 16)
            sp.dma_start(T[W:P, 1:2 * NB - 1:2, :, :], T[0:W, 2:2 * NB:2, :, :]).then_inc(s_odd, 16)
            sp.wait_ge(s_sw, 16 * 6)

            def step(g, s, n):
                f = stage(g, 0)
                if f is not None:
                    need(sp, s_ohT, GQ * (f - 2))
                    cnt = quads(f) * QE
                    sp.dma_start(Dbc[:, s, 0:cnt],
                                 rel_d[bass.ds(f * (GQ * QE), cnt)].rearrange("(o e) -> o e", o=1)
                                 .to_broadcast([P, cnt])).then_inc(s_db[s], 16)
                    need(sp, s_lx, f - 2)
                    passed(sp, "sp")
                    sp.dma_start(Dsc[:, s, :], bass.AP(scan_d.tensor, f * (GT * P), [[P, BT], [1, P + 1]])
                                 ).then_inc(s_ds[s], 16)
            run_steps(sp, step)

            sp.wait_ge(s_acc, 2 * NQ)
            def chunk(c):
                need(sp, s_m["xs"], c)
                sp.dma_start(xc, x[bass.ds(c * CW, CW), :].rearrange("(b p) c -> p b c", p=P)).then_inc(s_mx, 16)
                sp.wait_ge(s_m["ys"], c + 1)
                sp.dma_start(y_d[bass.ds(c * CW, CW), :].rearrange("(b p) c -> p b c", p=P), yS).then_inc(s_yw, 16)
            run_chunks(sp, chunk, NC - 1)

            r0 = (NC - 1) * CW
            sp.wait_ge(s_m["xs"], NC - 1)
            sp.dma_start(xc[0:NODES - FB * P, NCH - 1, :], x[FB * P:NODES, :]).then_inc(s_mr, 16)
            sp.wait_ge(s_mr, 16)
            sp.dma_start(xc[:, 0:NCH - 1, :],
                         x[r0:FB * P, :].rearrange("(b p) c -> p b c", p=P)).then_inc(s_mx, 16)
            sp.wait_ge(s_m["ys"], NC)
            sp.dma_start(y_d[r0:NB * P, :].rearrange("(b p) c -> p b c", p=P), yS).then_inc(s_yw, 16)

            def load(q, r, last=False):
                need(sp, s_b["at"], q - RB + 1)
                need(sp, s_b["tw"], q - RB + 1)
                if not last:
                    sp.dma_start(atB[:, r, :].rearrange("p (t c) -> p t c", c=EC),
                                 attr[bass.ds(q * QE, QE), :].rearrange("(t p) c -> p t c", p=P)).then_inc(s_at[r], 16)
                    sp.dma_start(ewB[:, r, :], ew[bass.ds(q * QE, QE)].rearrange("(o e) -> o e", o=1)
                                 .to_broadcast([P, QE])).then_inc(s_ew[r], 16)
                    return
                full = TAIL // P
                e0 = q * QE
                sp.wait_ge(s_b["cl"], 1)
                sp.dma_start(atB[:, r, 0:full * EC].rearrange("p (t c) -> p t c", c=EC),
                             attr[e0:e0 + full * P, :].rearrange("(t p) c -> p t c", p=P)).then_inc(s_at[r], 16)
                sp.dma_start(atB[0:TAIL - full * P, r, full * EC:(full + 1) * EC],
                             attr[e0 + full * P:EDGES, :]).then_inc(s_at[r], 16)
                sp.dma_start(ewB[:, r, 0:TAIL], ew[e0:EDGES].rearrange("(o e) -> o e", o=1)
                             .to_broadcast([P, TAIL])).then_inc(s_ew[r], 16)
            for q in range(RB):
                load(q, q)
            with sp.Fori(0, NQ // RB - 2) as k:
                for r in range(RB):
                    load(k * RB + RB + r, r)
            for q in range(NQ - RB, NQ):
                load(q, q % RB, q == NQ - 1)

            def chunk(c):
                sp.wait_ge(s_f["x2"], c + 1)
                sp.dma_start(out[bass.ds(c * CW, CW), :].rearrange("(b p) c -> p b c", p=P), yS).then_inc(s_out, 16)
            run_chunks(sp, chunk, NC - 1)

            sp.wait_ge(s_f["x2"], NC)
            sp.dma_start(out[r0:FB * P, :].rearrange("(b p) c -> p b c", p=P), yS[:, 0:NCH - 1, :]).then_inc(s_out, 16)
            sp.dma_start(out[FB * P:NODES, :], yS[0:NODES - FB * P, NCH - 1, :]).then_inc(s_out, 16)
            sp.wait_ge(s_out, 16 * (NC + 1))

        @block.gpsimd
        def _(pool):
            pool.memset(ident[:, :], 0.0).then_inc(s_c2, 1)
            pool.memset(down[:, :], 0.0).then_inc(s_c2, 1)
            pool.memset(up[:, :], 0.0).then_inc(s_c2, 1)
            pool.memset(Aw[:, :], 1.0).then_inc(s_c2, 1)
            pool.memset(ones[:, :], 1.0).then_inc(s_c2, 1)
            pool.memset(X16[:, :], 1.0).then_inc(s_c2, 1)
            pool.memset(XH[:, :], 1.0).then_inc(s_c2, 1)
            pool.iota(iotaI[:, :], [[1, W]], base=0, channel_multiplier=0).then_inc(s_c2, 1)
            pool.iota(pI[:, :], [[1, 1]], base=0, channel_multiplier=1).then_inc(s_c2, 1)
            pool.wait_ge(s_c2, 9)
            for m, off in ((ident, 0), (down, HEADS), (up, -HEADS)):
                pool.affine_select(out=m[:, :], in_=m[:, :], compare_op=ALU.not_equal, fill=1.0, base=off,
                                   pattern=[[-1, P]], channel_multiplier=1).then_inc(s_c, 1)
            pool.affine_select(out=Aw[:, :], in_=Aw[:, :], compare_op=ALU.is_ge, fill=0.0, base=0,
                               pattern=[[-HC, HEADS]], channel_multiplier=1).then_inc(s_c2, 1)
            pool.affine_select(out=X16[:, :], in_=X16[:, :], compare_op=ALU.is_ge, fill=0.0, base=0,
                               pattern=[[1, P]], channel_multiplier=-HEADS).then_inc(s_c2, 1)
            pool.affine_select(out=XH[:, :], in_=XH[:, :], compare_op=ALU.is_ge, fill=0.0, base=0,
                               pattern=[[1, P]], channel_multiplier=-HC).then_inc(s_c2, 1)
            pool.wait_ge(s_c2, 12)
            pool.affine_select(out=XH[:, :], in_=XH[:, :], compare_op=ALU.is_ge, fill=0.0, base=HC - 1,
                               pattern=[[-1, P]], channel_multiplier=HC).then_inc(s_c, 1)
            pool.affine_select(out=X16[:, :], in_=X16[:, :], compare_op=ALU.is_ge, fill=0.0, base=HEADS - 1,
                               pattern=[[-1, P]], channel_multiplier=HEADS).then_inc(s_c, 1)
            pool.affine_select(out=Aw[:, :], in_=Aw[:, :], compare_op=ALU.is_ge, fill=0.0, base=HC - 1,
                               pattern=[[HC, HEADS]], channel_multiplier=-1).then_inc(s_c, 1)
            for i in range(4):
                pool.wait_ge(s_hw[i], 16 * (NB // 8 + (i == 0)))
            pool.wait_ge(s_etc, 16)
            pool.wait_ge(s_sw, 16 * 6)

            def step(g, s, n):
                f = stage(g, 0)
                if f is None:
                    return
                pool.wait_ge(s_idx, f + 1)
                need(pool, s_msg, f - 2)
                passed(pool, "pool")
                for t in range(quads(f) * 4):
                    pool.indirect_dma_start(
                        out=G[:, s, t * C:(t + 1) * C], out_offset=None, in_=hi_d[:, :],
                        in_offset=bass.IndirectOffsetOnAxis(ap=idx[:, s, t:t + 1], axis=0)).then_inc(s_g[s], 16)
            run_steps(pool, step)

            pool.wait_ge(s_yw, 16 * NC)

            def gather_y(q, r):
                pool.wait_ge(s_b["idx"], q + 1)
                need(pool, s_b["zs"], q - RB + 1)
                passed(pool, "pool")
                for t in range(4):
                    pool.indirect_dma_start(
                        out=Yb[:, r, t * C:(t + 1) * C], out_offset=None, in_=y_d[:, :],
                        in_offset=bass.IndirectOffsetOnAxis(ap=idx[:, r, t:t + 1], axis=0)).then_inc(s_gy[r], 16)
            for q in range(RB):
                gather_y(q, q)
            with pool.Fori(0, NQ // RB - 1) as k:
                for r in range(RB):
                    gather_y(k * RB + RB + r, r)

        U = ps[0:3]
        Lp, LTp, EXp, AG = ps[3], ps[4], ps[5], ps[6]
        shp = ps[7]

        @block.scalar
        def _(act):
            for c in range(NC):
                act.wait_ge(s_xt, c + 1)
                for i, w_ in ((0, 4), (1, 3)):
                    act.activation(xT[:, c * CW + i * 512:c * CW + i * 512 + w_ * P], ps[i][:, 0:w_ * P],
                                   ACT.Copy).then_inc(s_xtc, 1)

            def second_part(pair, r, blocks=2):
                act.wait_ge(s_hr, pair + 1)
                act.activation(pair_of(pair, 1, blocks), hjr[:, r, 0:blocks, :], ACT.Copy).then_inc(s_h2, 1)

            def first_parts(pair, r, k, blocks=2):
                act.wait_ge(s_hh, pair + 1)
                need(act, s_hw[r], 16 * k)
                src_ = ps[2 + r][:, 0:blocks * 2 * C].rearrange("p (b h c) -> p b h c", b=blocks, h=2)
                act.activation(hiS[:, r, 0:blocks, :], src_[:, :, 0, :], ACT.Copy).then_inc(s_hic, 1)
                act.activation(pair_of(pair, 0, blocks), src_[:, :, 1, :], ACT.Copy).then_inc(s_h1, 1)
            for r in range(4):
                first_parts(r, r, 0)
                if r:
                    second_part(r - 1, r - 1)
            with act.Fori(1, NB // 8) as k:
                for r in range(4):
                    first_parts(4 * k + r, r, k)
                    second_part(4 * k + r - 1, (r - 1) % 4)
            first_parts(NB // 2, 0, NB // 8, 1)
            second_part(NB // 2 - 1, 3)
            second_part(NB // 2, 0, 1)

            def stage_idx(f, s):
                cnt = quads(f) * 4
                act.activation(idx[:, s, 0:cnt], IDX[:, bass.ds(f * GT, cnt)], ACT.Copy).then_inc(s_idx, 1)
            act.wait_ge(s_etc, 16)
            for f in range(3):
                stage_idx(f, f)

            def step(g, s, n):
                f, b = stage(g, 0), stage(g, 1)
                nq = quads(f) if f is not None else 0

                def scaled(j):
                    act.wait_ge(s_u, f * GQ + j + 1)
                    need(act, s_lk, (f - 1) * GQ + j + 1)
                    act.activation(V[:, j, :], U[j][:, :], ACT.Copy, scale=0.3).then_inc(s_v, 1)

                def keep(j):
                    act.wait_ge(s_log, f * GQ + j + 1)
                    logit = Lp[:, j * 32:(j + 1) * 32]
                    half = HALO * HEADS
                    if j == 0 and (not is_int(f) or f):
                        act.activation(L[:, (s - 1) % 3, BT * HEADS - half:BT * HEADS], logit[:, 0:half], ACT.Copy)
                    if j == GQ - 1:
                        act.activation(L[:, (s + 1) % 3, 0:half], logit[:, half:2 * half], ACT.Copy)
                    act.activation(L[:, s, half + j * 32:half + (j + 1) * 32], logit, ACT.Copy).then_inc(s_lc, 1)
                def links():
                    if b is None:
                        return
                    act.wait_ge(s_lx, b + 1)
                    need(act, s_r4, b)
                    act.activation(link[:, :], LTp[:, P:2 * P + 1], ACT.Copy, scale=BIG).then_inc(s_mask, 1)
                for j in range(nq):
                    scaled(j)
                    if j == 1:
                        keep(0)
                        links()
                        if not is_int(f) or f + 3 < NG:
                            stage_idx(f + 3, s)
                if nq <= 1:
                    if nq:
                        keep(0)
                    links()
                for j in range(1, nq):
                    keep(j)
                if b is not None:
                    act.wait_ge(s_xm, b + 1)
                    need(act, s_ext, b)
                    act.activation(EXT[:, :], XM[:, :], ACT.Exp).then_inc(s_exp, 1)
                    act.wait_ge(s_ext, b + 1)
                    need(act, s_agg, GQ * b)
                    act.activation(EXs[:, :], EXp[:, HALO * HEADS:(HALO + GT) * HEADS], ACT.Copy).then_inc(s_exs, 1)
            run_steps(act, step)

            def chunk(c):
                act.wait_ge(s_m["ve"], c + 1)
                act.activation(sd[:, :], ve[:, :], ACT.Sqrt).then_inc(s_m["sd"], 1)
                act.wait_ge(s_m["xT"], c + 1)
                need(act, s_m["y"], c)
                act.activation(x1T[:, 0:512], ps[2][:, :], ACT.Copy).then_inc(s_m["xTc"], 1)
                act.activation(x1T[:, 512:CW], ps[3][:, 0:CW - 512], ACT.Copy).then_inc(s_m["xTc"], 1)
                act.activation(X1[:, bass.ds(c * CW, CW)], T2[:, 6 * CW:7 * CW], ACT.Copy).then_inc(s_m["x1c"], 1)
            run_chunks(act, chunk, NC)

            def stage_b(q, r):
                act.activation(idx[:, r, 0:4], IDX[:, bass.ds(q * 4, 4)], ACT.Copy).then_inc(s_b["idx"], 1)
            for q in range(RB):
                stage_b(q, q)

            def edge(q, r, k):
                z, e, h = later(q, 3), later(q, 2), later(q, 1)
                if z is not None:
                    act.wait_ge(s_b["zs"], z + 1)
                    need(act, s_b["agg"], z)
                    act.activation(hS, zS, ACT.Relu).then_inc(s_b["h"], 1)
                    if not is_int(z) or z + RB < NQ:
                        stage_b(z + RB, (r - 3) % RB)
                if e is not None:
                    rr, kk = slot(r, k, 2)
                    act.wait_ge(s_ew[rr], 16 * (kk + 1))
                    need(act, s_b["efs"], e)
                    act.activation(twS, ewB[:, rr, :], ACT.Sigmoid, bias=cols[:, 4:5],
                                   scale=cols[:, 3:4]).then_inc(s_b["tw"], 1)
                if h is not None:
                    act.wait_ge(s_b["h1"], h + 1)
                    need(act, s_b["ef"], h)
                    act.activation(r1S, ps[1][:, :], ACT.Relu, bias=cols[:, 1:2]).then_inc(s_b["r1"], 1)
            run_edges(act, edge)

            act.wait_ge(s_b["acc"], 2 * NQ)
            def chunk(c):
                need(act, s_f["o"], c)
                act.activation(gat, accH[:, bass.ds(c * CW, CW)], ACT.Copy).then_inc(s_f["ac"], 1)
                act.activation(rec[0:1, :], accN[:, bass.ds(c * CW, CW)], ACT.Copy).then_inc(s_f["ac"], 1)
                act.wait_ge(s_f["ve"], c + 1)
                act.activation(sd[:, :], ve[:, :], ACT.Sqrt).then_inc(s_f["sd"], 1)
            run_chunks(act, chunk, NC)

        @block.vector
        def _(dve):
            steps = [0]

            def settled(ins):
                steps[0] += 1
                ins.then_inc(s_own, 1)
                dve.wait_ge(s_own, steps[0])
            dve.memset(xN[:, NB - 1, :], 0.0).then_inc(s_fill, 1)
            settled(dve.memset(P4i[:, :, :], NO_NODE))
            dve.memset(D4i[:, 1, :], NO_NODE).then_inc(s_fill, 1)
            dve.memset(S4i[:, 1, :], 0).then_inc(s_fill, 1)
            dve.memset(P4i[0:1, 0, 0:1], -1).then_inc(s_fill, 1)
            dve.memset(T[W:P, 2 * NB - 1, :, :], 0.0).then_inc(s_fill, 1)
            dve.memset(front[:, :], -1.0).then_inc(s_fill, 1)
            dve.memset(back[:, :], -1.0).then_inc(s_fill, 1)
            dve.memset(xT[:, NB * C:NP], 0.0).then_inc(s_fill, 1)
            dve.memset(L[:, :, :], 0.0).then_inc(s_fill, 1)
            dve.wait_ge(s_c, 6)
            dve.wait_ge(s_c2, 9)
            dve.tensor_copy(iotaF[:, :], iotaI[:, :])
            dve.tensor_copy(pF[:, :], pI[:, :])
            dve.wait_ge(s_col, 16 * 11)
            dve.tensor_scalar(Aw[:, :], Aw[:, :], cols[:, 0:1], None, ALU.mult)
            dve.wait_ge(s_row, 16)
            settled(dve.tensor_scalar(tabR[:, :], baseR[:, :], -W, None, ALU.bitwise_and))
            dve.tensor_scalar(tabR[:, :], tabR[:, :], 3.0 * C / W, None, ALU.mult).then_inc(s_tab, 1)
            dve.wait_ge(s_e, 16 * 10)
            dve.tensor_copy(D4[:, :, :], D4i)
            dve.tensor_copy(S4[:, :, :], S4i)
            settled(dve.tensor_scalar(B64i[:, :], D4i[:, :, 0], -W, None, ALU.bitwise_and))
            settled(dve.tensor_copy(B64[:, :], B64i[:, :]))
            for k in range(2):
                dve.tensor_scalar(D128[:, k, :], D4[:, k, :], B64[:, k:k + 1], None, ALU.subtract)
                dve.tensor_scalar(DR[:, k, :], D4[:, k, :], D4[:, k, 0:1], None, ALU.subtract)
            dve.tensor_tensor(DS, P4i, D4i, ALU.subtract).then_inc(s_p, 1)

            for i in range(16):
                lst, k, j = i // 8, i // 4 % 2, i % 4
                to = (R64, IDX)[lst][:, k * QP * 4:(k + 1) * QP * 4].rearrange("p (q j) -> p j q", j=4)[:, j, :]
                dve.wait_ge(s_et, i + 1)
                dve.tensor_copy(to, ps[6 + i % 2][:, 0:QP]).then_inc(s_etc, 1)

            def remainder(pair, r, blocks=2):
                dve.wait_ge(s_h1, pair + 1)
                hj = ps[2 + r][:, 0:blocks * 2 * C].rearrange("p (b h c) -> p b h c", b=blocks, h=2)[:, :, 1, :]
                dve.tensor_tensor(hjr[:, r, 0:blocks, :], hj, pair_of(pair, 0, blocks),
                                  ALU.subtract).then_inc(s_hr, 1)

            def third_part(pair, r, blocks=2):
                dve.wait_ge(s_h2, pair + 1)
                dve.tensor_tensor(pair_of(pair, 2, blocks), hjr[:, r, 0:blocks, :], pair_of(pair, 1, blocks),
                                  ALU.subtract).then_inc(s_h3, 1)
            for r in range(4):
                remainder(r, r)
                if r:
                    third_part(r - 1, r - 1)
            with dve.Fori(1, NB // 8) as k:
                for r in range(4):
                    remainder(4 * k + r, r)
                    third_part(4 * k + r - 1, (r - 1) % 4)
            remainder(NB // 2, 0, 1)
            third_part(NB // 2 - 1, 3)
            third_part(NB // 2, 0, 1)
            dve.wait_ge(s_sw, 16 * 6)
            dve.wait_ge(s_h3, NB // 2 + 1)
            dve.wait_ge(s_hh, NB // 2 + 1)
            dve.memset(acc[:, :, :], 0.0).then_inc(s_zero, 1)

            def block_onehot(f, s, n, j):
                if j == 0:
                    dve.wait_ge(s_db[s], 16 * (n + 1))
                need(dve, s_u, (f - 1) * GQ + j + 1)
                dve.tensor_scalar(ohT[:, j, :], Dbc[:, s, j * QE:(j + 1) * QE], pF[:, 0:1], None,
                                  ALU.is_equal).then_inc(s_ohT, 1)
            for j in range(GQ):
                block_onehot(0, 0, 0, j)

            def step(g, s, n):
                f, b, p, nx = stage(g, 0), stage(g, 1), stage(g, 2), stage(g, -1)
                nq = quads(f) if f is not None else 0
                nxq = quads(nx) if nx is not None else 0

                def leaky(j):
                    if j >= nq:
                        return
                    dve.wait_ge(s_v, f * GQ + j + 1)
                    need(dve, s_log, (f - 1) * GQ + j + 1)
                    dve.tensor_tensor(E[:, j, :], U[j][:, :], V[:, j, :], ALU.max).then_inc(s_lk, 1)

                def add(j):
                    if p is None or j >= quads(p):
                        return
                    dve.wait_ge(s_agg, p * GQ + j + 1)
                    need(dve, s_acc, 2 * (p * GQ + j))
                    base = dve.value_load(baseR[0:1, bass.ds(p * GQ + j, 1)], min_val=0, max_val=NODES - 1)
                    w_ = acc[:, 0, bass.ds(base, W)]
                    dve.tensor_tensor(w_, AG[:, j * P:j * P + W], w_, ALU.add).then_inc(s_acc, 1)
                    w_ = accD[:, bass.ds(base, W)]
                    dve.tensor_tensor(w_, AG[0:HEADS, j * P + W:(j + 1) * P], w_, ALU.add).then_inc(s_acc, 1)

                def nxt(j):
                    if j < nxq:
                        block_onehot(nx, (s + 1) % 3, n + (s + 1) // 3, j)
                leaky(0)
                add(0)
                nxt(0)
                leaky(1)
                add(1)
                nxt(1)
                if b is not None:
                    bs = (s - 1) % 3
                    dve.wait_ge(s_mask, b + 1)
                    dve.wait_ge(s_lt, b + 1)
                    dve.tensor_tensor_scan(R1[:, :], link[:, 0:P], LTp[:, 0:P], -1e30, ALU.add,
                                           ALU.max).then_inc(s_r1, 1)
                leaky(2)
                add(2)
                if b is not None:
                    dve.wait_ge(s_sh1, b + 1)
                    dve.tensor_tensor_scan(R2[:, :], link[:, 0:P], LTp[:, 0:P], shp[:, 0:1], ALU.add,
                                           ALU.max).then_inc(s_r2, 1)
                    dve.wait_ge(s_r2, b + 1)
                    dve.tensor_tensor_scan(R3[:, ::-1], link[:, P:0:-1], R2[:, ::-1], -1e30, ALU.add,
                                           ALU.max).then_inc(s_r3, 1)
                nxt(2)
                if b is not None:
                    need(dve, s_agg, GQ * b)
                    cnt = quads(b) * 4
                    dve.tensor_tensor(oh[:, 0:cnt * W].rearrange("p (t n) -> p t n", n=W),
                                      iotaF[:, :].unsqueeze(1).to_broadcast([P, cnt, W]),
                                      R64[:, bass.ds(b * GT, cnt)].unsqueeze(2).to_broadcast([P, cnt, W]),
                                      ALU.is_equal).then_inc(s_oh, 1)
                    dve.wait_ge(s_sh2, b + 1)
                    dve.tensor_tensor_scan(R4[:, ::-1], link[:, P:0:-1], R2[:, ::-1], shp[:, 1:2], ALU.add,
                                           ALU.max).then_inc(s_r4, 1)
                    dve.wait_ge(s_r4, b + 1)
                    need(dve, s_exp, b)
                    dve.tensor_tensor(XM[:, :], LTp[:, 0:P], R4[:, :], ALU.subtract).then_inc(s_xm, 1)
                    dve.wait_ge(s_exs, b + 1)
                    ex = EXp[:, HALO * HEADS:(HALO + cnt) * HEADS]
                    dve.tensor_tensor(msg[:, 0:cnt * C].rearrange("p (a c) -> p a c", c=HC),
                                      ex.unsqueeze(2).to_broadcast([P, cnt * HEADS, HC]),
                                      G[:, bs, 0:cnt * C].rearrange("p (a c) -> p a c", c=HC),
                                      ALU.mult).then_inc(s_msg, 1)
            run_steps(dve, step)

            def normalise(c, S, src_x, dst_x, row_ready):
                for i in range(NCH):
                    ins = dve.bn_stats(st[:, i, :], src_x[:, i, :])
                ins.then_inc(S["st"], 1)
                dve.wait_ge(S["st"], c + 1)
                passed(dve, "dve")
                for i in range(NCH):
                    ins = dve.bn_aggr(mv[:, i, :], st[:, i, :])
                ins.then_inc(S["mv"], 1)
                dve.wait_ge(S["mv"], c + 1)
                dve.tensor_scalar(ve[:, :], mv[:, :, 1], EPS, None, ALU.add).then_inc(S["ve"], 1)
                dve.wait_ge(S["sd"], c + 1)
                dve.reciprocal(rs[:, :], sd[:, :]).then_inc(S["rs"], 1)
                dve.wait_ge(S["rs"], c + 1)
                for i in range(NCH):
                    ins = dve.tensor_scalar(dst_x(i), src_x[:, i, :], mv[:, i, 0:1], rs[:, i:i + 1],
                                            ALU.subtract, ALU.mult)
                ins.then_inc(row_ready, 1)

            dve.wait_ge(s_acc, 2 * NQ)
            def chunk(c):
                dve.wait_ge(s_m["dx"], c + 1)
                dve.tensor_scalar(rec[:, 0:512], ps[6][:, :], 1e-30, None, ALU.max)
                dve.tensor_scalar(rec[:, 512:CW], ps[7][:, 0:CW - 512], 1e-30, None, ALU.max).then_inc(s_m["den"], 1)
                dve.wait_ge(s_m["den"], c + 1)
                dve.reciprocal(rec, rec).then_inc(s_m["rec"], 1)
                dve.wait_ge(s_m["rec"], c + 1)
                dve.tensor_tensor(gat, acc[:, 0, bass.ds(c * CW, CW)], rec, ALU.mult).then_inc(s_m["gat"], 1)
                dve.wait_ge(s_m["gT"], c + 1)
                dve.wait_ge(s_mx, 16 * (c + 1))
                dve.tensor_tensor(xs[:, 0:4, :], ps[0][:, :].rearrange("p (b c) -> p b c", b=4), xc[:, 0:4, :], ALU.add)
                dve.tensor_tensor(xs[:, 4:NCH, :], ps[1][:, 0:CW - 512].rearrange("p (b c) -> p b c", b=3),
                                  xc[:, 4:NCH, :], ALU.add).then_inc(s_m["xs"], 1)
                dve.wait_ge(s_m["xs"], c + 1)
                need(dve, s_m["x1c"], c)
                normalise(c, s_m, xs, lambda i: x1S[:, i, :], s_m["x1"])
                dve.wait_ge(s_m["y"], c + 1)
                need(dve, s_yw, 16 * c)
                for i, (bk, w_) in enumerate(((4, 4), (5, 3))):
                    ins = dve.tensor_tensor(yS[:, 4 * i:4 * i + w_, :],
                                            ps[bk][:, 0:w_ * C].rearrange("p (b c) -> p b c", b=w_),
                                            bn1B[:, :].unsqueeze(1).to_broadcast([P, w_, C]), ALU.add)
                ins.then_inc(s_m["ys"], 1)
            run_chunks(dve, chunk, NC)

            dve.memset(acc[:, :, :], 0.0).then_inc(s_m["cl"], 1)
            dve.wait_ge(s_m["cl"], 1)

            def edge(q, r, k):
                g4, z, e = later(q, 4), later(q, 3), later(q, 2)
                t = later(q, 0)
                if g4 is not None:
                    dve.wait_ge(s_b["agg"], g4 + 1)
                    need(dve, s_b["acc"], 2 * g4)
                    base = dve.value_load(baseR[0:1, bass.ds(g4, 1)], min_val=0, max_val=NODES - 1)
                    w_ = accH[:, bass.ds(base, W)]
                    dve.tensor_tensor(w_, ps[4][:, 0:W], w_, ALU.add).then_inc(s_b["acc"], 1)
                    w_ = accN[:, bass.ds(base, W)]
                    dve.tensor_tensor(w_, ps[4][0:1, W:2 * W], w_, ALU.add).then_inc(s_b["acc"], 1)
                if z is not None:
                    rr, kk = slot(r, k, 3)
                    dve.wait_ge(s_gy[rr], 64 * (kk + 1))
                    dve.wait_ge(s_b["z"], z + 1)
                    need(dve, s_b["h"], z)
                    dve.tensor_tensor(zS, ps[3][:, :], Yb[:, rr, :], ALU.add).then_inc(s_b["zs"], 1)
                    need(dve, s_b["agg"], z)
                    dve.tensor_tensor(ohB.rearrange("p (t n) -> p t n", n=W),
                                      iotaF[:, :].unsqueeze(1).to_broadcast([P, 4, W]),
                                      R64[:, bass.ds(z * 4, 4)].unsqueeze(2).to_broadcast([P, 4, W]),
                                      ALU.is_equal).then_inc(s_b["oh"], 1)
                if e is not None:
                    dve.wait_ge(s_b["ef"], e + 1)
                    dve.wait_ge(s_b["tw"], e + 1)
                    need(dve, s_b["z"], e)
                    dve.scalar_tensor_tensor(out=efS, in0=ps[2][:, :], scalar=cols[:, 2:3], in1=twS,
                                             op0=ALU.add, op1=ALU.mult).then_inc(s_b["efs"], 1)
                if t is not None:
                    dve.wait_ge(s_b["at"], t + 1)
                    need(dve, s_b["h1"], t)
                    dve.tensor_copy(atS, ps[0][0:EC, :]).then_inc(s_b["atc"], 1)
                if is_int(q) and q == NQ - 2:
                    dve.wait_ge(s_b["tw"], NQ - RB)
                    dve.memset(atB[:, RB - 1, :], 0.0)
                    dve.memset(ewB[:, RB - 1, :], 0.0).then_inc(s_b["cl"], 1)
            run_edges(dve, edge)

            dve.wait_ge(s_b["acc"], 2 * NQ)
            def chunk(c):
                need(dve, s_f["x2"], c)
                dve.wait_ge(s_f["o"], c + 1)
                for i, (bk, w_) in enumerate(((0, 4), (1, 3))):
                    ins = dve.scalar_tensor_tensor(
                        out=xs[:, 4 * i:4 * i + w_, :].rearrange("p b c -> p (b c)"),
                        in0=X1[:, bass.ds(c * CW + i * 512, w_ * C)], scalar=2.0,
                        in1=ps[bk][:, 0:w_ * C], op0=ALU.mult, op1=ALU.add)
                ins.then_inc(s_f["xs"], 1)
                dve.wait_ge(s_f["xs"], c + 1)
                need(dve, s_out, 16 * c)
                normalise(c, s_f, xs, lambda i: yS[:, i, :], s_f["x2"])
            run_chunks(dve, chunk, NC)

        @block.tensor
        def _(pe):
            pe.wait_ge(s_c, 6)
            pe.wait_ge(s_x, 16 * (NC + 1))
            for c in range(NC):
                need(pe, s_xtc, 2 * c)
                for i in range(NCH):
                    ins = pe.transpose(ps[i // 4][:, (i % 4) * P:(i % 4 + 1) * P], xN[:, c * NCH + i, :],
                                       ident[:, :])
                ins.then_inc(s_xt, 1)
            pe.wait_ge(s_p, 1)
            for i in range(16):
                lst, k, j = i // 8, i // 4 % 2, i % 4
                need(pe, s_etc, i - 1)
                pe.transpose(ps[6 + i % 2][:, 0:QP], (DR, S4)[lst][:, k, j * P:(j + 1) * P],
                             ident[0:QP, 0:QP]).then_inc(s_et, 1)
            pe.wait_ge(s_xtc, 2 * NC)
            pe.wait_ge(s_fill, 9)
            pe.wait_ge(s_w, 32)

            for b in range(NB):
                pair, r = b // 2, b // 2 % 4
                if b % 2 == 0:
                    need(pe, s_hr, pair - 3)
                c0 = b % 2 * 2 * C
                ins = pe.matmul(ps[2 + r][:, c0:c0 + 2 * C], xT[:, b * C:(b + 1) * C], W12[:, :],
                                start=True, stop=True)
                if b % 2 == 1 or b == NB - 1:
                    ins.then_inc(s_hh, 1)
            pe.wait_ge(s_hr, NB // 2 + 1)

            def step(g, s, n):
                f, b, p = stage(g, 0), stage(g, 1), stage(g, 2)
                nq = quads(f) if f is not None else 0

                def sums(j):
                    if j >= nq:
                        return
                    if j == 0:
                        pe.wait_ge(s_g[s], 192 * n + 64 * nq)
                    q = f * GQ + j
                    pe.wait_ge(s_ohT, q + 1)
                    need(pe, s_lk, (f - 1) * GQ + j + 1)
                    col = pe.value_load(tabR[0:1, bass.ds(q, 1)], min_val=0, max_val=(2 * NB - 1) * 3 * C)
                    for part in range(3):
                        pe.matmul(U[j][:, :], flatT[:, bass.ds(col + part * C, C)], ohT[:, j, :],
                                  start=(part == 0), stop=False)
                    for i in range(4):
                        t = 4 * j + i
                        ins = pe.matmul(U[j][:, i * P:(i + 1) * P], G[:, s, t * C:(t + 1) * C], ident[:, :],
                                        start=False, stop=(i == 3))
                    ins.then_inc(s_u, 1)

                def logits(j):
                    if j >= nq:
                        return
                    pe.wait_ge(s_lk, f * GQ + j + 1)
                    need(pe, s_lc, f * GQ + j)
                    for i in range(4):
                        c0 = j * 32 + i * HEADS
                        ins = pe.matmul(Lp[:, c0:c0 + HEADS], E[:, j, i * P:(i + 1) * P], Aw[:, :],
                                        start=True, stop=True)
                    ins.then_inc(s_log, 1)

                def aggregate(j):
                    if p is None or j >= quads(p):
                        return
                    if j == 0:
                        pe.wait_ge(s_oh, p + 1)
                        pe.wait_ge(s_msg, p + 1)
                        pe.wait_ge(s_exs, p + 1)
                    need(pe, s_acc, 2 * (p * GQ + j))
                    for i in range(4):
                        t = 4 * j + i
                        pe.matmul(AG[:, j * P:j * P + W], msg[:, t * C:(t + 1) * C], oh[:, t * W:(t + 1) * W],
                                  start=(i == 0), stop=(i == 3))
                    for i in range(4):
                        t = 4 * j + i
                        ins = pe.matmul(AG[0:HEADS, j * P + W:(j + 1) * P], EXs[:, t * HEADS:(t + 1) * HEADS],
                                        oh[:, t * W:(t + 1) * W], start=(i == 0), stop=(i == 3))
                    ins.then_inc(s_agg, 1)
                sums(0)
                aggregate(0)
                sums(1)
                if b is not None:
                    bs, bn_ = (s - 1) % 3, n + (s - 1) // 3
                    pe.wait_ge(s_ds[bs], 16 * (bn_ + 1))
                    need(pe, s_xm, b)
                    pe.matmul(LTp[:, P:2 * P + 1], X16[:, :], Dsc[:, bs, :], start=True, stop=True).then_inc(s_lx, 1)
                logits(0)
                aggregate(1)
                sums(2)
                if b is not None:
                    last = is_int(b) and b == NG - 1
                    pe.wait_ge(s_lc, NQ if last else (b + 1) * GQ + 1)
                    pe.wait_ge(s_mask, b + 1)
                    pe.transpose(LTp[:, 0:P], L[:, (s - 1) % 3, :], ident[:, :]).then_inc(s_lt, 1)
                logits(1)
                aggregate(2)
                if b is not None:
                    pe.wait_ge(s_r1, b + 1)
                    need(pe, s_r4, b)
                    pe.matmul(shp[:, 0:1], down[:, :], R1[:, P - 1:P], start=True, stop=True).then_inc(s_sh1, 1)
                logits(2)
                if b is not None:
                    pe.wait_ge(s_r3, b + 1)
                    pe.matmul(shp[:, 1:2], up[:, :], R3[:, 0:1], start=True, stop=True).then_inc(s_sh2, 1)
                    pe.wait_ge(s_exp, b + 1)
                    need(pe, s_msg, b)
                    need(pe, s_exs, b)
                    pe.transpose(EXp[:, 0:P], EXT[:, :], ident[:, :]).then_inc(s_ext, 1)
            pe.wait_ge(s_tab, 1)
            pe.wait_ge(s_odd, 32)
            flatT = T[:, :, :, :].rearrange("p b k c -> p (b k c)")
            run_steps(pe, step)

            pe.wait_ge(s_acc, 2 * NQ)
            def chunk(c):
                need(pe, s_m["den"], c)
                pe.matmul(ps[6][:, :], XH[:, :], accD[:, bass.ds(c * CW, 512)], start=True, stop=True)
                pe.matmul(ps[7][:, 0:CW - 512], XH[:, :], accD[:, bass.ds(c * CW + 512, CW - 512)],
                          start=True, stop=True).then_inc(s_m["dx"], 1)
                pe.wait_ge(s_m["gat"], c + 1)
                need(pe, s_m["xs"], c)
                for i in range(NCH):
                    ins = pe.transpose(ps[i // 4][:, (i % 4) * P:(i % 4 + 1) * P], gat[:, i * C:(i + 1) * C],
                                       ident[:, :])
                ins.then_inc(s_m["gT"], 1)
                pe.wait_ge(s_m["x1"], c + 1)
                for i in range(NCH):
                    ins = pe.transpose(ps[2 + i // 4][:, (i % 4) * P:(i % 4 + 1) * P],
                                       x1S[:, i, :], ident[:, :])
                ins.then_inc(s_m["xT"], 1)
                pe.wait_ge(s_m["xTc"], 2 * c + 2)
                need(pe, s_m["ys"], c)
                for i in range(NCH):
                    ins = pe.matmul(ps[4 + i // 4][:, (i % 4) * P:(i % 4 + 1) * P], x1T[:, i * C:(i + 1) * C],
                                    wN1[:, 0, :], start=True, stop=True)
                ins.then_inc(s_m["y"], 1)
            run_chunks(pe, chunk, NC)

            def edge(q, r, k):
                g4, z, e, h, t = (later(q, lag) for lag in (4, 3, 2, 1, 0))
                if g4 is not None:
                    pe.wait_ge(s_b["h"], g4 + 1)
                    pe.wait_ge(s_b["oh"], g4 + 1)
                    need(pe, s_b["acc"], 2 * g4)
                    for i in range(4):
                        pe.matmul(ps[4][:, 0:W], hS[:, i * C:(i + 1) * C], ohB[:, i * W:(i + 1) * W],
                                  start=(i == 0), stop=(i == 3))
                    for i in range(4):
                        ins = pe.matmul(ps[4][0:1, W:2 * W], ones[:, 0:1], ohB[:, i * W:(i + 1) * W],
                                        start=(i == 0), stop=(i == 3))
                    ins.then_inc(s_b["agg"], 1)
                if z is not None:
                    pe.wait_ge(s_b["efs"], z + 1)
                    need(pe, s_b["zs"], z)
                    for i in range(4):
                        ins = pe.matmul(ps[3][:, i * C:(i + 1) * C], efS[:, i * P:(i + 1) * P], wN1[:, 1, :],
                                        start=True, stop=True)
                    ins.then_inc(s_b["z"], 1)
                if e is not None:
                    pe.wait_ge(s_b["r1"], e + 1)
                    need(pe, s_b["efs"], e)
                    pe.matmul(ps[2][:, :], wE2[:, :], r1S, start=True, stop=True).then_inc(s_b["ef"], 1)
                if h is not None:
                    pe.wait_ge(s_b["atc"], h + 1)
                    need(pe, s_b["r1"], h)
                    pe.matmul(ps[1][:, :], wE1[:, :], atS, start=True, stop=True).then_inc(s_b["h1"], 1)
                if t is not None:
                    last = is_int(t) and t == NQ - 1
                    pe.wait_ge(s_at[r], 16 * (k + 1) + 16 * last)
                    need(pe, s_b["atc"], t)
                    passed(pe, "pe")
                    for i in range(4):
                        ins = pe.transpose(ps[0][0:EC, i * P:(i + 1) * P], atB[:, r, i * EC:(i + 1) * EC],
                                           ident[:, :])
                    ins.then_inc(s_b["at"], 1)
            run_edges(pe, edge)

            pe.wait_ge(s_b["acc"], 2 * NQ)
            def chunk(c):
                pe.wait_ge(s_f["ac"], 2 * c + 2)
                need(pe, s_f["xs"], c)
                for i in range(NCH):
                    o = ps[i // 4][:, (i % 4) * P:(i % 4 + 1) * P]
                    pe.matmul(o, gat[:, i * C:(i + 1) * C], wN2[:, :], start=True, stop=False)
                    ins = pe.matmul(o, rec[0:1, i * C:(i + 1) * C], bn2R[:, :], start=False, stop=True)
                ins.then_inc(s_f["o"], 1)
            run_chunks(pe, chunk, NC)

_INS = ["x", "src", "dst", "edge_attr_64", "edge_weight", "L0_gnn_w1", "L0_gnn_w2", "L0_gnn_a", "L1_gnn_We1",
        "L1_gnn_be1", "L1_gnn_We2", "L1_gnn_be2", "L1_gnn_Wt", "L1_gnn_bt", "L1_gnn_Wn1", "L1_gnn_bn1",
        "L1_gnn_Wn2", "L1_gnn_bn2"]


def kernel(**inputs):
    import numpy as np
    import concourse.bacc as bacc
    from concourse.bass_utils import run_bass_kernel_spmd as run

    nc = bacc.Bacc("TRN2", target_bir_lowering=False, num_devices=1)
    arrays, args = {}, []
    for name in _INS:
        v = np.ascontiguousarray(inputs[name])
        arrays[f"in_{name}"] = v
        args.append(nc.dram_tensor(f"in_{name}", v.shape, mybir.dt.from_np(v.dtype), kind="ExternalInput").ap())
    hi_d = nc.dram_tensor("hi_rows", (NB * P, C), F32, kind="Internal").ap()
    y_d = nc.dram_tensor("y_rows", (NB * P, C), F32, kind="Internal").ap()
    rel_d = nc.dram_tensor("block_destinations", (NQ * QE,), BF16, kind="Internal").ap()
    scan_d = nc.dram_tensor("scan_destinations", (HALO * P + NQ * QE + 16 * P,), F32, kind="Internal").ap()
    out = nc.dram_tensor("out", (NODES, C), F32, kind="ExternalOutput").ap()
    build(nc, *args, hi_d, y_d, rel_d, scan_d, out)
    r = run(nc, [arrays], core_ids=[0])
    return r.results[0]["out"]
```

```python
from contextlib import ExitStack

import concourse.bass as bass
from concourse import mybir

ALU = mybir.AluOpType
ACT = mybir.ActivationFunctionType
F32 = mybir.dt.float32
BF16 = mybir.dt.bfloat16
I32 = mybir.dt.int32

P = 128
C = 128
NODES = 6250
EDGES = 106250
HEADS = 8
HC = C // HEADS
DC = HEADS + 1
EC = 64
NB = -(-NODES // P)
NCH = 7
NC = NB // NCH
QE = 512
NQ = -(-EDGES // QE)
QP = NQ // 2
TAIL = EDGES - (NQ - 1) * QE
GQ, GT = 3, 12
NG = -(-NQ // GQ)
RG = 4
LASTQ = NQ - (NG - 1) * GQ
W = 64
NP = 6400
HALO = 2
BT = GT + 2 * HALO
LT_TILES = (NG - 1) * GT + BT
NO_NODE = 30000
BIG = float(2 ** 100)
EPS = 1e-5
RB = 4
assert NCH * NC == NB and 2 * QP == NQ and NQ % RB == 0


def is_int(v):
    return isinstance(v, int)


def need(eng, sem, value):
    if is_int(value) and value <= 0:
        return
    eng.wait_ge(sem, value)


def build(nc, x, src, dst, attr, ew, w1, w2, a, We1, be1, We2, be2, Wt, bt, Wn1, bn1, Wn2, bn2,
          hi_d, y_d, rel_d, scan_d, out):
    with ExitStack() as ctx:
        def sb(name, shape, dt=F32):
            return ctx.enter_context(nc.sbuf_tensor(name, shape, dt))

        def sem(name):
            return ctx.enter_context(nc.semaphore(name))

        T = sb("T", [P, 2 * NB, 3, C], BF16)
        acc = sb("acc", [P, 2, NP])
        L = sb("L", [P, RG, BT * HEADS])
        G = sb("G", [P, RG, GT * C])
        Dbc = sb("Dbc", [P, RG, GT * P], BF16)
        ohT = sb("ohT", [P, GQ, QE], BF16)
        oh = sb("oh", [P, GT * W])
        msg = sb("msg", [P, GT * C])
        V = sb("V", [P, GQ, QE])
        E = sb("E", [P, GQ, QE])
        Dsc = sb("Dsc", [BT, RG, P + 1])
        X16 = sb("X16", [BT, P])
        
        link = sb("link", [P, P + 1])
        R1 = sb("R1", [P, P])
        R2 = sb("R2", [P, P])
        R3 = sb("R3", [P, P])
        R4 = sb("R4", [P, P])
        XM = sb("XM", [P, P])
        EXT = sb("EXT", [P, P])
        EXs = sb("EXs", [P, GT, DC])
        R64 = sb("R64", [P, NQ * 4])
        IDX = sb("IDX", [P, NQ * 4], I32)
        idx = sb("idx", [P, RG, GT], I32)
        baseR = sb("baseR", [1, NQ], I32)
        tabR = sb("tabR", [1, NQ], I32)
        ident = sb("ident", [P, P])
        down = sb("down", [P, P])
        up = sb("up", [P, P])
        iotaI = sb("iotaI", [P, W], I32)
        iotaF = sb("iotaF", [P, W])
        pI = sb("pI", [P, 1], I32)
        pF = sb("pF", [P, 1])
        Aw = sb("Aw", [P, HEADS])
        cols = sb("cols", [P, 8])
        W12 = sb("W12", [P, 2 * C])
        wE1 = sb("wE1", [EC, C])
        wE2 = sb("wE2", [P, C])
        wN1 = sb("wN1", [P, 2, C])
        wN2 = sb("wN2", [P, C])
        bn1B = sb("bn1B", [P, C])
        bn2R = sb("bn2R", [1, C])
        st = sb("st", [P, NCH, 6])
        mv = sb("mv", [P, 2, NCH, 2])
        ve = sb("ve", [P, 2, NCH])
        sd = sb("sd", [P, 2, NCH])
        rs = sb("rs", [P, 2, NCH])
        nm = sb("nm", [P, 2, NCH])
        rd = sb("rd", [P, NCH, HEADS])

        TF = T[:, :, :, :].rearrange("p b k c -> p (b k c)").bitcast(F32)
        xN = TF[:, 0:NB * C].rearrange("p (b c) -> p b c", b=NB)
        xT = acc[:, 0, :]
        oh2 = acc[:, 1, 0:2 * QE]
        hjr = acc[:, 1, 2 * QE:2 * QE + 4 * 2 * C].rearrange("p (r b c) -> p r b c", r=4, b=2)
        D4i = G[0:QP, 0, 0:2 * QE].bitcast(I32).rearrange("p (k e) -> p k e", k=2)
        S4i = G[0:QP, 1, 0:2 * QE].bitcast(I32).rearrange("p (k e) -> p k e", k=2)
        D4 = G[0:QP, 2, 0:2 * QE].rearrange("p (k e) -> p k e", k=2)
        S4 = msg[0:QP, 0:2 * QE].rearrange("p (k e) -> p k e", k=2)
        DR = V[0:QP, 0:2, :]
        DS = oh2[0:QP, 0:2 * QE].rearrange("p (k e) -> p k e", k=2)
        P4i = E[0:QP, 0:2, :].bitcast(I32)
        D128 = Dbc[0:QP, 0, 0:2 * QE].rearrange("p (k e) -> p k e", k=2)
        B64i = sb("B64i", [QP, 2], I32)
        B64 = sb("B64", [QP, 2])
        front = oh[0:HALO, 0:P]
        back = oh[0:16, P:2 * P]
        hiS = G[:, 3, 0:8 * C].rearrange("p (r b c) -> p r b c", r=4, b=2)

        X1 = TF[:, 0:NB * C].rearrange("p (b c) -> p b c", b=NB)
        T2 = TF[:, NB * C:3 * NB * C]
        CW = NCH * C
        def chunk_buffers(at):
            return [T2[:, (at + i) * CW:(at + i + 1) * CW].rearrange("p (b c) -> p b c", b=NCH) for i in range(2)]
        xc = chunk_buffers(0)
        xs = chunk_buffers(2)
        yS = chunk_buffers(4)
        x1T = T2[:, 6 * CW:7 * CW]
        T3 = T2[:, 7 * CW:2 * NB * C]
        Yb = T3[:, 0:RB * QE].rearrange("p (r c) -> p r c", r=RB)
        ewB = T3[:, RB * QE:2 * RB * QE].rearrange("p (r c) -> p r c", r=RB)
        atB = T3[:, 2 * RB * QE:2 * RB * QE + RB * 4 * EC].rearrange("p (r c) -> p r c", r=RB)
        atS = msg[0:EC, 0:QE]
        r1S = msg[:, QE:2 * QE]
        twS = G[:, 0, 0:QE]
        efS = G[:, 0, QE:2 * QE]
        zS = G[:, 1, 0:QE]
        hS = G[:, 1, QE:2 * QE]
        ohB = G[:, 2, 0:4 * W]
        accH = acc[:, 0, :]
        accD = acc[0:DC, 1, :]

        ps = [ctx.enter_context(nc.psum_tensor(f"ps{i}", [P, 512], F32)) for i in range(8)]

        s_w = sem("weights_loaded")
        s_col = sem("columns_loaded")
        s_x = sem("x_loaded")
        s_fill = sem("fills_done")
        s_e = sem("edge_lists_loaded")
        s_row = sem("base_row_loaded")
        s_own = sem("vector_steps")
        s_tab = sem("block_columns_made")
        s_c = sem("constants_made")
        s_c2 = sem("constants_step")
        s_p = sem("prologue_vector_steps")
        s_xt = sem("x_transposed")
        s_xtc = sem("x_transposed_copied")
        s_hh = sem("projections_ready")
        s_hic = sem("hi_copied")
        s_h1 = sem("hj_first_parts")
        s_hr = sem("hj_remainders")
        s_h2 = sem("hj_second_parts")
        s_h3 = sem("hj_third_parts")
        s_odd = sem("odd_blocks_copied")
        s_hw = [sem(f"hi_written_{i}") for i in range(4)]
        s_et = sem("edge_lists_transposed")
        s_etc = sem("edge_lists_copied")
        s_sw = sem("scan_lists_written")
        s_zero = sem("accumulators_cleared")
        s_idx = sem("indices_staged")
        s_g = [[sem(f"rows_gathered_{i}_{j}") for j in range(GQ)] for i in range(RG)]
        s_db = [sem(f"block_destinations_loaded_{i}") for i in range(RG)]
        s_ds = [sem(f"scan_destinations_loaded_{i}") for i in range(RG)]
        s_ohT = sem("block_onehots_ready")
        s_u = sem("sums_ready")
        s_v = sem("scaled_sums_ready")
        s_lk = sem("leaky_ready")
        s_log = sem("logits_ready")
        s_lc = sem("logits_copied")
        s_lt = sem("logits_transposed")
        s_lx = sem("links_spread")
        s_mask = sem("links_ready")
        s_r1 = sem("first_scan_done")
        s_sh1 = sem("carry_down_ready")
        s_r2 = sem("second_scan_done")
        s_r3 = sem("third_scan_done")
        s_sh2 = sem("carry_up_ready")
        s_r4 = sem("fourth_scan_done")
        s_xm = sem("max_subtracted")
        s_exp = sem("exponentials_ready")
        s_ext = sem("exponentials_transposed")
        s_exs = sem("exponentials_copied")
        s_oh = sem("window_onehots_ready")
        s_msg = sem("messages_ready")
        s_agg = sem("aggregates_ready")
        s_acc = sem("aggregates_added")
        s_m = {n: sem("mid_" + n) for n in ("gT", "dmax", "rd", "gat", "xs", "st", "mv", "ve", "sd", "rs", "nm",
                                            "x1", "xT", "xTc", "y", "ys", "cl")}
        s_mx = [sem(f"mid_x_loaded_{i}") for i in range(2)]
        s_yw = [sem(f"y_written_{i}") for i in range(2)]
        s_gy = [sem(f"y_gathered_{i}") for i in range(RB)]
        s_at = [sem(f"attributes_loaded_{i}") for i in range(RB)]
        s_ew = [sem(f"edge_weights_loaded_{i}") for i in range(RB)]
        s_b = {n: sem("edge_" + n) for n in ("at", "atc", "h1", "r1", "ef", "tw", "efs", "z", "zs", "h", "oh",
                                             "agg", "acc", "idx", "cl")}
        s_f = {n: sem("last_" + n) for n in ("o", "xs", "st", "mv", "ve", "sd", "rs", "nm", "x1")}
        s_out = [sem(f"output_written_{i}") for i in range(2)]
        s_passed = {n: sem("waits_passed_" + n) for n in ("sp", "pool", "pe")}

        ctx.enter_context(nc.allow_non_contiguous_dma(reason="a few hundred words in all"))
        block = ctx.enter_context(nc.Block())

        def pair_of(pair, part, blocks):
            flat = T[:, :, :, :].rearrange("p b k c -> p b (k c)")
            if is_int(pair):
                return flat[:, 4 * pair:4 * pair + 2 * blocks:2, part * C:(part + 1) * C]
            return flat[:, bass.ds(4 * pair, blocks, 2), part * C:(part + 1) * C]

        def passed(eng, name):
            eng.sem_inc(s_passed[name], 1)

        def quads(g):
            return LASTQ if is_int(g) and g == NG - 1 else GQ

        def run_steps(eng, step):
            for g in range(RG):
                step(g, g % RG, g // RG)
            turns = (NG - 1 - RG) // RG - 1
            with eng.Fori(0, turns) as k:
                for i in range(RG):
                    step(RG * k + RG + i, i, k + 1)
            for g in range(RG + RG * turns, NG + 2):
                step(g, g % RG, g // RG)

        def stage(g, lag):
            if is_int(g):
                return g - lag if 0 <= g - lag < NG else None
            return g - lag

        def later(q, lag):
            if is_int(q):
                return q - lag if 0 <= q - lag < NQ else None
            return q - lag

        def slot(r, k, lag):
            d = r - lag
            return d % RB, k + d // RB

        def run_edges(eng, edge):
            for q in range(2 * RB):
                edge(q, q % RB, q // RB)
            with eng.Fori(2, NQ // RB - 1) as k:
                for r in range(RB):
                    edge(k * RB + r, r, k)
            for q in range(NQ - RB, NQ + 4):
                edge(q, q % RB, q // RB)

        @block.sync
        def _(sp):
            sp.dma_start(W12[:, 0:C], w1).then_inc(s_w, 16)
            sp.dma_start(W12[:, C:2 * C], w2).then_inc(s_w, 16)
            FB = NB - 1
            for c in range(NC):
                b1 = min((c + 1) * NCH, FB)
                sp.dma_start(xN[:, c * NCH:b1, :],
                             x[c * NCH * P:b1 * P, :].rearrange("(b p) c -> p b c", p=P)).then_inc(s_x, 16)
            sp.wait_ge(s_fill, 10)
            sp.dma_start(xN[0:NODES - FB * P, FB, :], x[FB * P:NODES, :]).then_inc(s_x, 16)
            for lst, t in ((dst, D4i), (src, S4i)):
                sp.dma_start(t[:, 0, :], lst[0:QP * QE].rearrange("(p e) -> p e", e=QE)).then_inc(s_e, 16)
                sp.dma_start(t[0:QP - 1, 1, :],
                             lst[QP * QE:(NQ - 1) * QE].rearrange("(p e) -> p e", e=QE)).then_inc(s_e, 16)
                sp.dma_start(t[QP - 1:QP, 1, 0:TAIL],
                             lst[(NQ - 1) * QE:EDGES].rearrange("(p e) -> p e", p=1)).then_inc(s_e, 16)
            sp.dma_start(P4i[0:1, 0, 1:QE], dst[0:QE - 1].rearrange("(p e) -> p e", p=1)).then_inc(s_e, 16)
            sp.dma_start(P4i[1:QP, 0, :],
                         dst[QE - 1:QP * QE - 1].rearrange("(p e) -> p e", e=QE)).then_inc(s_e, 16)
            sp.dma_start(P4i[0:QP - 1, 1, :],
                         dst[QP * QE - 1:(NQ - 1) * QE - 1].rearrange("(p e) -> p e", e=QE)).then_inc(s_e, 16)
            sp.dma_start(P4i[QP - 1:QP, 1, 0:TAIL + 1],
                         dst[(NQ - 1) * QE - 1:EDGES].rearrange("(p e) -> p e", p=1)).then_inc(s_e, 16)
            sp.dma_start(baseR[:, :], dst[0:(NQ - 1) * QE + 1:QE].rearrange("(p q) -> p q", p=1)).then_inc(s_row, 16)
            for i, v in enumerate((a.rearrange("o c -> (o c)"), be1, be2, Wt.rearrange("o c -> (o c)"), bt)):
                sp.dma_start(cols[:, i:i + 1], v.rearrange("(c o) -> c o", o=1)).then_inc(s_col, 16)
            sp.dma_start(wE1[:, :], We1).then_inc(s_col, 16)
            sp.dma_start(wE2[:, :], We2).then_inc(s_col, 16)
            sp.dma_start(wN1[:, :, :], Wn1.rearrange("(k p) c -> p k c", p=P)).then_inc(s_col, 16)
            sp.dma_start(wN2[:, :], Wn2).then_inc(s_col, 16)
            sp.dma_start(bn1B[:, :], bn1.rearrange("(o c) -> o c", o=1).to_broadcast([P, C])).then_inc(s_col, 16)
            sp.dma_start(bn2R[:, :], bn2.rearrange("(o c) -> o c", o=1)).then_inc(s_col, 16)
            sp.wait_ge(s_p, 1)
            H0 = HALO * P
            sp.dma_start(scan_d[0:H0].rearrange("(p e) -> p e", e=P), front).then_inc(s_sw, 16)
            sp.dma_start(scan_d[H0 + NQ * QE:H0 + NQ * QE + 16 * P].rearrange("(p e) -> p e", e=P),
                         back).then_inc(s_sw, 16)
            for k in range(2):
                at = k * QP * QE
                sp.dma_start(scan_d[H0 + at:H0 + at + QP * QE].rearrange("(p e) -> p e", e=QE),
                             DS[:, k, :]).then_inc(s_sw, 16)
                sp.dma_start(rel_d[at:at + QP * QE].rearrange("(p e) -> p e", e=QE),
                             D128[:, k, :]).then_inc(s_sw, 16)

            with sp.Fori(0, NB // 8) as k:
                for r in range(4):
                    sp.wait_ge(s_hic, 4 * k + r + 1)
                    sp.dma_start(hi_d[bass.ds((k * 8 + r * 2) * P, 2 * P), :].rearrange("(b p) c -> p b c", p=P),
                                 hiS[:, r, :, :]).then_inc(s_hw[r], 16)
            sp.wait_ge(s_hic, NB // 2 + 1)
            sp.dma_start(hi_d[(NB - 1) * P:NB * P, :], hiS[:, 0, 0, :]).then_inc(s_hw[0], 16)
            sp.wait_ge(s_h3, NB // 2 + 1)
            sp.dma_start(T[0:W, 1:2 * NB:2, :, :], T[W:P, 0:2 * NB:2, :, :]).then_inc(s_odd, 16)
            sp.dma_start(T[W:P, 1:2 * NB - 1:2, :, :], T[0:W, 2:2 * NB:2, :, :]).then_inc(s_odd, 16)
            sp.wait_ge(s_sw, 16 * 6)

            def step(g, s, n):
                f = stage(g, 0)
                if f is not None:
                    need(sp, s_ohT, GQ * (f - RG + 1))
                    cnt = quads(f) * QE
                    sp.dma_start(Dbc[:, s, 0:cnt],
                                 rel_d[bass.ds(f * (GQ * QE), cnt)].rearrange("(o e) -> o e", o=1)
                                 .to_broadcast([P, cnt])).then_inc(s_db[s], 16)
                    need(sp, s_lx, f - RG + 1)
                    passed(sp, "sp")
                    sp.dma_start(Dsc[:, s, :], bass.AP(scan_d.tensor, f * (GT * P), [[P, BT], [1, P + 1]])
                                 ).then_inc(s_ds[s], 16)
            run_steps(sp, step)

            sp.wait_ge(s_acc, 2 * NQ)

            def load_x(c):
                if c >= NC:
                    return
                need(sp, s_m["xs"], c - 1)
                b1 = min((c + 1) * NCH, FB)
                if b1 < (c + 1) * NCH:
                    sp.dma_start(xc[c % 2][0:NODES - FB * P, NCH - 1, :], x[FB * P:NODES, :]).then_inc(s_mx[c % 2], 16)
                sp.dma_start(xc[c % 2][:, 0:b1 - c * NCH, :],
                             x[c * CW:b1 * P, :].rearrange("(b p) c -> p b c", p=P)).then_inc(s_mx[c % 2], 16)
            load_x(0)
            load_x(1)
            for c in range(NC):
                sp.wait_ge(s_m["ys"], c + 1)
                sp.dma_start(y_d[c * CW:(c + 1) * CW, :].rearrange("(b p) c -> p b c", p=P),
                             yS[c % 2]).then_inc(s_yw[c % 2], 16)
                load_x(c + 2)

            def load(q, r, last=False):
                need(sp, s_b["at"], q - RB + 1)
                need(sp, s_b["tw"], q - RB + 1)
                if not last:
                    sp.dma_start(atB[:, r, :].rearrange("p (t c) -> p t c", c=EC),
                                 attr[bass.ds(q * QE, QE), :].rearrange("(t p) c -> p t c", p=P)).then_inc(s_at[r], 16)
                    sp.dma_start(ewB[:, r, :], ew[bass.ds(q * QE, QE)].rearrange("(o e) -> o e", o=1)
                                 .to_broadcast([P, QE])).then_inc(s_ew[r], 16)
                    return
                full = TAIL // P
                e0 = q * QE
                sp.wait_ge(s_b["cl"], 1)
                sp.dma_start(atB[:, r, 0:full * EC].rearrange("p (t c) -> p t c", c=EC),
                             attr[e0:e0 + full * P, :].rearrange("(t p) c -> p t c", p=P)).then_inc(s_at[r], 16)
                sp.dma_start(atB[0:TAIL - full * P, r, full * EC:(full + 1) * EC],
                             attr[e0 + full * P:EDGES, :]).then_inc(s_at[r], 16)
                sp.dma_start(ewB[:, r, 0:TAIL], ew[e0:EDGES].rearrange("(o e) -> o e", o=1)
                             .to_broadcast([P, TAIL])).then_inc(s_ew[r], 16)
            for q in range(RB):
                load(q, q)
            with sp.Fori(0, NQ // RB - 2) as k:
                for r in range(RB):
                    load(k * RB + RB + r, r)
            for q in range(NQ - RB, NQ):
                load(q, q % RB, q == NQ - 1)

            for c in range(NC):
                sp.wait_ge(s_f["x1"], c + 1)
                b1 = min((c + 1) * NCH, FB)
                sp.dma_start(out[c * CW:b1 * P, :].rearrange("(b p) c -> p b c", p=P),
                             yS[c % 2][:, 0:b1 - c * NCH, :]).then_inc(s_out[c % 2], 16)
            last = yS[(NC - 1) % 2]
            sp.dma_start(out[FB * P:NODES, :], last[0:NODES - FB * P, NCH - 1, :]).then_inc(s_out[(NC - 1) % 2], 16)
            sp.wait_ge(s_out[0], 16 * ((NC + 1) // 2 + NC % 2))
            sp.wait_ge(s_out[1], 16 * (NC // 2 + 1 - NC % 2))

        @block.gpsimd
        def _(pool):
            pool.memset(ident[:, :], 0.0).then_inc(s_c2, 1)
            pool.memset(down[:, :], 0.0).then_inc(s_c2, 1)
            pool.memset(up[:, :], 0.0).then_inc(s_c2, 1)
            pool.memset(Aw[:, :], 1.0).then_inc(s_c2, 1)
            pool.memset(X16[:, :], 1.0).then_inc(s_c2, 1)
            pool.iota(iotaI[:, :], [[1, W]], base=0, channel_multiplier=0).then_inc(s_c2, 1)
            pool.iota(pI[:, :], [[1, 1]], base=0, channel_multiplier=1).then_inc(s_c2, 1)
            pool.wait_ge(s_c2, 7)
            for m, off in ((ident, 0), (down, HEADS), (up, -HEADS)):
                pool.affine_select(out=m[:, :], in_=m[:, :], compare_op=ALU.not_equal, fill=1.0, base=off,
                                   pattern=[[-1, P]], channel_multiplier=1).then_inc(s_c, 1)
            pool.affine_select(out=Aw[:, :], in_=Aw[:, :], compare_op=ALU.is_ge, fill=0.0, base=0,
                               pattern=[[-HC, HEADS]], channel_multiplier=1).then_inc(s_c2, 1)
            pool.affine_select(out=X16[:, :], in_=X16[:, :], compare_op=ALU.is_ge, fill=0.0, base=0,
                               pattern=[[1, P]], channel_multiplier=-HEADS).then_inc(s_c2, 1)
            pool.wait_ge(s_c2, 9)
            pool.affine_select(out=X16[:, :], in_=X16[:, :], compare_op=ALU.is_ge, fill=0.0, base=HEADS - 1,
                               pattern=[[-1, P]], channel_multiplier=HEADS).then_inc(s_c, 1)
            pool.affine_select(out=Aw[:, :], in_=Aw[:, :], compare_op=ALU.is_ge, fill=0.0, base=HC - 1,
                               pattern=[[HC, HEADS]], channel_multiplier=-1).then_inc(s_c, 1)
            for i in range(4):
                pool.wait_ge(s_hw[i], 16 * (NB // 8 + (i == 0)))
            pool.wait_ge(s_etc, 16)
            pool.wait_ge(s_sw, 16 * 6)

            def step(g, s, n):
                f = stage(g, 0)
                if f is None:
                    return
                pool.wait_ge(s_idx, f + 1)
                need(pool, s_msg, f - RG + 1)
                passed(pool, "pool")
                for t in range(quads(f) * 4):
                    pool.indirect_dma_start(
                        out=G[:, s, t * C:(t + 1) * C], out_offset=None, in_=hi_d[:, :],
                        in_offset=bass.IndirectOffsetOnAxis(ap=idx[:, s, t:t + 1], axis=0)).then_inc(s_g[s][t // 4], 16)
            run_steps(pool, step)

            pool.wait_ge(s_yw[0], 16 * ((NC + 1) // 2))
            pool.wait_ge(s_yw[1], 16 * (NC // 2))

            def gather_y(q, r):
                pool.wait_ge(s_b["idx"], q + 1)
                need(pool, s_b["zs"], q - RB + 1)
                passed(pool, "pool")
                for t in range(4):
                    pool.indirect_dma_start(
                        out=Yb[:, r, t * C:(t + 1) * C], out_offset=None, in_=y_d[:, :],
                        in_offset=bass.IndirectOffsetOnAxis(ap=idx[:, r, t:t + 1], axis=0)).then_inc(s_gy[r], 16)
            for q in range(RB):
                gather_y(q, q)
            with pool.Fori(0, NQ // RB - 1) as k:
                for r in range(RB):
                    gather_y(k * RB + RB + r, r)

        U = ps[0:3]
        Lp, LTp, EXp, AG = ps[3], ps[4], ps[5], ps[6:8]
        shp = EXp[:, P:P + 2]

        @block.scalar
        def _(act):
            for c in range(NC):
                act.wait_ge(s_xt, c + 1)
                for i, w_ in ((0, 4), (1, 3)):
                    act.activation(xT[:, c * CW + i * 512:c * CW + i * 512 + w_ * P], ps[i][:, 0:w_ * P],
                                   ACT.Copy).then_inc(s_xtc, 1)

            def second_part(pair, r, blocks=2):
                act.wait_ge(s_hr, pair + 1)
                act.activation(pair_of(pair, 1, blocks), hjr[:, r, 0:blocks, :], ACT.Copy).then_inc(s_h2, 1)

            def first_parts(pair, r, k, blocks=2):
                act.wait_ge(s_hh, pair + 1)
                need(act, s_hw[r], 16 * k)
                src_ = ps[2 + r][:, 0:blocks * 2 * C].rearrange("p (b h c) -> p b h c", b=blocks, h=2)
                act.activation(hiS[:, r, 0:blocks, :], src_[:, :, 0, :], ACT.Copy).then_inc(s_hic, 1)
                act.activation(pair_of(pair, 0, blocks), src_[:, :, 1, :], ACT.Copy).then_inc(s_h1, 1)
            for r in range(4):
                first_parts(r, r, 0)
                if r:
                    second_part(r - 1, r - 1)
            with act.Fori(1, NB // 8) as k:
                for r in range(4):
                    first_parts(4 * k + r, r, k)
                    second_part(4 * k + r - 1, (r - 1) % 4)
            first_parts(NB // 2, 0, NB // 8, 1)
            second_part(NB // 2 - 1, 3)
            second_part(NB // 2, 0, 1)

            def stage_idx(f, s):
                cnt = quads(f) * 4
                act.activation(idx[:, s, 0:cnt], IDX[:, bass.ds(f * GT, cnt)], ACT.Copy).then_inc(s_idx, 1)
            act.wait_ge(s_etc, 16)
            for f in range(RG):
                stage_idx(f, f)

            def step(g, s, n):
                f, b, p = stage(g, 0), stage(g, 1), stage(g, 2)
                nq = quads(f) if f is not None else 0

                def scaled(j):
                    if j >= nq:
                        return
                    act.wait_ge(s_u, f * GQ + j + 1)
                    need(act, s_lk, (f - 1) * GQ + j + 1)
                    act.activation(V[:, j, :], U[j][:, :], ACT.Copy, scale=0.3).then_inc(s_v, 1)

                def keep(of, at, j):
                    if of is None or j >= quads(of):
                        return
                    act.wait_ge(s_log, of * GQ + j + 1)
                    logit = Lp[:, j * 32:(j + 1) * 32]
                    half = HALO * HEADS
                    if j == 0 and (not is_int(of) or of):
                        act.activation(L[:, (at - 1) % RG, BT * HEADS - half:BT * HEADS], logit[:, 0:half], ACT.Copy)
                    if j == GQ - 1:
                        act.activation(L[:, (at + 1) % RG, 0:half], logit[:, half:2 * half], ACT.Copy)
                    act.activation(L[:, at, half + j * 32:half + (j + 1) * 32], logit, ACT.Copy).then_inc(s_lc, 1)
                scaled(0)
                if p is not None:
                    act.wait_ge(s_ext, p + 1)
                    need(act, s_agg, GQ * p)
                    act.activation(EXs[:, :, 1:DC],
                                   EXp[:, HALO * HEADS:(HALO + GT) * HEADS].rearrange("p (t h) -> p t h", h=HEADS),
                                   ACT.Copy).then_inc(s_exs, 1)
                if b is not None:
                    act.wait_ge(s_lx, b + 1)
                    need(act, s_r4, b)
                    act.activation(link[:, :], LTp[:, P:2 * P + 1], ACT.Copy, scale=BIG).then_inc(s_mask, 1)
                keep(b, (s - 1) % RG, 2)
                scaled(1)
                keep(f, s, 0)
                scaled(2)
                if f is not None and (not is_int(f) or f + RG < NG):
                    stage_idx(f + RG, s)
                keep(f, s, 1)
                if b is not None:
                    act.wait_ge(s_xm, b + 1)
                    need(act, s_ext, b)
                    act.activation(EXT[:, :], XM[:, :], ACT.Exp).then_inc(s_exp, 1)
            run_steps(act, step)

            def scale_rows(c, S, src_x, dst_x):
                act.wait_ge(S["nm"], c + 1)
                for i in range(NCH):
                    ins = act.activation(dst_x[:, i, :], src_x[:, i, :], ACT.Identity,
                                         bias=nm[:, c % 2, i:i + 1], scale=rs[:, c % 2, i:i + 1])
                ins.then_inc(S["x1"], 1)

            def deviation(c, S):
                act.wait_ge(S["ve"], c + 1)
                act.activation(sd[:, c % 2, :], ve[:, c % 2, :], ACT.Sqrt).then_inc(S["sd"], 1)

            for c in range(NC + 1):
                if c < NC:
                    deviation(c, s_m)
                if c >= 1:
                    act.wait_ge(s_m["xT"], c)
                    need(act, s_m["y"], c - 1)
                    act.activation(x1T[:, 0:512], ps[2][:, :], ACT.Copy).then_inc(s_m["xTc"], 1)
                    act.activation(x1T[:, 512:CW], ps[3][:, 0:CW - 512], ACT.Copy).then_inc(s_m["xTc"], 1)
                if c < NC:
                    scale_rows(c, s_m, xs[c % 2], X1[:, c * NCH:(c + 1) * NCH, :])

            def stage_b(q, r):
                act.activation(idx[:, r, 0:4], IDX[:, bass.ds(q * 4, 4)], ACT.Copy).then_inc(s_b["idx"], 1)
            for q in range(RB):
                stage_b(q, q)

            def edge(q, r, k):
                z, e, h = later(q, 3), later(q, 2), later(q, 1)
                if z is not None:
                    act.wait_ge(s_b["zs"], z + 1)
                    need(act, s_b["agg"], z)
                    act.activation(hS, zS, ACT.Relu).then_inc(s_b["h"], 1)
                    if not is_int(z) or z + RB < NQ:
                        stage_b(z + RB, (r - 3) % RB)
                if e is not None:
                    rr, kk = slot(r, k, 2)
                    act.wait_ge(s_ew[rr], 16 * (kk + 1))
                    need(act, s_b["efs"], e)
                    act.activation(twS, ewB[:, rr, :], ACT.Sigmoid, bias=cols[:, 4:5],
                                   scale=cols[:, 3:4]).then_inc(s_b["tw"], 1)
                if h is not None:
                    act.wait_ge(s_b["h1"], h + 1)
                    need(act, s_b["ef"], h)
                    act.activation(r1S, ps[1][:, :], ACT.Relu, bias=cols[:, 1:2]).then_inc(s_b["r1"], 1)
            run_edges(act, edge)

            for c in range(NC):
                deviation(c, s_f)
                need(act, s_out[c % 2], 16 * (c // 2))
                scale_rows(c, s_f, xs[c % 2], yS[c % 2])

        @block.vector
        def _(dve):
            steps = [0]

            def settled(ins):
                steps[0] += 1
                ins.then_inc(s_own, 1)
                dve.wait_ge(s_own, steps[0])
            dve.memset(xN[:, NB - 1, :], 0.0).then_inc(s_fill, 1)
            settled(dve.memset(P4i[:, :, :], NO_NODE))
            dve.memset(D4i[:, 1, :], NO_NODE).then_inc(s_fill, 1)
            dve.memset(S4i[:, 1, :], 0).then_inc(s_fill, 1)
            dve.memset(P4i[0:1, 0, 0:1], -1).then_inc(s_fill, 1)
            dve.memset(T[W:P, 2 * NB - 1, :, :], 0.0).then_inc(s_fill, 1)
            dve.memset(front, -1.0).then_inc(s_fill, 1)
            dve.memset(back, -1.0).then_inc(s_fill, 1)
            dve.memset(xT[:, NB * C:NP], 0.0).then_inc(s_fill, 1)
            dve.memset(L[:, :, :], 0.0).then_inc(s_fill, 1)
            dve.memset(EXs[:, :, 0:1], 1.0).then_inc(s_fill, 1)
            dve.wait_ge(s_c, 5)
            dve.wait_ge(s_c2, 7)
            dve.tensor_copy(iotaF[:, :], iotaI[:, :])
            dve.tensor_copy(pF[:, :], pI[:, :])
            dve.wait_ge(s_col, 16 * 11)
            dve.tensor_scalar(Aw[:, :], Aw[:, :], cols[:, 0:1], None, ALU.mult)
            dve.wait_ge(s_row, 16)
            settled(dve.tensor_scalar(tabR[:, :], baseR[:, :], -W, None, ALU.bitwise_and))
            dve.tensor_scalar(tabR[:, :], tabR[:, :], 3.0 * C / W, None, ALU.mult).then_inc(s_tab, 1)
            dve.wait_ge(s_e, 16 * 10)
            dve.tensor_copy(D4[:, :, :], D4i)
            dve.tensor_copy(S4[:, :, :], S4i)
            settled(dve.tensor_scalar(B64i[:, :], D4i[:, :, 0], -W, None, ALU.bitwise_and))
            settled(dve.tensor_copy(B64[:, :], B64i[:, :]))
            for k in range(2):
                dve.tensor_scalar(D128[:, k, :], D4[:, k, :], B64[:, k:k + 1], None, ALU.subtract)
                dve.tensor_scalar(DR[:, k, :], D4[:, k, :], D4[:, k, 0:1], None, ALU.subtract)
            dve.tensor_tensor(DS, P4i, D4i, ALU.subtract).then_inc(s_p, 1)

            for i in range(16):
                lst, k, j = i // 8, i // 4 % 2, i % 4
                to = (R64, IDX)[lst][:, k * QP * 4:(k + 1) * QP * 4].rearrange("p (q j) -> p j q", j=4)[:, j, :]
                dve.wait_ge(s_et, i + 1)
                dve.tensor_copy(to, ps[6 + i % 2][:, 0:QP]).then_inc(s_etc, 1)

            def remainder(pair, r, blocks=2):
                dve.wait_ge(s_h1, pair + 1)
                hj = ps[2 + r][:, 0:blocks * 2 * C].rearrange("p (b h c) -> p b h c", b=blocks, h=2)[:, :, 1, :]
                dve.tensor_tensor(hjr[:, r, 0:blocks, :], hj, pair_of(pair, 0, blocks),
                                  ALU.subtract).then_inc(s_hr, 1)

            def third_part(pair, r, blocks=2):
                dve.wait_ge(s_h2, pair + 1)
                dve.tensor_tensor(pair_of(pair, 2, blocks), hjr[:, r, 0:blocks, :], pair_of(pair, 1, blocks),
                                  ALU.subtract).then_inc(s_h3, 1)
            for r in range(4):
                remainder(r, r)
                if r:
                    third_part(r - 1, r - 1)
            with dve.Fori(1, NB // 8) as k:
                for r in range(4):
                    remainder(4 * k + r, r)
                    third_part(4 * k + r - 1, (r - 1) % 4)
            remainder(NB // 2, 0, 1)
            third_part(NB // 2 - 1, 3)
            third_part(NB // 2, 0, 1)
            dve.wait_ge(s_sw, 16 * 6)
            dve.wait_ge(s_h3, NB // 2 + 1)
            dve.wait_ge(s_hh, NB // 2 + 1)
            dve.memset(acc[:, :, :], 0.0).then_inc(s_zero, 1)

            def block_onehot(f, s, n, j):
                if j == 0:
                    dve.wait_ge(s_db[s], 16 * (n + 1))
                need(dve, s_u, (f - 1) * GQ + j + 1)
                dve.tensor_scalar(ohT[:, j, :], Dbc[:, s, j * QE:(j + 1) * QE], pF[:, 0:1], None,
                                  ALU.is_equal).then_inc(s_ohT, 1)
            for j in range(GQ):
                block_onehot(0, 0, 0, j)

            def step(g, s, n):
                f, b, p, nx = stage(g, 0), stage(g, 1), stage(g, 2), stage(g, -1)
                nq = quads(f) if f is not None else 0
                nxq = quads(nx) if nx is not None else 0

                def leaky(j):
                    if j >= nq:
                        return
                    dve.wait_ge(s_v, f * GQ + j + 1)
                    need(dve, s_log, (f - 1) * GQ + j + 1)
                    dve.tensor_tensor(E[:, j, :], U[j][:, :], V[:, j, :], ALU.max).then_inc(s_lk, 1)

                def add(j):
                    if p is None or j >= quads(p):
                        return
                    dve.wait_ge(s_agg, p * GQ + j + 1)
                    need(dve, s_acc, 2 * (p * GQ + j))
                    base = dve.value_load(baseR[0:1, bass.ds(p * GQ + j, 1)], min_val=0, max_val=NODES - 1)
                    w_ = acc[:, 0, bass.ds(base, W)]
                    dve.tensor_tensor(w_, AG[j % 2][:, 0:W], w_, ALU.add).then_inc(s_acc, 1)
                    w_ = accD[:, bass.ds(base, W)]
                    dve.tensor_tensor(w_, AG[j % 2][0:DC, W:2 * W], w_, ALU.add).then_inc(s_acc, 1)

                def nxt(j):
                    if j < nxq:
                        block_onehot(nx, (s + 1) % RG, n + (s + 1) // RG, j)
                leaky(0)
                nxt(0)
                if p is not None:
                    dve.wait_ge(s_exs, p + 1)
                    need(dve, s_agg, GQ * p)
                    cnt = quads(p) * 4
                    ex = EXp[:, HALO * HEADS:(HALO + cnt) * HEADS]
                    dve.tensor_tensor(msg[:, 0:cnt * C].rearrange("p (a c) -> p a c", c=HC),
                                      ex.unsqueeze(2).to_broadcast([P, cnt * HEADS, HC]),
                                      G[:, (s - 2) % RG, 0:cnt * C].rearrange("p (a c) -> p a c", c=HC),
                                      ALU.mult).then_inc(s_msg, 1)
                leaky(1)
                nxt(1)
                if b is not None:
                    dve.wait_ge(s_mask, b + 1)
                    dve.wait_ge(s_lt, b + 1)
                    dve.tensor_tensor_scan(R1[:, :], link[:, 0:P], LTp[:, 0:P], -1e30, ALU.add,
                                           ALU.max).then_inc(s_r1, 1)
                leaky(2)
                add(0)
                if b is not None:
                    dve.wait_ge(s_sh1, b + 1)
                    dve.tensor_tensor_scan(R2[:, :], link[:, 0:P], LTp[:, 0:P], shp[:, 0:1], ALU.add,
                                           ALU.max).then_inc(s_r2, 1)
                    dve.wait_ge(s_r2, b + 1)
                    dve.tensor_tensor_scan(R3[:, ::-1], link[:, P:0:-1], R2[:, ::-1], -1e30, ALU.add,
                                           ALU.max).then_inc(s_r3, 1)
                nxt(2)
                add(1)
                if b is not None:
                    dve.wait_ge(s_sh2, b + 1)
                    dve.tensor_tensor_scan(R4[:, ::-1], link[:, P:0:-1], R2[:, ::-1], shp[:, 1:2], ALU.add,
                                           ALU.max).then_inc(s_r4, 1)
                    dve.wait_ge(s_r4, b + 1)
                    need(dve, s_exp, b)
                    dve.tensor_tensor(XM[:, :], LTp[:, 0:P], R4[:, :], ALU.subtract).then_inc(s_xm, 1)
                add(2)
                if b is not None:
                    need(dve, s_agg, GQ * b)
                    cnt = quads(b) * 4
                    dve.tensor_tensor(oh[:, 0:cnt * W].rearrange("p (t n) -> p t n", n=W),
                                      iotaF[:, :].unsqueeze(1).to_broadcast([P, cnt, W]),
                                      R64[:, bass.ds(b * GT, cnt)].unsqueeze(2).to_broadcast([P, cnt, W]),
                                      ALU.is_equal).then_inc(s_oh, 1)
            run_steps(dve, step)

            def moments(c, S):
                dve.wait_ge(S["xs"], c + 1)
                for i in range(NCH):
                    ins = dve.bn_stats(st[:, i, :], xs[c % 2][:, i, :])
                ins.then_inc(S["st"], 1)
                dve.wait_ge(S["st"], c + 1)
                need(dve, S["x1"], c - 1)
                for i in range(NCH):
                    ins = dve.bn_aggr(mv[:, c % 2, i, :], st[:, i, :])
                ins.then_inc(S["mv"], 1)
                dve.wait_ge(S["mv"], c + 1)
                dve.tensor_scalar(ve[:, c % 2, :], mv[:, c % 2, :, 1], EPS, None, ALU.add).then_inc(S["ve"], 1)

            def factors(c, S):
                dve.wait_ge(S["sd"], c + 1)
                dve.reciprocal(rs[:, c % 2, :], sd[:, c % 2, :]).then_inc(S["rs"], 1)
                dve.wait_ge(S["rs"], c + 1)
                dve.scalar_tensor_tensor(out=nm[:, c % 2, :], in0=mv[:, c % 2, :, 0], scalar=-1.0,
                                         in1=rs[:, c % 2, :], op0=ALU.mult, op1=ALU.mult).then_inc(S["nm"], 1)

            BANKS = ((0, 4), (4, NCH - 4))
            dve.wait_ge(s_acc, 2 * NQ)
            for c in range(NC + 1):
                if c < NC:
                    dve.wait_ge(s_m["gT"], c + 1)
                    dve.tensor_scalar(rd[:, :, :],
                                      ps[6][:, 0:NCH * DC].rearrange("p (b h) -> p b h", h=DC)[:, :, 1:DC],
                                      1e-30, None, ALU.max).then_inc(s_m["dmax"], 1)
                    dve.wait_ge(s_m["dmax"], c + 1)
                    dve.reciprocal(rd[:, :, :], rd[:, :, :]).then_inc(s_m["rd"], 1)
                    dve.wait_ge(s_m["rd"], c + 1)
                    need(dve, s_m["x1"], c - 1)
                    for k, (b0, n) in enumerate(BANKS):
                        ins = dve.tensor_tensor(
                            xs[c % 2][:, b0:b0 + n, :].rearrange("p b (h c) -> p (b h) c", c=HC),
                            ps[k][:, 0:n * C].rearrange("p (a c) -> p a c", c=HC),
                            rd[:, b0:b0 + n, :].rearrange("p b h -> p (b h)").unsqueeze(2)
                            .to_broadcast([P, n * HEADS, HC]), ALU.mult)
                    ins.then_inc(s_m["gat"], 1)
                    dve.wait_ge(s_m["gat"], c + 1)
                    dve.wait_ge(s_mx[c % 2], 16 * (c // 2 + 1) + 16 * (c == NC - 1))
                    dve.tensor_tensor(xs[c % 2], xs[c % 2], xc[c % 2], ALU.add).then_inc(s_m["xs"], 1)
                    moments(c, s_m)
                if c >= 1:
                    dve.wait_ge(s_m["y"], c)
                    need(dve, s_yw[(c - 1) % 2], 16 * ((c - 1) // 2))
                    for k, (b0, n) in enumerate(BANKS):
                        ins = dve.tensor_tensor(yS[(c - 1) % 2][:, b0:b0 + n, :],
                                                ps[4 + k][:, 0:n * C].rearrange("p (b c) -> p b c", b=n),
                                                bn1B[:, :].unsqueeze(1).to_broadcast([P, n, C]), ALU.add)
                    ins.then_inc(s_m["ys"], 1)
                if c < NC:
                    factors(c, s_m)

            dve.memset(accH, 0.0).then_inc(s_m["cl"], 1)
            dve.wait_ge(s_m["cl"], 1)

            def edge(q, r, k):
                g4, z, e = later(q, 4), later(q, 3), later(q, 2)
                t = later(q, 0)
                if g4 is not None:
                    dve.wait_ge(s_b["agg"], g4 + 1)
                    need(dve, s_b["acc"], g4)
                    base = dve.value_load(baseR[0:1, bass.ds(g4, 1)], min_val=0, max_val=NODES - 1)
                    w_ = accH[:, bass.ds(base, W)]
                    dve.tensor_tensor(w_, ps[4][:, 0:W], w_, ALU.add).then_inc(s_b["acc"], 1)
                if z is not None:
                    rr, kk = slot(r, k, 3)
                    dve.wait_ge(s_gy[rr], 64 * (kk + 1))
                    dve.wait_ge(s_b["z"], z + 1)
                    need(dve, s_b["h"], z)
                    dve.tensor_tensor(zS, ps[3][:, :], Yb[:, rr, :], ALU.add).then_inc(s_b["zs"], 1)
                    need(dve, s_b["agg"], z)
                    dve.tensor_tensor(ohB.rearrange("p (t n) -> p t n", n=W),
                                      iotaF[:, :].unsqueeze(1).to_broadcast([P, 4, W]),
                                      R64[:, bass.ds(z * 4, 4)].unsqueeze(2).to_broadcast([P, 4, W]),
                                      ALU.is_equal).then_inc(s_b["oh"], 1)
                if e is not None:
                    dve.wait_ge(s_b["ef"], e + 1)
                    dve.wait_ge(s_b["tw"], e + 1)
                    need(dve, s_b["z"], e)
                    dve.scalar_tensor_tensor(out=efS, in0=ps[2][:, :], scalar=cols[:, 2:3], in1=twS,
                                             op0=ALU.add, op1=ALU.mult).then_inc(s_b["efs"], 1)
                if t is not None:
                    dve.wait_ge(s_b["at"], t + 1)
                    need(dve, s_b["h1"], t)
                    dve.tensor_copy(atS, ps[0][0:EC, :]).then_inc(s_b["atc"], 1)
                if is_int(q) and q == NQ - 2:
                    dve.wait_ge(s_b["tw"], NQ - RB)
                    dve.memset(atB[:, RB - 1, :], 0.0)
                    dve.memset(ewB[:, RB - 1, :], 0.0).then_inc(s_b["cl"], 1)
            run_edges(dve, edge)

            for c in range(NC + 1):
                if c < NC:
                    dve.wait_ge(s_f["o"], c + 1)
                    need(dve, s_f["x1"], c - 1)
                    for k, (b0, n) in enumerate(BANKS):
                        ins = dve.scalar_tensor_tensor(
                            out=xs[c % 2][:, b0:b0 + n, :].rearrange("p b c -> p (b c)"),
                            in0=X1[:, c * NCH + b0:c * NCH + b0 + n, :].rearrange("p b c -> p (b c)"), scalar=2.0,
                            in1=ps[2 * (c % 2) + k][:, 0:n * C], op0=ALU.mult, op1=ALU.add)
                    ins.then_inc(s_f["xs"], 1)
                    moments(c, s_f)
                    factors(c, s_f)

        @block.tensor
        def _(pe):
            pe.wait_ge(s_c, 5)
            pe.wait_ge(s_x, 16 * (NC + 1))
            for c in range(NC):
                need(pe, s_xtc, 2 * c)
                for i in range(NCH):
                    ins = pe.transpose(ps[i // 4][:, (i % 4) * P:(i % 4 + 1) * P], xN[:, c * NCH + i, :],
                                       ident[:, :])
                ins.then_inc(s_xt, 1)
            pe.wait_ge(s_p, 1)
            for i in range(16):
                lst, k, j = i // 8, i // 4 % 2, i % 4
                need(pe, s_etc, i - 1)
                pe.transpose(ps[6 + i % 2][:, 0:QP], (DR, S4)[lst][:, k, j * P:(j + 1) * P],
                             ident[0:QP, 0:QP]).then_inc(s_et, 1)
            pe.wait_ge(s_xtc, 2 * NC)
            pe.wait_ge(s_fill, 10)
            pe.wait_ge(s_w, 32)

            for b in range(NB):
                pair, r = b // 2, b // 2 % 4
                if b % 2 == 0:
                    need(pe, s_hr, pair - 3)
                c0 = b % 2 * 2 * C
                ins = pe.matmul(ps[2 + r][:, c0:c0 + 2 * C], xT[:, b * C:(b + 1) * C], W12[:, :],
                                start=True, stop=True)
                if b % 2 == 1 or b == NB - 1:
                    ins.then_inc(s_hh, 1)
            pe.wait_ge(s_hr, NB // 2 + 1)

            def step(g, s, n):
                f, b, p = stage(g, 0), stage(g, 1), stage(g, 2)
                nq = quads(f) if f is not None else 0

                def sums(j):
                    if j >= nq:
                        return
                    pe.wait_ge(s_g[s][j], 64 * (n + 1))
                    q = f * GQ + j
                    pe.wait_ge(s_ohT, q + 1)
                    need(pe, s_lk, (f - 1) * GQ + j + 1)
                    col = pe.value_load(tabR[0:1, bass.ds(q, 1)], min_val=0, max_val=(2 * NB - 1) * 3 * C)
                    for i in range(4):
                        t = 4 * j + i
                        pe.matmul(U[j][:, i * P:(i + 1) * P], G[:, s, t * C:(t + 1) * C], ident[:, :],
                                  is_transpose=True, start=(i == 0), stop=False, skip_group_check=True)
                    for part in range(3):
                        ins = pe.matmul(U[j][:, :], flatT[:, bass.ds(col + part * C, C)], ohT[:, j, :],
                                        start=False, stop=(part == 2), skip_group_check=True)
                    ins.then_inc(s_u, 1)

                def logits(of, j):
                    if of is None or j >= quads(of):
                        return
                    pe.wait_ge(s_lk, of * GQ + j + 1)
                    need(pe, s_lc, of * GQ + j)
                    for i in range(4):
                        c0 = j * 32 + i * HEADS
                        ins = pe.matmul(Lp[:, c0:c0 + HEADS], E[:, j, i * P:(i + 1) * P], Aw[:, :],
                                        start=True, stop=True)
                    ins.then_inc(s_log, 1)

                def aggregate(j):
                    if p is None or j >= quads(p):
                        return
                    if j == 0:
                        pe.wait_ge(s_oh, p + 1)
                        pe.wait_ge(s_msg, p + 1)
                        pe.wait_ge(s_exs, p + 1)
                    need(pe, s_acc, 2 * (p * GQ + j - (j > 0)))
                    for i in range(4):
                        t = 4 * j + i
                        pe.matmul(AG[j % 2][:, 0:W], msg[:, t * C:(t + 1) * C], oh[:, t * W:(t + 1) * W],
                                  start=(i == 0), stop=(i == 3))
                    for i in range(4):
                        t = 4 * j + i
                        ins = pe.matmul(AG[j % 2][0:DC, W:2 * W], EXs[:, t, :],
                                        oh[:, t * W:(t + 1) * W], start=(i == 0), stop=(i == 3))
                    ins.then_inc(s_agg, 1)
                sums(0)
                if p is not None:
                    pe.wait_ge(s_exp, p + 1)
                    need(pe, s_msg, p)
                    pe.transpose(EXp[:, 0:P], EXT[:, :], ident[:, :]).then_inc(s_ext, 1)
                bs, bn_ = (s - 1) % RG, n + (s - 1) // RG
                if b is not None:
                    pe.wait_ge(s_ds[bs], 16 * (bn_ + 1))
                    need(pe, s_xm, b)
                    pe.matmul(LTp[:, P:2 * P + 1], X16[:, :], Dsc[:, bs, :], start=True, stop=True).then_inc(s_lx, 1)
                logits(b, 2)
                sums(1)
                logits(f, 0)
                sums(2)
                if b is not None:
                    last = is_int(b) and b == NG - 1
                    pe.wait_ge(s_lc, NQ if last else (b + 1) * GQ + 1)
                    pe.wait_ge(s_mask, b + 1)
                    pe.transpose(LTp[:, 0:P], L[:, bs, :], ident[:, :]).then_inc(s_lt, 1)
                aggregate(0)
                if b is not None:
                    pe.wait_ge(s_r1, b + 1)
                    need(pe, s_msg, b)
                    pe.matmul(shp[:, 0:1], down[:, :], R1[:, P - 1:P], start=True, stop=True).then_inc(s_sh1, 1)
                logits(f, 1)
                aggregate(1)
                if b is not None:
                    pe.wait_ge(s_r3, b + 1)
                    pe.matmul(shp[:, 1:2], up[:, :], R3[:, 0:1], start=True, stop=True).then_inc(s_sh2, 1)
                aggregate(2)
            pe.wait_ge(s_tab, 1)
            pe.wait_ge(s_odd, 32)
            flatT = T[:, :, :, :].rearrange("p b k c -> p (b k c)")
            run_steps(pe, step)

            pe.wait_ge(s_acc, 2 * NQ)

            def bank(first, i):
                return ps[first + i // 4][:, (i % 4) * P:(i % 4 + 1) * P]
            for c in range(NC + 1):
                if c < NC:
                    need(pe, s_m["gat"], c)
                    for i in range(NCH):
                        n0 = (c * NCH + i) * P
                        pe.transpose(bank(0, i), accH[:, n0:n0 + P], ident[:, :])
                        ins = pe.matmul(ps[6][:, i * DC:(i + 1) * DC], accD[:, n0:n0 + P], ident[0:DC, 0:DC],
                                        start=True, stop=True)
                    ins.then_inc(s_m["gT"], 1)
                if c >= 1:
                    pe.wait_ge(s_m["x1"], c)
                    need(pe, s_m["xTc"], 2 * (c - 1))
                    for i in range(NCH):
                        ins = pe.transpose(bank(2, i), X1[:, (c - 1) * NCH + i, :], ident[:, :])
                    ins.then_inc(s_m["xT"], 1)
                    pe.wait_ge(s_m["xTc"], 2 * c)
                    need(pe, s_m["ys"], c - 1)
                    for i in range(NCH):
                        ins = pe.matmul(bank(4, i), x1T[:, i * C:(i + 1) * C], wN1[:, 0, :], start=True, stop=True)
                    ins.then_inc(s_m["y"], 1)

            def edge(q, r, k):
                g4, z, e, h, t = (later(q, lag) for lag in (4, 3, 2, 1, 0))
                if g4 is not None:
                    pe.wait_ge(s_b["h"], g4 + 1)
                    pe.wait_ge(s_b["oh"], g4 + 1)
                    need(pe, s_b["acc"], g4)
                    for i in range(4):
                        ins = pe.matmul(ps[4][:, 0:W], hS[:, i * C:(i + 1) * C], ohB[:, i * W:(i + 1) * W],
                                        start=(i == 0), stop=(i == 3))
                    ins.then_inc(s_b["agg"], 1)
                if z is not None:
                    pe.wait_ge(s_b["efs"], z + 1)
                    need(pe, s_b["zs"], z)
                    for i in range(4):
                        ins = pe.matmul(ps[3][:, i * C:(i + 1) * C], efS[:, i * P:(i + 1) * P], wN1[:, 1, :],
                                        start=True, stop=True)
                    ins.then_inc(s_b["z"], 1)
                if e is not None:
                    pe.wait_ge(s_b["r1"], e + 1)
                    need(pe, s_b["efs"], e)
                    pe.matmul(ps[2][:, :], wE2[:, :], r1S, start=True, stop=True).then_inc(s_b["ef"], 1)
                if h is not None:
                    pe.wait_ge(s_b["atc"], h + 1)
                    need(pe, s_b["r1"], h)
                    pe.matmul(ps[1][:, :], wE1[:, :], atS, start=True, stop=True).then_inc(s_b["h1"], 1)
                if t is not None:
                    last = is_int(t) and t == NQ - 1
                    pe.wait_ge(s_at[r], 16 * (k + 1) + 16 * last)
                    need(pe, s_b["atc"], t)
                    passed(pe, "pe")
                    for i in range(4):
                        ins = pe.transpose(ps[0][0:EC, i * P:(i + 1) * P], atB[:, r, i * EC:(i + 1) * EC],
                                           ident[:, :])
                    ins.then_inc(s_b["at"], 1)
            run_edges(pe, edge)

            pe.wait_ge(s_b["acc"], NQ)
            for c in range(NC):
                need(pe, s_f["xs"], c - 1)
                for i in range(NCH):
                    n0 = (c * NCH + i) * P
                    pe.matmul(bank(2 * (c % 2), i), accH[:, n0:n0 + P], wN2[:, :], start=True, stop=False)
                    ins = pe.matmul(bank(2 * (c % 2), i), accD[0:1, n0:n0 + P], bn2R[:, :], start=False, stop=True)
                ins.then_inc(s_f["o"], 1)


_INS = ["x", "src", "dst", "edge_attr_64", "edge_weight", "L0_gnn_w1", "L0_gnn_w2", "L0_gnn_a", "L1_gnn_We1",
        "L1_gnn_be1", "L1_gnn_We2", "L1_gnn_be2", "L1_gnn_Wt", "L1_gnn_bt", "L1_gnn_Wn1", "L1_gnn_bn1",
        "L1_gnn_Wn2", "L1_gnn_bn2"]


def kernel(**inputs):
    import numpy as np
    import concourse.bacc as bacc
    from concourse.bass_utils import run_bass_kernel_spmd as run

    nc = bacc.Bacc("TRN2", target_bir_lowering=False, num_devices=1)
    arrays, args = {}, []
    for name in _INS:
        v = np.ascontiguousarray(inputs[name])
        arrays[f"in_{name}"] = v
        args.append(nc.dram_tensor(f"in_{name}", v.shape, mybir.dt.from_np(v.dtype), kind="ExternalInput").ap())
    hi_d = nc.dram_tensor("hi_rows", (NB * P, C), F32, kind="Internal").ap()
    y_d = nc.dram_tensor("y_rows", (NB * P, C), F32, kind="Internal").ap()
    rel_d = nc.dram_tensor("block_destinations", (NQ * QE,), BF16, kind="Internal").ap()
    scan_d = nc.dram_tensor("scan_destinations", (HALO * P + NQ * QE + 16 * P,), F32, kind="Internal").ap()
    out = nc.dram_tensor("out", (NODES, C), F32, kind="ExternalOutput").ap()
    build(nc, *args, hi_d, y_d, rel_d, scan_d, out)
    r = run(nc, [arrays], core_ids=[0])
    return r.results[0]["out"]
```

```python
from contextlib import ExitStack

import concourse.bass as bass
from concourse import mybir

ALU = mybir.AluOpType
ACT = mybir.ActivationFunctionType
F32 = mybir.dt.float32
BF16 = mybir.dt.bfloat16
I32 = mybir.dt.int32
AX = mybir.AxisListType

P = 128
C = 128
NODES = 6250
EDGES = 106250
HEADS = 8
HC = C // HEADS
DC = HEADS + 1
EC = 64
NB = -(-NODES // P)
NCH = 7
NC = NB // NCH
QE = 512
NQ = -(-EDGES // QE)
QP = NQ // 2
TAIL = EDGES - (NQ - 1) * QE
GQ, GT = 3, 12
NG = -(-NQ // GQ)
RG = 4
LASTQ = NQ - (NG - 1) * GQ
W = 64
NP = 6400
HALO = 2
BT = GT + 2 * HALO
NO_NODE = 30000
BIG = float(2 ** 100)
EPS = 1e-5
NT = -(-EDGES // P)
UB = 4
NU = NB // UB
HR = 3
RB = 4
assert NQ // RB - 3 == NB and NU * UB + 1 == NB and NU % HR == 0 and NU % 4 == 0
assert NCH * NC == NB and 2 * QP == NQ and NQ % RB == 0


def is_int(v):
    return isinstance(v, int)


def need(eng, sem, value):
    if is_int(value) and value <= 0:
        return
    eng.wait_ge(sem, value)


def build(nc, x, src, dst, attr, ew, w1, w2, a, We1, be1, We2, be2, Wt, bt, Wn1, bn1, Wn2, bn2,
          hi_d, y_d, rel_d, scan_d, max_d, sum_d, agg_d, out):
    with ExitStack() as ctx:
        def sb(name, shape, dt=F32):
            return ctx.enter_context(nc.sbuf_tensor(name, shape, dt))

        def sem(name):
            return ctx.enter_context(nc.semaphore(name))

        T = sb("T", [P, 2 * NB, 3, C], BF16)
        acc = sb("acc", [P, 2, NP])
        L = sb("L", [P, RG, BT * HEADS])
        G = sb("G", [P, RG, GT * C])
        Dbc = sb("Dbc", [P, RG, GT * P], BF16)
        ohT = sb("ohT", [P, GQ, QE], BF16)
        oh = sb("oh", [P, GT * W])
        msg = sb("msg", [P, GT * C])
        V = sb("V", [P, GQ, QE])
        E = sb("E", [P, GQ, QE])
        Dsc = sb("Dsc", [BT, RG, P + 1])
        X16 = sb("X16", [BT, P])
        
        link = sb("link", [P, P + 1])
        R1 = sb("R1", [P, P])
        R2 = sb("R2", [P, P])
        R3 = sb("R3", [P, P])
        R4 = sb("R4", [P, P])
        XM = sb("XM", [P, P])
        EXT = sb("EXT", [P, P])
        EXs = sb("EXs", [P, GT, DC])
        R64 = sb("R64", [P, NQ * 4])
        IDX = sb("IDX", [P, NQ * 4], I32)
        idx = sb("idx", [P, RG, GT], I32)
        baseR = sb("baseR", [1, NQ], I32)
        tabR = sb("tabR", [1, NQ], I32)
        ident = sb("ident", [P, P])
        down = sb("down", [P, P])
        up = sb("up", [P, P])
        iotaI = sb("iotaI", [P, W], I32)
        iotaF = sb("iotaF", [P, W])
        pI = sb("pI", [P, 1], I32)
        pF = sb("pF", [P, 1])
        Aw = sb("Aw", [P, HEADS])
        cols = sb("cols", [P, 8])
        W12 = sb("W12", [P, 2 * C])
        wE1 = sb("wE1", [EC, C])
        wE2 = sb("wE2", [P, C])
        wN1 = sb("wN1", [P, 2, C])
        wN2 = sb("wN2", [P, C])
        bn1B = sb("bn1B", [P, C])
        bn2B = sb("bn2B", [P, C])
        st = sb("st", [P, NCH, 6])
        mv = sb("mv", [P, 2, NCH, 2])
        ve = sb("ve", [P, 2, NCH])
        sd = sb("sd", [P, 2, NCH])
        rs = sb("rs", [P, 2, NCH])
        nm = sb("nm", [P, 2, NCH])
        rd = sb("rd", [P, NCH, HEADS])

        TF = T[:, :, :, :].rearrange("p b k c -> p (b k c)").bitcast(F32)
        xN = TF[:, 0:NB * C].rearrange("p (b c) -> p b c", b=NB)
        xT = acc[:, 0, :]
        oh2 = acc[:, 1, 0:2 * QE]
        hjr = acc[:, 1, 2 * QE:2 * QE + 4 * UB * C].rearrange("p (r b c) -> p r b c", r=4, b=UB)
        D4i = G[0:QP, 0, 0:2 * QE].bitcast(I32).rearrange("p (k e) -> p k e", k=2)
        S4i = G[0:QP, 1, 0:2 * QE].bitcast(I32).rearrange("p (k e) -> p k e", k=2)
        D4 = G[0:QP, 2, 0:2 * QE].rearrange("p (k e) -> p k e", k=2)
        S4 = msg[0:QP, 0:2 * QE].rearrange("p (k e) -> p k e", k=2)
        DR = V[0:QP, 0:2, :]
        DS = oh2[0:QP, 0:2 * QE].rearrange("p (k e) -> p k e", k=2)
        P4i = E[0:QP, 0:2, :].bitcast(I32)
        D128 = Dbc[0:QP, 0, 0:2 * QE].rearrange("p (k e) -> p k e", k=2)
        B64i = sb("B64i", [QP, 2], I32)
        B64 = sb("B64", [QP, 2])
        front = oh[0:HALO, 0:P]
        back = oh[0:16, P:2 * P]
        hiS = G[:, 3, 0:HR * UB * C].rearrange("p (r b c) -> p r b c", r=HR, b=UB)

        share = oh[:, 0:C]
        count = link[:, 0:NB]

        unusual = sb("unusual", [1, 1], I32)
        odd = sb("odd", [P, 4])
        halves = Dbc[:, :, :].rearrange("p s e -> p (s e)").bitcast(F32)
        DSTf = halves[:, 0:4 * NQ]
        DSTi = halves[:, 4 * NQ:8 * NQ].bitcast(I32)
        DSTx = halves[:, 8 * NQ:12 * NQ].bitcast(I32)
        LG = acc[:, :, :].rearrange("p k n -> p (k n)")
        hiT, xR, oldR = G[:, 0, 0:C], G[:, 0, C:2 * C], G[:, 0, 2 * C:3 * C + DC]
        newR, R = G[:, 1, 0:C + DC], G[:, 1, 2 * C:3 * C + DC]
        Dc, same, apart = V[:, 0, 0:P], V[:, 0, P:2 * P], V[:, 0, 2 * P:3 * P]
        xRT, u3, uM, atT = V[:, 1, 0:P], V[:, 1, P:2 * P], V[:, 1, 2 * P:3 * P], V[0:EC, 1, 3 * P:4 * P]
        r1T, twT, efT, zR = V[:, 2, 0:P], V[:, 2, P:2 * P], V[:, 2, 2 * P:3 * P], V[:, 2, 3 * P:4 * P]
        LB = msg[:, 0:HEADS * P].rearrange("p (h e) -> p h e", h=HEADS)
        LM = E[:, 0:2, :].rearrange("p k e -> p (k e)").rearrange("p (h e) -> p h e", h=HEADS)
        hR, at0, ew0 = R1[:, :], R2[:, 0:EC], R3[:, :]
        mOld, mTile, mNew, less = (XM[:, i * HEADS:(i + 1) * HEADS] for i in range(4))
        ones, baseF = R4[0:1, :], oh[0:1, 0:NQ]

        X1 = TF[:, 0:NB * C].rearrange("p (b c) -> p b c", b=NB)
        T2 = TF[:, NB * C:3 * NB * C]
        CW = NCH * C
        def chunk_buffers(at):
            return [T2[:, (at + i) * CW:(at + i + 1) * CW].rearrange("p (b c) -> p b c", b=NCH) for i in range(2)]
        xc = chunk_buffers(0)
        xs = chunk_buffers(2)
        yS = chunk_buffers(4)
        x1T = T2[:, 6 * CW:7 * CW]
        T3 = T2[:, 7 * CW:2 * NB * C]
        Yb = T3[:, 0:RB * QE].rearrange("p (r c) -> p r c", r=RB)
        ewB = T3[:, RB * QE:2 * RB * QE].rearrange("p (r c) -> p r c", r=RB)
        atB = T3[:, 2 * RB * QE:2 * RB * QE + RB * 4 * EC].rearrange("p (r c) -> p r c", r=RB)
        atS = msg[0:EC, 0:QE]
        r1S = msg[:, QE:2 * QE]
        twS = G[:, 0, 0:QE]
        efS = G[:, 0, QE:2 * QE]
        zS = G[:, 1, 0:QE]
        hS = G[:, 1, QE:2 * QE]
        ohB = G[:, 2, 0:4 * W]
        accH = acc[:, 0, :]
        accD = acc[0:DC, 1, :]

        ps = [ctx.enter_context(nc.psum_tensor(f"ps{i}", [P, 512], F32)) for i in range(8)]

        s_w = sem("weights_loaded")
        s_col = sem("columns_loaded")
        s_x = [sem(f"x_loaded_{c}") for c in range(NC)]
        s_fill = sem("fills_done")
        s_e = sem("edge_lists_loaded")
        s_row = sem("base_row_loaded")
        s_own = sem("vector_steps")
        s_tab = sem("block_columns_made")
        s_c = sem("constants_made")
        s_c2 = sem("constants_step")
        s_p = sem("prologue_vector_steps")
        s_xt = sem("x_transposed")
        s_xtc = sem("x_transposed_copied")
        s_hp = sem("hi_ready")
        s_hh = sem("hj_ready")
        s_hic = sem("hi_copied")
        s_h1 = sem("hj_first_parts")
        s_hr = sem("hj_remainders")
        s_h2 = sem("hj_second_parts")
        s_h3 = sem("hj_third_parts")
        s_odd = sem("odd_blocks_copied")
        s_hw = [sem(f"hi_written_{i}") for i in range(HR)]
        s_et = sem("edge_lists_transposed")
        s_etc = sem("edge_lists_copied")
        s_sw = sem("scan_lists_written")
        s_zero = sem("accumulators_cleared")
        s_idx = sem("indices_staged")
        s_g = [[sem(f"rows_gathered_{i}_{j}") for j in range(GQ)] for i in range(RG)]
        s_db = [sem(f"block_destinations_loaded_{i}") for i in range(RG)]
        s_ds = [sem(f"scan_destinations_loaded_{i}") for i in range(RG)]
        s_ohT = sem("block_onehots_ready")
        s_u = sem("sums_ready")
        s_v = sem("scaled_sums_ready")
        s_lk = sem("leaky_ready")
        s_log = sem("logits_ready")
        s_lc = sem("logits_copied")
        s_lt = sem("logits_transposed")
        s_lx = sem("links_spread")
        s_mask = sem("links_ready")
        s_r1 = sem("first_scan_done")
        s_sh1 = sem("carry_down_ready")
        s_r2 = sem("second_scan_done")
        s_r3 = sem("third_scan_done")
        s_sh2 = sem("carry_up_ready")
        s_r4 = sem("fourth_scan_done")
        s_xm = sem("max_subtracted")
        s_exp = sem("exponentials_ready")
        s_ext = sem("exponentials_transposed")
        s_exs = sem("exponentials_copied")
        s_oh = sem("window_onehots_ready")
        s_msg = sem("messages_ready")
        s_agg = sem("aggregates_ready")
        s_acc = sem("aggregates_added")
        s_m = {n: sem("mid_" + n) for n in ("gT", "dmax", "rd", "gat", "xs", "st", "mv", "ve", "sd", "rs", "nm",
                                            "x1", "xT", "xTc", "y", "ys", "cl")}
        s_mx = [sem(f"mid_x_loaded_{i}") for i in range(2)]
        s_yw = [sem(f"y_written_{i}") for i in range(2)]
        s_gy = [sem(f"y_gathered_{i}") for i in range(RB)]
        s_at = [sem(f"attributes_loaded_{i}") for i in range(RB)]
        s_ew = [sem(f"edge_weights_loaded_{i}") for i in range(RB)]
        s_b = {n: sem("edge_" + n) for n in ("at", "atc", "h1", "r1", "ef", "tw", "efs", "z", "zs", "h", "oh",
                                             "agg", "acc", "idx", "cl")}
        s_share = sem("shares_ready")
        s_x2 = sem("shares_added")
        s_f = {n: sem("last_" + n) for n in ("o", "xs", "st", "mv", "ve", "sd", "rs", "nm", "x1")}
        s_out = [sem(f"output_written_{i}") for i in range(2)]
        s_flag = sem("edges_judged")
        s_odd_q = sem("oddities_found")
        s_odd_s = sem("oddities_summed")
        s_pre = {"ones": s_oh, "base": s_exs, "dst": s_db[0], "rows": s_db[1], "fill": s_db[2], "tables": s_ds[0]}
        s_1 = {"turn": s_g[0][0], "idx": s_ds[1], "rows": s_g[0][1], "dc": s_g[0][2], "xt": s_g[1][0],
               "dt": s_g[1][1], "xc": s_g[1][2], "u": s_u, "v": s_v, "e": s_lk, "log": s_log, "lc": s_lc,
               "apart": s_mask, "lb": s_ohT, "lt": s_lt, "lm": s_r1, "tm": s_r2, "new": s_r3,
               "stored": s_g[2][0]}
        s_2 = {"turn": s_g[2][1], "idx": s_r4, "rows": s_g[2][2], "dc": s_sh1, "dt": s_sh2, "same": s_lx,
               "less": s_xm, "ex": s_exp, "r": s_msg, "sum": s_agg, "new": s_acc, "stored": s_g[3][0],
               "back": s_g[3][1], "loaded": s_g[3][2], "t": s_ext}
        s_3 = {"table": s_ew[1], "turn": s_at[1], "idx": s_b["idx"], "rows": s_gy[0], "dc": s_at[2],
               "dt": s_at[3], "same": s_b["oh"], "at": s_at[0], "ew": s_ew[0], "t": s_b["at"],
               "tc": s_b["atc"], "h1": s_b["h1"], "r1": s_b["r1"], "ef": s_b["ef"], "tw": s_b["tw"],
               "efs": s_b["efs"], "z": s_b["z"], "zs": s_b["zs"], "h": s_b["h"], "sum": s_b["agg"],
               "new": s_b["acc"], "stored": s_gy[1], "back": s_ew[2], "loaded": s_ew[3], "bt": s_gy[2]}
        s_passed = {n: sem("waits_passed_" + n) for n in ("sp", "pool", "pe")}

        ctx.enter_context(nc.allow_non_contiguous_dma(reason="a few hundred words in all"))
        block = ctx.enter_context(nc.Block())

        def unit_of(unit, part, blocks):
            flat = T[:, :, :, :].rearrange("p b k c -> p b (k c)")
            if is_int(unit):
                return flat[:, 2 * UB * unit:2 * UB * unit + 2 * blocks:2, part * C:(part + 1) * C]
            return flat[:, bass.ds(2 * UB * unit, blocks, 2), part * C:(part + 1) * C]

        def passed(eng, name):
            eng.sem_inc(s_passed[name], 1)

        def quads(g):
            return LASTQ if is_int(g) and g == NG - 1 else GQ

        def run_steps(eng, step):
            for g in range(RG):
                step(g, g % RG, g // RG)
            turns = (NG - 1 - RG) // RG - 1
            with eng.Fori(0, turns) as k:
                for i in range(RG):
                    step(RG * k + RG + i, i, k + 1)
            for g in range(RG + RG * turns, NG + 2):
                step(g, g % RG, g // RG)

        def stage(g, lag):
            if is_int(g):
                return g - lag if 0 <= g - lag < NG else None
            return g - lag

        def later(q, lag):
            if is_int(q):
                return q - lag if 0 <= q - lag < NQ else None
            return q - lag

        def slot(r, k, lag):
            d = r - lag
            return d % RB, k + d // RB

        def run_edges(eng, edge):
            for q in range(2 * RB):
                edge(q, q % RB, q // RB)
            with eng.Fori(2, NQ // RB - 1) as k:
                for r in range(RB):
                    edge(k * RB + r, r, k)
            for q in range(NQ - RB, NQ + 4):
                edge(q, q % RB, q // RB)

        @block.sync
        def _(sp):
            sp.dma_start(W12[:, 0:C], w1).then_inc(s_w, 16)
            sp.dma_start(W12[:, C:2 * C], w2).then_inc(s_w, 16)
            FB = NB - 1
            for c in range(NC):
                b1 = min((c + 1) * NCH, FB)
                sp.dma_start(xN[:, c * NCH:b1, :],
                             x[c * NCH * P:b1 * P, :].rearrange("(b p) c -> p b c", p=P)).then_inc(s_x[c], 16)
            sp.wait_ge(s_fill, 10)
            sp.dma_start(xN[0:NODES - FB * P, FB, :], x[FB * P:NODES, :]).then_inc(s_x[NC - 1], 16)
            for lst, t in ((dst, D4i), (src, S4i)):
                sp.dma_start(t[:, 0, :], lst[0:QP * QE].rearrange("(p e) -> p e", e=QE)).then_inc(s_e, 16)
                sp.dma_start(t[0:QP - 1, 1, :],
                             lst[QP * QE:(NQ - 1) * QE].rearrange("(p e) -> p e", e=QE)).then_inc(s_e, 16)
                sp.dma_start(t[QP - 1:QP, 1, 0:TAIL],
                             lst[(NQ - 1) * QE:EDGES].rearrange("(p e) -> p e", p=1)).then_inc(s_e, 16)
            sp.dma_start(P4i[0:1, 0, 1:QE], dst[0:QE - 1].rearrange("(p e) -> p e", p=1)).then_inc(s_e, 16)
            sp.dma_start(P4i[1:QP, 0, :],
                         dst[QE - 1:QP * QE - 1].rearrange("(p e) -> p e", e=QE)).then_inc(s_e, 16)
            sp.dma_start(P4i[0:QP - 1, 1, :],
                         dst[QP * QE - 1:(NQ - 1) * QE - 1].rearrange("(p e) -> p e", e=QE)).then_inc(s_e, 16)
            sp.dma_start(P4i[QP - 1:QP, 1, 0:TAIL + 1],
                         dst[(NQ - 1) * QE - 1:EDGES].rearrange("(p e) -> p e", p=1)).then_inc(s_e, 16)
            sp.dma_start(baseR[:, :], dst[0:(NQ - 1) * QE + 1:QE].rearrange("(p q) -> p q", p=1)).then_inc(s_row, 16)
            for i, v in enumerate((a.rearrange("o c -> (o c)"), be1, be2, Wt.rearrange("o c -> (o c)"), bt)):
                sp.dma_start(cols[:, i:i + 1], v.rearrange("(c o) -> c o", o=1)).then_inc(s_col, 16)
            sp.dma_start(wE1[:, :], We1).then_inc(s_col, 16)
            sp.dma_start(wE2[:, :], We2).then_inc(s_col, 16)
            sp.dma_start(wN1[:, :, :], Wn1.rearrange("(k p) c -> p k c", p=P)).then_inc(s_col, 16)
            sp.dma_start(wN2[:, :], Wn2).then_inc(s_col, 16)
            sp.dma_start(bn1B[:, :], bn1.rearrange("(o c) -> o c", o=1).to_broadcast([P, C])).then_inc(s_col, 16)
            sp.dma_start(bn2B[:, :], bn2.rearrange("(o c) -> o c", o=1).to_broadcast([P, C])).then_inc(s_col, 16)
            with sp.Fori(0, NU // HR) as k:
                for r in range(HR):
                    sp.wait_ge(s_hic, HR * k + r + 1)
                    sp.dma_start(hi_d[bass.ds((k * HR + r) * UB * P, UB * P), :].rearrange("(b p) c -> p b c", p=P),
                                 hiS[:, r, :, :]).then_inc(s_hw[r], 16)
            sp.wait_ge(s_hic, NU + 1)
            sp.dma_start(hi_d[(NB - 1) * P:NB * P, :], hiS[:, 0, 0, :]).then_inc(s_hw[0], 16)
            sp.wait_ge(s_p, 1)
            H0 = HALO * P
            sp.dma_start(scan_d[0:H0].rearrange("(p e) -> p e", e=P), front).then_inc(s_sw, 16)
            sp.dma_start(scan_d[H0 + NQ * QE:H0 + NQ * QE + 16 * P].rearrange("(p e) -> p e", e=P),
                         back).then_inc(s_sw, 16)
            for k in range(2):
                at = k * QP * QE
                sp.dma_start(scan_d[H0 + at:H0 + at + QP * QE].rearrange("(p e) -> p e", e=QE),
                             DS[:, k, :]).then_inc(s_sw, 16)
                sp.dma_start(rel_d[at:at + QP * QE].rearrange("(p e) -> p e", e=QE),
                             D128[:, k, :]).then_inc(s_sw, 16)
            for b0, b1, units in ((0, 4 * UB, 4), (4 * UB, 8 * UB, 8), (8 * UB, NB, NU + 1)):
                sp.wait_ge(s_h3, units)
                sp.dma_start(T[0:W, 2 * b0 + 1:2 * b1:2, :, :], T[W:P, 2 * b0:2 * b1:2, :, :]).then_inc(s_odd, 16)
                first = max(b0 - 1, 0)
                sp.dma_start(T[W:P, 2 * first + 1:2 * b1 - 1:2, :, :],
                             T[0:W, 2 * first + 2:2 * b1:2, :, :]).then_inc(s_odd, 16)
            sp.wait_ge(s_sw, 16 * 6)

            sp.wait_ge(s_flag, 1)
            with sp.If(sp.value_load(unusual[0:1, 0:1], min_val=0, max_val=4 * P) > 0):
                sp.wait_ge(s_pre["fill"], 1)
                sp.wait_ge(s_zero, 2)
                sp.dma_start(max_d.rearrange("(p b) h -> p (b h)", p=P), msg[:, 0:NB * HEADS]
                             ).then_inc(s_pre["tables"], 16)
                sp.dma_start(sum_d.rearrange("(p b) c -> p (b c)", p=P), LG[:, 0:NB * (C + DC)]
                             ).then_inc(s_pre["tables"], 16)
                sp.wait_ge(s_2["turn"], NT + 1)
                with sp.Fori(0, NB) as b:
                    sp.wait_ge(s_2["back"], b + 1)
                    passed(sp, "sp")
                    sp.dma_start(oldR, sum_d[bass.ds(b * P, P), :]).then_inc(s_2["loaded"], 16)
                sp.wait_ge(s_2["back"], NB + 1)
            with sp.Else():
                def step(g, s, n):
                    f = stage(g, 0)
                    if f is not None:
                        need(sp, s_ohT, GQ * (f - RG + 1))
                        cnt = quads(f) * QE
                        sp.dma_start(Dbc[:, s, 0:cnt],
                                     rel_d[bass.ds(f * (GQ * QE), cnt)].rearrange("(o e) -> o e", o=1)
                                     .to_broadcast([P, cnt])).then_inc(s_db[s], 16)
                        need(sp, s_lx, f - RG + 1)
                        passed(sp, "sp")
                        sp.dma_start(Dsc[:, s, :], bass.AP(scan_d.tensor, f * (GT * P), [[P, BT], [1, P + 1]])
                                     ).then_inc(s_ds[s], 16)
                run_steps(sp, step)
                sp.wait_ge(s_acc, 2 * NQ)


            def load_x(c):
                if c >= NC:
                    return
                need(sp, s_m["xs"], c - 1)
                b1 = min((c + 1) * NCH, FB)
                if b1 < (c + 1) * NCH:
                    sp.dma_start(xc[c % 2][0:NODES - FB * P, NCH - 1, :], x[FB * P:NODES, :]).then_inc(s_mx[c % 2], 16)
                sp.dma_start(xc[c % 2][:, 0:b1 - c * NCH, :],
                             x[c * CW:b1 * P, :].rearrange("(b p) c -> p b c", p=P)).then_inc(s_mx[c % 2], 16)
            load_x(0)
            load_x(1)
            for c in range(NC):
                load_x(c + 2)
                sp.wait_ge(s_m["ys"], c + 1)
                sp.dma_start(y_d[c * CW:(c + 1) * CW, :].rearrange("(b p) c -> p b c", p=P),
                             yS[c % 2]).then_inc(s_yw[c % 2], 16)

            with sp.If(sp.value_load(unusual[0:1, 0:1], min_val=0, max_val=4 * P) > 0):
                sp.wait_ge(s_m["cl"], 1)
                sp.dma_start(agg_d.rearrange("(p b) c -> p (b c)", p=P), accH[:, 0:NB * C]
                             ).then_inc(s_3["table"], 16)

                def load_tile(t, n):
                    sp.wait_ge(s_3["turn"], t + 1)
                    passed(sp, "sp")
                    sp.dma_start(at0[0:n, :], attr[bass.ds(t * P, n), :]).then_inc(s_3["at"], 16)
                    sp.dma_start(ew0[:, 0:n], ew[bass.ds(t * P, n)].rearrange("(o e) -> o e", o=1)
                                 .to_broadcast([P, n])).then_inc(s_3["ew"], 16)
                with sp.Fori(0, NT - 1) as t:
                    load_tile(t, P)
                load_tile(NT - 1, EDGES - (NT - 1) * P)
                sp.wait_ge(s_3["turn"], NT + 1)
                with sp.Fori(0, NB) as b:
                    sp.wait_ge(s_3["back"], b + 1)
                    passed(sp, "sp")
                    sp.dma_start(oldR[:, 0:C], agg_d[bass.ds(b * P, P), :]).then_inc(s_3["loaded"], 16)
            with sp.Else():
                def load(q, r, last=False):
                    need(sp, s_b["at"], q - RB + 1)
                    need(sp, s_b["tw"], q - RB + 1)
                    if not last:
                        sp.dma_start(atB[:, r, :].rearrange("p (t c) -> p t c", c=EC),
                                     attr[bass.ds(q * QE, QE), :].rearrange("(t p) c -> p t c", p=P)).then_inc(s_at[r], 16)
                        sp.dma_start(ewB[:, r, :], ew[bass.ds(q * QE, QE)].rearrange("(o e) -> o e", o=1)
                                     .to_broadcast([P, QE])).then_inc(s_ew[r], 16)
                        return
                    full = TAIL // P
                    e0 = q * QE
                    sp.wait_ge(s_b["cl"], 1)
                    sp.dma_start(atB[:, r, 0:full * EC].rearrange("p (t c) -> p t c", c=EC),
                                 attr[e0:e0 + full * P, :].rearrange("(t p) c -> p t c", p=P)).then_inc(s_at[r], 16)
                    sp.dma_start(atB[0:TAIL - full * P, r, full * EC:(full + 1) * EC],
                                 attr[e0 + full * P:EDGES, :]).then_inc(s_at[r], 16)
                    sp.dma_start(ewB[:, r, 0:TAIL], ew[e0:EDGES].rearrange("(o e) -> o e", o=1)
                                 .to_broadcast([P, TAIL])).then_inc(s_ew[r], 16)
                for q in range(RB):
                    load(q, q)
                with sp.Fori(0, NQ // RB - 2) as k:
                    for r in range(RB):
                        load(k * RB + RB + r, r)
                for q in range(NQ - RB, NQ):
                    load(q, q % RB, q == NQ - 1)

            for c in range(NC):
                sp.wait_ge(s_f["x1"], c + 1)
                b1 = min((c + 1) * NCH, FB)
                sp.dma_start(out[c * CW:b1 * P, :].rearrange("(b p) c -> p b c", p=P),
                             yS[c % 2][:, 0:b1 - c * NCH, :]).then_inc(s_out[c % 2], 16)
            last = yS[(NC - 1) % 2]
            sp.dma_start(out[FB * P:NODES, :], last[0:NODES - FB * P, NCH - 1, :]).then_inc(s_out[(NC - 1) % 2], 16)
            sp.wait_ge(s_out[0], 16 * ((NC + 1) // 2 + NC % 2))
            sp.wait_ge(s_out[1], 16 * (NC // 2 + 1 - NC % 2))

        @block.gpsimd
        def _(pool):
            pool.memset(ident[:, :], 0.0).then_inc(s_c2, 1)
            pool.memset(down[:, :], 0.0).then_inc(s_c2, 1)
            pool.memset(up[:, :], 0.0).then_inc(s_c2, 1)
            pool.memset(Aw[:, :], 1.0).then_inc(s_c2, 1)
            pool.memset(X16[:, :], 1.0).then_inc(s_c2, 1)
            pool.iota(iotaI[:, :], [[1, W]], base=0, channel_multiplier=0).then_inc(s_c2, 1)
            pool.iota(pI[:, :], [[1, 1]], base=0, channel_multiplier=1).then_inc(s_c2, 1)
            pool.wait_ge(s_c2, 7)
            for m, off in ((ident, 0), (down, HEADS), (up, -HEADS)):
                pool.affine_select(out=m[:, :], in_=m[:, :], compare_op=ALU.not_equal, fill=1.0, base=off,
                                   pattern=[[-1, P]], channel_multiplier=1).then_inc(s_c, 1)
            pool.affine_select(out=Aw[:, :], in_=Aw[:, :], compare_op=ALU.is_ge, fill=0.0, base=0,
                               pattern=[[-HC, HEADS]], channel_multiplier=1).then_inc(s_c2, 1)
            pool.affine_select(out=X16[:, :], in_=X16[:, :], compare_op=ALU.is_ge, fill=0.0, base=0,
                               pattern=[[1, P]], channel_multiplier=-HEADS).then_inc(s_c2, 1)
            pool.wait_ge(s_c2, 9)
            pool.affine_select(out=X16[:, :], in_=X16[:, :], compare_op=ALU.is_ge, fill=0.0, base=HEADS - 1,
                               pattern=[[-1, P]], channel_multiplier=HEADS).then_inc(s_c, 1)
            pool.affine_select(out=Aw[:, :], in_=Aw[:, :], compare_op=ALU.is_ge, fill=0.0, base=HC - 1,
                               pattern=[[HC, HEADS]], channel_multiplier=-1).then_inc(s_c, 1)
            pool.wait_ge(s_flag, 1)
            for i in range(HR):
                pool.wait_ge(s_hw[i], 16 * (NU // HR + (i == 0)))
            pool.wait_ge(s_etc, 4)

            with pool.If(pool.value_load(unusual[0:1, 0:1], min_val=0, max_val=4 * P) > 0):
                def gathered(row, table, k, done):
                    pool.indirect_dma_start(out=row, out_offset=None, in_=table,
                                            in_offset=bass.IndirectOffsetOnAxis(ap=idx[:, 0, k:k + 1], axis=0)
                                            ).then_inc(done, 16)

                def scattered(row, table, done):
                    pool.indirect_dma_start(out=table, out_offset=bass.IndirectOffsetOnAxis(ap=idx[:, 0, 1:2], axis=0),
                                            in_=row, in_offset=None).then_inc(done, 16)
                pool.wait_ge(s_pre["tables"], 32)
                pool.wait_ge(s_pre["rows"], 1)
                pool.sem_inc(s_1["turn"], 1)
                with pool.Fori(0, NT) as t:
                    pool.wait_ge(s_1["idx"], t + 1)
                    passed(pool, "pool")
                    gathered(hiT, hi_d[:, :], 0, s_1["rows"])
                    gathered(xR, x[:, :], 2, s_1["rows"])
                    gathered(mOld, max_d[:, :], 1, s_1["rows"])
                    pool.wait_ge(s_1["new"], t + 1)
                    passed(pool, "pool")
                    scattered(mNew, max_d[:, :], s_1["stored"])
                    pool.wait_ge(s_1["stored"], 16 * (t + 1))
                    pool.sem_inc(s_1["turn"], 1)
                pool.sem_inc(s_2["turn"], 1)
                with pool.Fori(0, NT) as t:
                    pool.wait_ge(s_2["idx"], t + 1)
                    passed(pool, "pool")
                    gathered(hiT, hi_d[:, :], 0, s_2["rows"])
                    gathered(mOld, max_d[:, :], 1, s_2["rows"])
                    gathered(oldR, sum_d[:, :], 1, s_2["rows"])
                    pool.wait_ge(s_2["new"], t + 1)
                    passed(pool, "pool")
                    scattered(newR, sum_d[:, :], s_2["stored"])
                    pool.wait_ge(s_2["stored"], 16 * (t + 1))
                    pool.sem_inc(s_2["turn"], 1)
            with pool.Else():
                def step(g, s, n):
                    f = stage(g, 0)
                    if f is None:
                        return
                    pool.wait_ge(s_idx, f + 1)
                    need(pool, s_msg, f - RG + 1)
                    passed(pool, "pool")
                    for t in range(quads(f) * 4):
                        pool.indirect_dma_start(
                            out=G[:, s, t * C:(t + 1) * C], out_offset=None, in_=hi_d[:, :],
                            in_offset=bass.IndirectOffsetOnAxis(ap=idx[:, s, t:t + 1], axis=0)).then_inc(s_g[s][t // 4], 16)
                run_steps(pool, step)

            pool.wait_ge(s_yw[0], 16 * ((NC + 1) // 2))
            pool.wait_ge(s_yw[1], 16 * (NC // 2))

            with pool.If(pool.value_load(unusual[0:1, 0:1], min_val=0, max_val=4 * P) > 0):
                def gathered(row, table, k):
                    pool.indirect_dma_start(out=row, out_offset=None, in_=table,
                                            in_offset=bass.IndirectOffsetOnAxis(ap=idx[:, 0, k:k + 1], axis=0)
                                            ).then_inc(s_3["rows"], 16)
                pool.wait_ge(s_3["table"], 16)
                pool.sem_inc(s_3["turn"], 1)
                with pool.Fori(0, NT) as t:
                    pool.wait_ge(s_3["idx"], t + 1)
                    passed(pool, "pool")
                    gathered(hiT, y_d[:, :], 0)
                    gathered(oldR[:, 0:C], agg_d[:, :], 1)
                    pool.wait_ge(s_3["new"], t + 1)
                    passed(pool, "pool")
                    pool.indirect_dma_start(out=agg_d[:, :], out_offset=bass.IndirectOffsetOnAxis(ap=idx[:, 0, 1:2], axis=0),
                                            in_=newR[:, 0:C], in_offset=None).then_inc(s_3["stored"], 16)
                    pool.wait_ge(s_3["stored"], 16 * (t + 1))
                    pool.sem_inc(s_3["turn"], 1)
            with pool.Else():
                def gather_y(q, r):
                    pool.wait_ge(s_b["idx"], q + 1)
                    need(pool, s_b["zs"], q - RB + 1)
                    passed(pool, "pool")
                    for t in range(4):
                        pool.indirect_dma_start(
                            out=Yb[:, r, t * C:(t + 1) * C], out_offset=None, in_=y_d[:, :],
                            in_offset=bass.IndirectOffsetOnAxis(ap=idx[:, r, t:t + 1], axis=0)).then_inc(s_gy[r], 16)
                for q in range(RB):
                    gather_y(q, q)
                with pool.Fori(0, NQ // RB - 1) as k:
                    for r in range(RB):
                        gather_y(k * RB + RB + r, r)

        HJ = [ps[5], ps[0], ps[1], ps[2]]
        U = ps[0:3]
        Lp, LTp, EXp, AG = ps[3], ps[4], ps[5], ps[6:8]
        shp = EXp[:, P:P + 2]

        @block.scalar
        def _(act):
            for c in range(NC):
                act.wait_ge(s_xt, c + 1)
                for i, w_ in ((0, 4), (1, 3)):
                    act.activation(xT[:, c * CW + i * 512:c * CW + i * 512 + w_ * P], ps[2 * (c % 2) + i][:, 0:w_ * P],
                                   ACT.Copy).then_inc(s_xtc, 1)

            def keep_hi(unit, r, k, blocks=UB):
                act.wait_ge(s_hp, unit + 1)
                need(act, s_hw[r], 16 * k)
                act.activation(hiS[:, r, 0:blocks, :].rearrange("p b c -> p (b c)"), ps[2 + r][:, 0:blocks * C],
                               ACT.Copy).then_inc(s_hic, 1)
            for u in range(HR):
                keep_hi(u, u, 0)
            with act.Fori(1, NU // HR) as k:
                for r in range(HR):
                    keep_hi(HR * k + r, r, k)
            keep_hi(NU, 0, NU // HR, 1)

            def stage_idx(f, s):
                cnt = quads(f) * 4
                act.activation(idx[:, s, 0:cnt], IDX[:, bass.ds(f * GT, cnt)], ACT.Copy).then_inc(s_idx, 1)
            act.wait_ge(s_etc, 4)
            for f in range(RG):
                stage_idx(f, f)

            def second_part(unit, r, blocks=UB):
                act.wait_ge(s_hr, unit + 1)
                act.activation(unit_of(unit, 1, blocks), hjr[:, r, 0:blocks, :], ACT.Copy).then_inc(s_h2, 1)

            def first_part(unit, r, blocks=UB):
                act.wait_ge(s_hh, unit + 1)
                act.activation(unit_of(unit, 0, blocks), HJ[r][:, 0:blocks * C].rearrange("p (b c) -> p b c", b=blocks),
                               ACT.Copy).then_inc(s_h1, 1)
            for r in range(4):
                first_part(r, r)
                if r:
                    second_part(r - 1, r - 1)
            with act.Fori(1, NU // 4) as k:
                for r in range(4):
                    first_part(4 * k + r, r)
                    second_part(4 * k + r - 1, (r - 1) % 4)
            first_part(NU, 0, 1)
            second_part(NU - 1, 3)
            second_part(NU, 0, 1)
            act.wait_ge(s_flag, 1)
            with act.If(act.value_load(unusual[0:1, 0:1], min_val=0, max_val=4 * P) > 0):
                def stage_rows(t, lists, done):
                    for k, rows in enumerate(lists):
                        ins = act.activation(idx[:, 0, k:k + 1], rows[:, bass.ds(t, 1)], ACT.Copy)
                    ins.then_inc(done, 1)
                with act.Fori(0, NT) as t:
                    act.wait_ge(s_1["turn"], t + 1)
                    stage_rows(t, (IDX, DSTi, DSTx), s_1["idx"])
                    act.wait_ge(s_1["xt"], t + 1)
                    act.activation(xRT, ps[0][:, 0:P], ACT.Copy).then_inc(s_1["xc"], 1)
                    act.wait_ge(s_1["u"], t + 1)
                    act.activation(u3, ps[2][:, 0:P], ACT.Copy, scale=0.3).then_inc(s_1["v"], 1)
                    act.wait_ge(s_1["log"], t + 1)
                    act.activation(LG[:, bass.ds(t * HEADS, HEADS)], ps[3][:, 0:HEADS], ACT.Copy).then_inc(s_1["lc"], 1)
                with act.Fori(0, NT) as t:
                    act.wait_ge(s_2["turn"], t + 1)
                    stage_rows(t, (IDX, DSTi), s_2["idx"])
                    act.wait_ge(s_2["less"], t + 1)
                    act.activation(R[:, C + 1:C + DC], less, ACT.Exp).then_inc(s_2["ex"], 1)
            with act.Else():
                def step(g, s, n):
                    f, b, p = stage(g, 0), stage(g, 1), stage(g, 2)
                    nq = quads(f) if f is not None else 0

                    def scaled(j):
                        if j >= nq:
                            return
                        act.wait_ge(s_u, f * GQ + j + 1)
                        need(act, s_lk, (f - 1) * GQ + j + 1)
                        act.activation(V[:, j, :], U[j][:, :], ACT.Copy, scale=0.3).then_inc(s_v, 1)

                    def keep(of, at, j):
                        if of is None or j >= quads(of):
                            return
                        act.wait_ge(s_log, of * GQ + j + 1)
                        logit = Lp[:, j * 32:(j + 1) * 32]
                        half = HALO * HEADS
                        if j == 0 and (not is_int(of) or of):
                            act.activation(L[:, (at - 1) % RG, BT * HEADS - half:BT * HEADS], logit[:, 0:half], ACT.Copy)
                        if j == GQ - 1:
                            act.activation(L[:, (at + 1) % RG, 0:half], logit[:, half:2 * half], ACT.Copy)
                        act.activation(L[:, at, half + j * 32:half + (j + 1) * 32], logit, ACT.Copy).then_inc(s_lc, 1)
                    scaled(0)
                    if p is not None:
                        act.wait_ge(s_ext, p + 1)
                        need(act, s_agg, GQ * p)
                        act.activation(EXs[:, :, 1:DC],
                                       EXp[:, HALO * HEADS:(HALO + GT) * HEADS].rearrange("p (t h) -> p t h", h=HEADS),
                                       ACT.Copy).then_inc(s_exs, 1)
                    if b is not None:
                        act.wait_ge(s_lx, b + 1)
                        need(act, s_r4, b)
                        act.activation(link[:, :], LTp[:, P:2 * P + 1], ACT.Copy, scale=BIG).then_inc(s_mask, 1)
                    keep(b, (s - 1) % RG, 2)
                    scaled(1)
                    keep(f, s, 0)
                    scaled(2)
                    if f is not None and (not is_int(f) or f + RG < NG):
                        stage_idx(f + RG, s)
                    keep(f, s, 1)
                    if b is not None:
                        act.wait_ge(s_xm, b + 1)
                        need(act, s_ext, b)
                        act.activation(EXT[:, :], XM[:, :], ACT.Exp).then_inc(s_exp, 1)
                run_steps(act, step)

            def scale_rows(c, S, src_x, dst_x):
                act.wait_ge(S["nm"], c + 1)
                for i in range(NCH):
                    ins = act.activation(dst_x[:, i, :], src_x[:, i, :], ACT.Identity,
                                         bias=nm[:, c % 2, i:i + 1], scale=rs[:, c % 2, i:i + 1])
                ins.then_inc(S["x1"], 1)

            def deviation(c, S):
                act.wait_ge(S["ve"], c + 1)
                act.activation(sd[:, c % 2, :], ve[:, c % 2, :], ACT.Sqrt).then_inc(S["sd"], 1)

            for c in range(NC + 1):
                if c >= 1:
                    act.wait_ge(s_m["xT"], c)
                    need(act, s_m["y"], c - 1)
                    act.activation(x1T[:, 0:512], ps[2][:, :], ACT.Copy).then_inc(s_m["xTc"], 1)
                    act.activation(x1T[:, 512:CW], ps[3][:, 0:CW - 512], ACT.Copy).then_inc(s_m["xTc"], 1)
                if c < NC:
                    deviation(c, s_m)
                    scale_rows(c, s_m, xs[c % 2], X1[:, c * NCH:(c + 1) * NCH, :])

            with act.If(act.value_load(unusual[0:1, 0:1], min_val=0, max_val=4 * P) > 0):
                with act.Fori(0, NT) as t:
                    act.wait_ge(s_3["turn"], t + 1)
                    act.activation(idx[:, 0, 0:1], IDX[:, bass.ds(t, 1)], ACT.Copy)
                    act.activation(idx[:, 0, 1:2], DSTi[:, bass.ds(t, 1)], ACT.Copy).then_inc(s_3["idx"], 1)
                    act.wait_ge(s_3["h1"], t + 1)
                    act.activation(r1T, ps[2][:, 0:P], ACT.Relu, bias=cols[:, 1:2]).then_inc(s_3["r1"], 1)
                    act.wait_ge(s_3["ew"], 16 * (t + 1))
                    act.activation(twT, ew0, ACT.Sigmoid, bias=cols[:, 4:5], scale=cols[:, 3:4]).then_inc(s_3["tw"], 1)
                    act.wait_ge(s_3["zs"], t + 1)
                    act.activation(hR, zR, ACT.Relu).then_inc(s_3["h"], 1)
            with act.Else():
                def stage_b(q, r):
                    act.activation(idx[:, r, 0:4], IDX[:, bass.ds(q * 4, 4)], ACT.Copy).then_inc(s_b["idx"], 1)
                for q in range(RB):
                    stage_b(q, q)

                def edge(q, r, k):
                    z, e, h = later(q, 3), later(q, 2), later(q, 1)
                    if e is not None:
                        rr, kk = slot(r, k, 2)
                        act.wait_ge(s_ew[rr], 16 * (kk + 1))
                        need(act, s_b["efs"], e)
                        act.activation(twS, ewB[:, rr, :], ACT.Sigmoid, bias=cols[:, 4:5],
                                       scale=cols[:, 3:4]).then_inc(s_b["tw"], 1)
                    if z is not None:
                        act.wait_ge(s_b["zs"], z + 1)
                        need(act, s_b["agg"], z)
                        act.activation(hS, zS, ACT.Relu).then_inc(s_b["h"], 1)
                        if not is_int(z) or z + RB < NQ:
                            stage_b(z + RB, (r - 3) % RB)
                    if h is not None:
                        act.wait_ge(s_b["h1"], h + 1)
                        need(act, s_b["ef"], h)
                        act.activation(r1S, ps[1][:, :], ACT.Relu, bias=cols[:, 1:2]).then_inc(s_b["r1"], 1)
                run_edges(act, edge)

            for c in range(NC):
                deviation(c, s_f)
                need(act, s_out[c % 2], 16 * (c // 2))
                scale_rows(c, s_f, xs[c % 2], yS[c % 2])

        @block.vector
        def _(dve):
            steps = [0]

            def settled(ins):
                steps[0] += 1
                ins.then_inc(s_own, 1)
                dve.wait_ge(s_own, steps[0])
            dve.memset(xN[:, NB - 1, :], 0.0).then_inc(s_fill, 1)
            settled(dve.memset(P4i[:, :, :], NO_NODE))
            dve.memset(D4i[:, 1, :], NO_NODE).then_inc(s_fill, 1)
            dve.memset(S4i[:, 1, :], 0).then_inc(s_fill, 1)
            dve.memset(P4i[0:1, 0, 0:1], -1).then_inc(s_fill, 1)
            dve.memset(T[W:P, 2 * NB - 1, :, :], 0.0).then_inc(s_fill, 1)
            dve.memset(front, -1.0).then_inc(s_fill, 1)
            dve.memset(back, -1.0).then_inc(s_fill, 1)
            dve.memset(xT[:, NB * C:NP], 0.0).then_inc(s_fill, 1)
            dve.memset(L[:, :, :], 0.0).then_inc(s_fill, 1)
            dve.memset(EXs[:, :, 0:1], 1.0).then_inc(s_fill, 1)
            dve.wait_ge(s_c, 5)
            dve.wait_ge(s_c2, 7)
            dve.tensor_copy(iotaF[:, :], iotaI[:, :])
            dve.tensor_copy(pF[:, :], pI[:, :])
            dve.wait_ge(s_e, 16 * 10)
            dve.tensor_copy(D4[:, :, :], D4i)
            dve.tensor_copy(S4[:, :, :], S4i)
            settled(dve.tensor_scalar(B64i[:, :], D4i[:, :, 0], -W, None, ALU.bitwise_and))
            settled(dve.tensor_copy(B64[:, :], B64i[:, :]))
            for k in range(2):
                dve.tensor_scalar(D128[:, k, :], D4[:, k, :], B64[:, k:k + 1], None, ALU.subtract)
                dve.tensor_scalar(DR[:, k, :], D4[:, k, :], D4[:, k, 0:1], None, ALU.subtract)
            dve.tensor_tensor(DS, P4i, D4i, ALU.subtract).then_inc(s_p, 1)

            dve.wait_ge(s_p, 1)
            dve.tensor_reduce(odd[0:QP, 0:1], DS.rearrange("p k e -> p (k e)"), AX.X, ALU.max)
            seen = P4i.bitcast(F32)
            settled(dve.scalar_tensor_tensor(out=seen, in0=D4, scalar=float(NO_NODE), in1=DR,
                                             op0=ALU.is_lt, op1=ALU.mult))
            dve.tensor_reduce(odd[0:QP, 1:2], seen.rearrange("p k e -> p (k e)"), AX.X, ALU.max)
            ends = msg[0:QP, 2 * QE:2 * QE + 8].rearrange("p (k t) -> p k t", k=2)
            settled(dve.tensor_tensor(ends, D4[:, :, 0:QE:P], D4[:, :, P - 1:QE:P], ALU.is_equal))
            settled(dve.scalar_tensor_tensor(out=ends, in0=D4[:, :, 0:QE:P], scalar=float(NO_NODE), in1=ends,
                                             op0=ALU.is_lt, op1=ALU.mult))
            settled(dve.tensor_reduce(odd[0:QP, 2:3], ends.rearrange("p k t -> p (k t)"), AX.X, ALU.max))
            dve.tensor_scalar(odd[0:QP, 0:1], odd[0:QP, 0:1], 0.0, None, ALU.is_gt)
            settled(dve.tensor_scalar(odd[0:QP, 1:2], odd[0:QP, 1:2], float(W - 1), None, ALU.is_gt))
            dve.tensor_reduce(odd[0:QP, 3:4], odd[0:QP, 0:3], AX.X, ALU.add).then_inc(s_odd_q, 1)
            dve.wait_ge(s_odd_s, 1)
            dve.tensor_copy(unusual[:, :], ps[5][0:1, 0:1]).then_inc(s_flag, 1)

            for i in range(4):
                lst, k = i // 2, i % 2
                to = (IDX, R64)[lst][:, k * QP * 4:(k + 1) * QP * 4].rearrange("p (q j) -> p j q", j=4)
                dve.wait_ge(s_et, i + 1)
                dve.tensor_copy(to, ps[6 + i % 2][:, 0:4 * QP].rearrange("p (j q) -> p j q", j=4)).then_inc(s_etc, 1)
            dve.wait_ge(s_col, 16 * 11)
            dve.tensor_scalar(Aw[:, :], Aw[:, :], cols[:, 0:1], None, ALU.mult)
            dve.wait_ge(s_row, 16)
            settled(dve.tensor_scalar(tabR[:, :], baseR[:, :], -W, None, ALU.bitwise_and))
            dve.tensor_scalar(tabR[:, :], tabR[:, :], 3.0 * C / W, None, ALU.mult).then_inc(s_tab, 1)

            def remainder(unit, r, blocks=UB):
                dve.wait_ge(s_h1, unit + 1)
                hj = HJ[r][:, 0:blocks * C].rearrange("p (b c) -> p b c", b=blocks)
                dve.tensor_tensor(hjr[:, r, 0:blocks, :], hj, unit_of(unit, 0, blocks),
                                  ALU.subtract).then_inc(s_hr, 1)

            def third_part(unit, r, blocks=UB):
                dve.wait_ge(s_h2, unit + 1)
                dve.tensor_tensor(unit_of(unit, 2, blocks), hjr[:, r, 0:blocks, :], unit_of(unit, 1, blocks),
                                  ALU.subtract).then_inc(s_h3, 1)
            for r in range(4):
                remainder(r, r)
                if r:
                    third_part(r - 1, r - 1)
            with dve.Fori(1, NU // 4) as k:
                for r in range(4):
                    remainder(4 * k + r, r)
                    third_part(4 * k + r - 1, (r - 1) % 4)
            remainder(NU, 0, 1)
            third_part(NU - 1, 3)
            third_part(NU, 0, 1)
            dve.wait_ge(s_sw, 16 * 6)
            dve.wait_ge(s_h3, NU + 1)
            dve.wait_ge(s_hh, NU + 1)
            dve.memset(acc[:, 0, :], 0.0).then_inc(s_zero, 1)
            dve.wait_ge(s_flag, 1)

            with dve.If(dve.value_load(unusual[0:1, 0:1], min_val=0, max_val=4 * P) > 0):
                dve.memset(acc[:, 1, :], 0.0).then_inc(s_zero, 1)
                dve.memset(ones, 1.0).then_inc(s_pre["ones"], 1)
                dve.tensor_copy(baseF, baseR[:, :]).then_inc(s_pre["base"], 1)
                dve.memset(msg[:, 0:NB * HEADS], -1e30).then_inc(s_pre["fill"], 1)
                dve.memset(R[:, C:C + 1], 1.0)
                dve.wait_ge(s_pre["dst"], 1)
                settled(dve.tensor_tensor(DSTf.rearrange("p (q j) -> p q j", j=4),
                                          ps[0][:, 0:NQ].unsqueeze(2).to_broadcast([P, NQ, 4]),
                                          R64[:, :].rearrange("p (q j) -> p q j", j=4), ALU.add))
                settled(dve.tensor_scalar(DSTf, DSTf, float(NODES), None, ALU.min))
                dve.tensor_scalar(DSTx, DSTf, float(NODES - 1), None, ALU.min)
                dve.tensor_copy(DSTi, DSTf).then_inc(s_pre["rows"], 1)

                def spread_destination(t, S):
                    dve.wait_ge(S["turn"], t + 1)
                    dve.tensor_copy(Dc, DSTf[:, bass.ds(t, 1)].to_broadcast([P, P])).then_inc(S["dc"], 1)
                    dve.wait_ge(S["dc"], t + 1)
                    dve.wait_ge(S["dt"], t + 1)
                with dve.Fori(0, NT) as t:
                    spread_destination(t, s_1)
                    dve.tensor_scalar(apart, ps[1][:, 0:P], Dc[:, 0:1], -BIG, ALU.not_equal,
                                      ALU.mult).then_inc(s_1["apart"], 1)
                    dve.wait_ge(s_1["v"], t + 1)
                    dve.tensor_tensor(uM, ps[2][:, 0:P], u3, ALU.max).then_inc(s_1["e"], 1)
                    dve.wait_ge(s_1["lc"], t + 1)
                    dve.tensor_copy(LB, LG[:, bass.ds(t * HEADS, HEADS)].unsqueeze(2).to_broadcast([P, HEADS, P])
                                    ).then_inc(s_1["lb"], 1)
                    dve.wait_ge(s_1["apart"], t + 1)
                    dve.wait_ge(s_1["lt"], t + 1)
                    for k in range(2):
                        ins = dve.tensor_tensor(LM[:, 4 * k:4 * k + 4, :],
                                                ps[4 + k][:, :].rearrange("p (h e) -> p h e", h=4),
                                                apart.unsqueeze(1).to_broadcast([P, 4, P]), ALU.add)
                    ins.then_inc(s_1["lm"], 1)
                    dve.wait_ge(s_1["lm"], t + 1)
                    dve.tensor_reduce(mTile, LM, AX.X, ALU.max).then_inc(s_1["tm"], 1)
                    dve.wait_ge(s_1["tm"], t + 1)
                    dve.wait_ge(s_1["rows"], 48 * (t + 1))
                    dve.tensor_tensor(mNew, mTile, mOld, ALU.max).then_inc(s_1["new"], 1)
                with dve.Fori(0, NT) as t:
                    spread_destination(t, s_2)
                    dve.tensor_scalar(same, ps[1][:, 0:P], Dc[:, 0:1], None, ALU.is_equal).then_inc(s_2["same"], 1)
                    dve.wait_ge(s_2["rows"], 48 * (t + 1))
                    dve.tensor_tensor(less, LG[:, bass.ds(t * HEADS, HEADS)], mOld, ALU.subtract).then_inc(s_2["less"], 1)
                    dve.wait_ge(s_2["ex"], t + 1)
                    dve.tensor_tensor(R[:, 0:C].rearrange("p (h c) -> p h c", h=HEADS),
                                      hiT.rearrange("p (h c) -> p h c", h=HEADS),
                                      R[:, C + 1:C + DC].unsqueeze(2).to_broadcast([P, HEADS, HC]),
                                      ALU.mult).then_inc(s_2["r"], 1)
                    dve.wait_ge(s_2["sum"], t + 1)
                    dve.tensor_tensor(newR, ps[0][:, 0:C + DC], oldR, ALU.add).then_inc(s_2["new"], 1)
                dve.wait_ge(s_2["turn"], NT + 1)
                dve.sem_inc(s_2["back"], 1)
                with dve.Fori(0, NB) as b:
                    dve.wait_ge(s_2["t"], b + 1)
                    dve.tensor_copy(accH[:, bass.ds(b * P, P)], ps[0][:, 0:P])
                    dve.tensor_copy(accD[:, bass.ds(b * P, P)], ps[1][0:DC, 0:P]).then_inc(s_2["back"], 1)
                dve.wait_ge(s_2["back"], NB + 1)
            with dve.Else():
                def block_onehot(f, s, n, j):
                    if j == 0:
                        dve.wait_ge(s_db[s], 16 * (n + 1))
                    need(dve, s_u, (f - 1) * GQ + j + 1)
                    dve.tensor_scalar(ohT[:, j, :], Dbc[:, s, j * QE:(j + 1) * QE], pF[:, 0:1], None,
                                      ALU.is_equal).then_inc(s_ohT, 1)
                for j in range(GQ):
                    block_onehot(0, 0, 0, j)

                def step(g, s, n):
                    f, b, p, nx = stage(g, 0), stage(g, 1), stage(g, 2), stage(g, -1)
                    nq = quads(f) if f is not None else 0
                    nxq = quads(nx) if nx is not None else 0

                    def leaky(j):
                        if j >= nq:
                            return
                        dve.wait_ge(s_v, f * GQ + j + 1)
                        need(dve, s_log, (f - 1) * GQ + j + 1)
                        dve.tensor_tensor(E[:, j, :], U[j][:, :], V[:, j, :], ALU.max).then_inc(s_lk, 1)

                    def add(j):
                        if p is None or j >= quads(p):
                            return
                        dve.wait_ge(s_agg, p * GQ + j + 1)
                        need(dve, s_acc, 2 * (p * GQ + j))
                        base = dve.value_load(baseR[0:1, bass.ds(p * GQ + j, 1)], min_val=0, max_val=NODES - 1)
                        w_ = acc[:, 0, bass.ds(base, W)]
                        dve.tensor_tensor(w_, AG[j % 2][:, 0:W], w_, ALU.add).then_inc(s_acc, 1)
                        w_ = accD[:, bass.ds(base, W)]
                        dve.tensor_tensor(w_, AG[j % 2][0:DC, W:2 * W], w_, ALU.add).then_inc(s_acc, 1)

                    def nxt(j):
                        if j < nxq:
                            block_onehot(nx, (s + 1) % RG, n + (s + 1) // RG, j)
                        if is_int(g) and g == 0:
                            dve.memset(acc[:, 1, j * NP // GQ:(j + 1) * NP // GQ], 0.0).then_inc(s_zero, 1)
                    leaky(0)
                    nxt(0)
                    if p is not None:
                        dve.wait_ge(s_exs, p + 1)
                        need(dve, s_agg, GQ * p)
                        cnt = quads(p) * 4
                        ex = EXp[:, HALO * HEADS:(HALO + cnt) * HEADS]
                        dve.tensor_tensor(msg[:, 0:cnt * C].rearrange("p (a c) -> p a c", c=HC),
                                          ex.unsqueeze(2).to_broadcast([P, cnt * HEADS, HC]),
                                          G[:, (s - 2) % RG, 0:cnt * C].rearrange("p (a c) -> p a c", c=HC),
                                          ALU.mult).then_inc(s_msg, 1)
                    leaky(1)
                    nxt(1)
                    if b is not None:
                        dve.wait_ge(s_mask, b + 1)
                        dve.wait_ge(s_lt, b + 1)
                        dve.tensor_tensor_scan(R1[:, :], link[:, 0:P], LTp[:, 0:P], -1e30, ALU.add,
                                               ALU.max).then_inc(s_r1, 1)
                    leaky(2)
                    add(0)
                    if b is not None:
                        dve.wait_ge(s_sh1, b + 1)
                        dve.tensor_tensor_scan(R2[:, :], link[:, 0:P], LTp[:, 0:P], shp[:, 0:1], ALU.add,
                                               ALU.max).then_inc(s_r2, 1)
                        dve.wait_ge(s_r2, b + 1)
                        dve.tensor_tensor_scan(R3[:, ::-1], link[:, P:0:-1], R2[:, ::-1], -1e30, ALU.add,
                                               ALU.max).then_inc(s_r3, 1)
                    nxt(2)
                    add(1)
                    if b is not None:
                        dve.wait_ge(s_sh2, b + 1)
                        dve.tensor_tensor_scan(R4[:, ::-1], link[:, P:0:-1], R2[:, ::-1], shp[:, 1:2], ALU.add,
                                               ALU.max).then_inc(s_r4, 1)
                        dve.wait_ge(s_r4, b + 1)
                        need(dve, s_exp, b)
                        dve.tensor_tensor(XM[:, :], LTp[:, 0:P], R4[:, :], ALU.subtract).then_inc(s_xm, 1)
                    add(2)
                    if b is not None:
                        need(dve, s_agg, GQ * b)
                        cnt = quads(b) * 4
                        dve.tensor_tensor(oh[:, 0:cnt * W].rearrange("p (t n) -> p t n", n=W),
                                          iotaF[:, :].unsqueeze(1).to_broadcast([P, cnt, W]),
                                          R64[:, bass.ds(b * GT, cnt)].unsqueeze(2).to_broadcast([P, cnt, W]),
                                          ALU.is_equal).then_inc(s_oh, 1)
                run_steps(dve, step)
                dve.wait_ge(s_acc, 2 * NQ)

            def moments(c, S):
                dve.wait_ge(S["xs"], c + 1)
                for i in range(NCH):
                    ins = dve.bn_stats(st[:, i, :], xs[c % 2][:, i, :])
                ins.then_inc(S["st"], 1)
                dve.wait_ge(S["st"], c + 1)
                need(dve, S["x1"], c - 1)
                for i in range(NCH):
                    ins = dve.bn_aggr(mv[:, c % 2, i, :], st[:, i, :])
                ins.then_inc(S["mv"], 1)
                dve.wait_ge(S["mv"], c + 1)
                dve.tensor_scalar(ve[:, c % 2, :], mv[:, c % 2, :, 1], EPS, None, ALU.add).then_inc(S["ve"], 1)

            def factors(c, S):
                dve.wait_ge(S["sd"], c + 1)
                dve.reciprocal(rs[:, c % 2, :], sd[:, c % 2, :]).then_inc(S["rs"], 1)
                dve.wait_ge(S["rs"], c + 1)
                dve.scalar_tensor_tensor(out=nm[:, c % 2, :], in0=mv[:, c % 2, :, 0], scalar=-1.0,
                                         in1=rs[:, c % 2, :], op0=ALU.mult, op1=ALU.mult).then_inc(S["nm"], 1)

            BANKS = ((0, 4), (4, NCH - 4))
            for c in range(NC + 2):
                if c < NC:
                    dve.wait_ge(s_m["gT"], c + 1)
                    dve.tensor_scalar(rd[:, :, :],
                                      ps[6][:, 0:NCH * DC].rearrange("p (b h) -> p b h", h=DC)[:, :, 1:DC],
                                      1e-30, None, ALU.max).then_inc(s_m["dmax"], 1)
                    dve.tensor_copy(count[:, c * NCH:(c + 1) * NCH],
                                    ps[6][:, 0:NCH * DC].rearrange("p (b h) -> p b h", h=DC)[:, :, 0])
                    dve.wait_ge(s_m["dmax"], c + 1)
                    dve.reciprocal(rd[:, :, :], rd[:, :, :]).then_inc(s_m["rd"], 1)
                    dve.wait_ge(s_m["rd"], c + 1)
                    need(dve, s_m["x1"], c - 1)
                    for k, (b0, n) in enumerate(BANKS):
                        ins = dve.tensor_tensor(
                            xs[c % 2][:, b0:b0 + n, :].rearrange("p b (h c) -> p (b h) c", c=HC),
                            ps[k][:, 0:n * C].rearrange("p (a c) -> p a c", c=HC),
                            rd[:, b0:b0 + n, :].rearrange("p b h -> p (b h)").unsqueeze(2)
                            .to_broadcast([P, n * HEADS, HC]), ALU.mult)
                    ins.then_inc(s_m["gat"], 1)
                    dve.wait_ge(s_m["gat"], c + 1)
                    dve.wait_ge(s_mx[c % 2], 16 * (c // 2 + 1) + 16 * (c == NC - 1))
                    dve.tensor_tensor(xs[c % 2], xs[c % 2], xc[c % 2], ALU.add).then_inc(s_m["xs"], 1)
                    moments(c, s_m)
                if c >= 2:
                    dve.wait_ge(s_m["y"], c - 1)
                    need(dve, s_yw[c % 2], 16 * ((c - 2) // 2))
                    for k, (b0, n) in enumerate(BANKS):
                        ins = dve.tensor_tensor(yS[c % 2][:, b0:b0 + n, :],
                                                ps[4 + k][:, 0:n * C].rearrange("p (b c) -> p b c", b=n),
                                                bn1B[:, :].unsqueeze(1).to_broadcast([P, n, C]), ALU.add)
                    ins.then_inc(s_m["ys"], 1)
                if c < NC:
                    factors(c, s_m)

            def add_shares(b):
                dve.tensor_scalar(share, bn2B[:, :], count[:, bass.ds(b, 1)], None,
                                  ALU.mult).then_inc(s_share, 1)
                dve.wait_ge(s_share, b + 1)
                row = X1[:, bass.ds(b, 1), :].rearrange("p b c -> p (b c)")
                dve.scalar_tensor_tensor(out=row, in0=row, scalar=2.0, in1=share, op0=ALU.mult,
                                         op1=ALU.add).then_inc(s_x2, 1)
            dve.memset(accH, 0.0).then_inc(s_m["cl"], 1)
            dve.wait_ge(s_m["cl"], 1)

            with dve.If(dve.value_load(unusual[0:1, 0:1], min_val=0, max_val=4 * P) > 0):
                with dve.Fori(0, NT) as t:
                    spread_destination(t, s_3)
                    dve.tensor_scalar(same, ps[1][:, 0:P], Dc[:, 0:1], None, ALU.is_equal).then_inc(s_3["same"], 1)
                    dve.wait_ge(s_3["t"], t + 1)
                    dve.tensor_copy(atT, ps[0][0:EC, 0:P]).then_inc(s_3["tc"], 1)
                    dve.wait_ge(s_3["ef"], t + 1)
                    dve.wait_ge(s_3["tw"], t + 1)
                    dve.scalar_tensor_tensor(out=efT, in0=ps[3][:, 0:P], scalar=cols[:, 2:3], in1=twT,
                                             op0=ALU.add, op1=ALU.mult).then_inc(s_3["efs"], 1)
                    dve.wait_ge(s_3["z"], t + 1)
                    dve.wait_ge(s_3["rows"], 32 * (t + 1))
                    dve.tensor_tensor(zR, ps[4][:, 0:C], hiT, ALU.add).then_inc(s_3["zs"], 1)
                    dve.wait_ge(s_3["sum"], t + 1)
                    dve.tensor_tensor(newR[:, 0:C], ps[5][:, 0:C], oldR[:, 0:C], ALU.add).then_inc(s_3["new"], 1)
                with dve.Fori(0, NB) as b:
                    add_shares(b)
                    dve.wait_ge(s_x2, b + 1)
                dve.wait_ge(s_3["turn"], NT + 1)
                dve.sem_inc(s_3["back"], 1)
                with dve.Fori(0, NB) as b:
                    dve.wait_ge(s_3["bt"], b + 1)
                    dve.tensor_copy(accH[:, bass.ds(b * P, P)], ps[0][:, 0:P]).then_inc(s_3["back"], 1)
            with dve.Else():
                def edge(q, r, k):
                    g4, z, e = later(q, 4), later(q, 3), later(q, 2)
                    t = later(q, 0)
                    if g4 is not None:
                        dve.wait_ge(s_b["agg"], g4 + 1)
                        need(dve, s_b["acc"], g4)
                        base = dve.value_load(baseR[0:1, bass.ds(g4, 1)], min_val=0, max_val=NODES - 1)
                        w_ = accH[:, bass.ds(base, W)]
                        dve.tensor_tensor(w_, ps[4][:, 0:W], w_, ALU.add).then_inc(s_b["acc"], 1)
                    if z is not None:
                        rr, kk = slot(r, k, 3)
                        dve.wait_ge(s_gy[rr], 64 * (kk + 1))
                        dve.wait_ge(s_b["z"], z + 1)
                        need(dve, s_b["h"], z)
                        dve.tensor_tensor(zS, ps[3][:, :], Yb[:, rr, :], ALU.add).then_inc(s_b["zs"], 1)
                        need(dve, s_b["agg"], z)
                        dve.tensor_tensor(ohB.rearrange("p (t n) -> p t n", n=W),
                                          iotaF[:, :].unsqueeze(1).to_broadcast([P, 4, W]),
                                          R64[:, bass.ds(z * 4, 4)].unsqueeze(2).to_broadcast([P, 4, W]),
                                          ALU.is_equal).then_inc(s_b["oh"], 1)
                    if e is not None:
                        dve.wait_ge(s_b["ef"], e + 1)
                        dve.wait_ge(s_b["tw"], e + 1)
                        need(dve, s_b["z"], e)
                        dve.scalar_tensor_tensor(out=efS, in0=ps[2][:, :], scalar=cols[:, 2:3], in1=twS,
                                                 op0=ALU.add, op1=ALU.mult).then_inc(s_b["efs"], 1)
                    if t is not None:
                        dve.wait_ge(s_b["at"], t + 1)
                        need(dve, s_b["h1"], t)
                        dve.tensor_copy(atS, ps[0][0:EC, :]).then_inc(s_b["atc"], 1)
                    if not is_int(q) and r == 0:
                        add_shares(k - 2)
                    if is_int(q) and q == NQ - 2:
                        dve.wait_ge(s_b["tw"], NQ - RB)
                        dve.memset(atB[:, RB - 1, :], 0.0)
                        dve.memset(ewB[:, RB - 1, :], 0.0).then_inc(s_b["cl"], 1)
                run_edges(dve, edge)

            dve.wait_ge(s_x2, NB)
            for c in range(NC + 1):
                if c < NC:
                    dve.wait_ge(s_f["o"], c + 1)
                    need(dve, s_f["x1"], c - 1)
                    for k, (b0, n) in enumerate(BANKS):
                        ins = dve.tensor_tensor(
                            xs[c % 2][:, b0:b0 + n, :].rearrange("p b c -> p (b c)"),
                            X1[:, c * NCH + b0:c * NCH + b0 + n, :].rearrange("p b c -> p (b c)"),
                            ps[2 * (c % 2) + k][:, 0:n * C], ALU.add)
                    ins.then_inc(s_f["xs"], 1)
                    moments(c, s_f)
                    factors(c, s_f)

        @block.tensor
        def _(pe):
            pe.wait_ge(s_c, 5)
            for c in range(NC):
                pe.wait_ge(s_x[c], 16 * (1 + (c == NC - 1)))
                need(pe, s_xtc, 2 * (c - 1))
                for i in range(NCH):
                    ins = pe.transpose(ps[2 * (c % 2) + i // 4][:, (i % 4) * P:(i % 4 + 1) * P],
                                       xN[:, c * NCH + i, :], ident[:, :])
                ins.then_inc(s_xt, 1)
            pe.wait_ge(s_xtc, 2 * NC)
            pe.wait_ge(s_fill, 10)
            pe.wait_ge(s_w, 32)

            def project(unit, banks, turns, half, copied, done):
                need(pe, copied, unit - turns + 1)
                for b in range(unit * UB, min((unit + 1) * UB, NB)):
                    c0 = b % UB * C
                    ins = pe.matmul(banks[unit % turns][:, c0:c0 + C], xT[:, b * C:(b + 1) * C],
                                    W12[:, half * C:(half + 1) * C], start=True, stop=True)
                ins.then_inc(done, 1)
            for u in range(NU + 1):
                project(u, ps[2:2 + HR], HR, 0, s_hic, s_hp)
            pe.wait_ge(s_odd_q, 1)
            pe.matmul(ps[5][0:1, 0:1], odd[0:QP, 3:4], iotaF[0:QP, 1:2], start=True, stop=True).then_inc(s_odd_s, 1)
            for i in range(4):
                lst, k = i // 2, i % 2
                need(pe, s_etc, i - 1)
                for j in range(4):
                    ins = pe.transpose(ps[6 + i % 2][:, j * QP:(j + 1) * QP],
                                       (S4, DR)[lst][:, k, j * P:(j + 1) * P], ident[0:QP, 0:QP])
                ins.then_inc(s_et, 1)
            pe.wait_ge(s_flag, 1)
            for u in range(NU + 1):
                if u == 3:
                    pe.wait_ge(s_hic, NU + 1)
                project(u, HJ, 4, 1, s_hr, s_hh)
            pe.wait_ge(s_hr, NU + 1)

            with pe.If(pe.value_load(unusual[0:1, 0:1], min_val=0, max_val=4 * P) > 0):
                pe.wait_ge(s_pre["ones"], 1)
                pe.wait_ge(s_pre["base"], 1)
                pe.matmul(ps[0][:, 0:NQ], ones, baseF, start=True, stop=True).then_inc(s_pre["dst"], 1)

                def turn_destination(t, S):
                    pe.wait_ge(S["dc"], t + 1)
                    passed(pe, "pe")
                    pe.transpose(ps[1][:, 0:P], Dc, ident[:, :]).then_inc(S["dt"], 1)
                with pe.Fori(0, NT) as t:
                    turn_destination(t, s_1)
                    pe.wait_ge(s_1["rows"], 48 * (t + 1))
                    passed(pe, "pe")
                    pe.transpose(ps[0][:, 0:P], xR, ident[:, :]).then_inc(s_1["xt"], 1)
                    pe.wait_ge(s_1["xc"], t + 1)
                    passed(pe, "pe")
                    pe.matmul(ps[2][:, 0:P], hiT, ident[:, :], is_transpose=True, start=True, stop=False,
                              skip_group_check=True)
                    pe.matmul(ps[2][:, 0:P], W12[:, C:2 * C], xRT, start=False, stop=True,
                              skip_group_check=True).then_inc(s_1["u"], 1)
                    pe.wait_ge(s_1["e"], t + 1)
                    passed(pe, "pe")
                    pe.matmul(ps[3][:, 0:HEADS], uM, Aw[:, :], start=True, stop=True).then_inc(s_1["log"], 1)
                    pe.wait_ge(s_1["lb"], t + 1)
                    passed(pe, "pe")
                    for h in range(HEADS):
                        ins = pe.transpose(ps[4 + h // 4][:, h % 4 * P:(h % 4 + 1) * P], LB[:, h, :], ident[:, :])
                    ins.then_inc(s_1["lt"], 1)
                with pe.Fori(0, NT) as t:
                    turn_destination(t, s_2)
                    pe.wait_ge(s_2["same"], t + 1)
                    pe.wait_ge(s_2["r"], t + 1)
                    passed(pe, "pe")
                    pe.matmul(ps[0][:, 0:C + DC], same, R, start=True, stop=True).then_inc(s_2["sum"], 1)
                with pe.Fori(0, NB) as b:
                    pe.wait_ge(s_2["loaded"], 16 * (b + 1))
                    passed(pe, "pe")
                    pe.transpose(ps[0][:, 0:P], oldR[:, 0:C], ident[:, :])
                    pe.matmul(ps[1][0:DC, 0:P], oldR[:, C:C + DC], ident[:, :], start=True, stop=True
                              ).then_inc(s_2["t"], 1)
                pe.wait_ge(s_2["back"], NB + 1)
            with pe.Else():
                def step(g, s, n):
                    f, b, p = stage(g, 0), stage(g, 1), stage(g, 2)
                    nq = quads(f) if f is not None else 0

                    def sums(j, of=None, lj=0):
                        if j >= nq:
                            logits(of, lj)
                            return
                        lone = of is None or lj >= quads(of)
                        if not lone:
                            pe.wait_ge(s_lk, of * GQ + lj + 1)
                            need(pe, s_lc, of * GQ + lj)
                        pe.wait_ge(s_g[s][j], 64 * (n + 1))
                        q = f * GQ + j
                        pe.wait_ge(s_ohT, q + 1)
                        need(pe, s_lk, (f - 1) * GQ + j + 1)
                        col = pe.value_load(tabR[0:1, bass.ds(q, 1)], min_val=0, max_val=(2 * NB - 1) * 3 * C)
                        for i in range(4):
                            t = 4 * j + i
                            pe.matmul(U[j][:, i * P:(i + 1) * P], G[:, s, t * C:(t + 1) * C], ident[:, :],
                                      is_transpose=True, start=(i == 0), stop=False, skip_group_check=True)
                            if not lone:
                                ins = logit(lj, i)
                        if not lone:
                            ins.then_inc(s_log, 1)
                        for part in range(3):
                            ins = pe.matmul(U[j][:, :], flatT[:, bass.ds(col + part * C, C)], ohT[:, j, :],
                                            start=False, stop=(part == 2), skip_group_check=True)
                        ins.then_inc(s_u, 1)

                    def logit(j, i):
                        c0 = j * 32 + i * HEADS
                        return pe.matmul(Lp[:, c0:c0 + HEADS], E[:, j, i * P:(i + 1) * P], Aw[:, :],
                                         start=True, stop=True)

                    def logits(of, j):
                        if of is None or j >= quads(of):
                            return
                        pe.wait_ge(s_lk, of * GQ + j + 1)
                        need(pe, s_lc, of * GQ + j)
                        for i in range(4):
                            ins = logit(j, i)
                        ins.then_inc(s_log, 1)

                    def aggregate(j):
                        if p is None or j >= quads(p):
                            return
                        if j == 0:
                            pe.wait_ge(s_oh, p + 1)
                            pe.wait_ge(s_msg, p + 1)
                            pe.wait_ge(s_exs, p + 1)
                        need(pe, s_acc, 2 * (p * GQ + j - (j > 0)))
                        for i in range(4):
                            t = 4 * j + i
                            pe.matmul(AG[j % 2][:, 0:W], msg[:, t * C:(t + 1) * C], oh[:, t * W:(t + 1) * W],
                                      start=(i == 0), stop=(i == 3))
                        for i in range(4):
                            t = 4 * j + i
                            ins = pe.matmul(AG[j % 2][0:DC, W:2 * W], EXs[:, t, :],
                                            oh[:, t * W:(t + 1) * W], start=(i == 0), stop=(i == 3))
                        ins.then_inc(s_agg, 1)
                    sums(0, b, 2)
                    if p is not None:
                        pe.wait_ge(s_exp, p + 1)
                        need(pe, s_msg, p)
                        pe.transpose(EXp[:, 0:P], EXT[:, :], ident[:, :]).then_inc(s_ext, 1)
                    bs, bn_ = (s - 1) % RG, n + (s - 1) // RG
                    if b is not None:
                        pe.wait_ge(s_ds[bs], 16 * (bn_ + 1))
                        need(pe, s_xm, b)
                        pe.matmul(LTp[:, P:2 * P + 1], X16[:, :], Dsc[:, bs, :], start=True, stop=True).then_inc(s_lx, 1)
                    sums(1)
                    logits(f, 0)
                    sums(2)
                    if b is not None:
                        last = is_int(b) and b == NG - 1
                        pe.wait_ge(s_lc, NQ if last else (b + 1) * GQ + 1)
                        pe.wait_ge(s_mask, b + 1)
                        pe.transpose(LTp[:, 0:P], L[:, bs, :], ident[:, :]).then_inc(s_lt, 1)
                    aggregate(0)
                    if b is not None:
                        pe.wait_ge(s_r1, b + 1)
                        need(pe, s_msg, b)
                        pe.matmul(shp[:, 0:1], down[:, :], R1[:, P - 1:P], start=True, stop=True).then_inc(s_sh1, 1)
                    logits(f, 1)
                    aggregate(1)
                    if b is not None:
                        pe.wait_ge(s_r3, b + 1)
                        pe.matmul(shp[:, 1:2], up[:, :], R3[:, 0:1], start=True, stop=True).then_inc(s_sh2, 1)
                    aggregate(2)
                pe.wait_ge(s_tab, 1)
                pe.wait_ge(s_odd, 96)
                flatT = T[:, :, :, :].rearrange("p b k c -> p (b k c)")
                run_steps(pe, step)
                pe.wait_ge(s_acc, 2 * NQ)


            def bank(first, i):
                return ps[first + i // 4][:, (i % 4) * P:(i % 4 + 1) * P]
            for c in range(NC + 2):
                if c < NC:
                    need(pe, s_m["gat"], c)
                    for i in range(NCH):
                        n0 = (c * NCH + i) * P
                        pe.transpose(bank(0, i), accH[:, n0:n0 + P], ident[:, :])
                        ins = pe.transpose(ps[6][:, i * DC:(i + 1) * DC], accD[:, n0:n0 + P], ident[0:DC, 0:DC])
                    ins.then_inc(s_m["gT"], 1)
                if c >= 2:
                    pe.wait_ge(s_m["xTc"], 2 * (c - 1))
                    need(pe, s_m["ys"], c - 2)
                    for i in range(NCH):
                        ins = pe.matmul(bank(4, i), x1T[:, i * C:(i + 1) * C], wN1[:, 0, :], start=True, stop=True)
                    ins.then_inc(s_m["y"], 1)
                if 1 <= c <= NC:
                    pe.wait_ge(s_m["x1"], c)
                    need(pe, s_m["xTc"], 2 * (c - 1))
                    for i in range(NCH):
                        ins = pe.transpose(bank(2, i), X1[:, (c - 1) * NCH + i, :], ident[:, :])
                    ins.then_inc(s_m["xT"], 1)

            with pe.If(pe.value_load(unusual[0:1, 0:1], min_val=0, max_val=4 * P) > 0):
                with pe.Fori(0, NT) as t:
                    turn_destination(t, s_3)
                    pe.wait_ge(s_3["at"], 16 * (t + 1))
                    passed(pe, "pe")
                    pe.transpose(ps[0][0:EC, 0:P], at0, ident[:, :]).then_inc(s_3["t"], 1)
                    pe.wait_ge(s_3["tc"], t + 1)
                    passed(pe, "pe")
                    pe.matmul(ps[2][:, 0:P], wE1[:, :], atT, start=True, stop=True).then_inc(s_3["h1"], 1)
                    pe.wait_ge(s_3["r1"], t + 1)
                    passed(pe, "pe")
                    pe.matmul(ps[3][:, 0:P], wE2[:, :], r1T, start=True, stop=True).then_inc(s_3["ef"], 1)
                    pe.wait_ge(s_3["efs"], t + 1)
                    passed(pe, "pe")
                    pe.matmul(ps[4][:, 0:C], efT, wN1[:, 1, :], start=True, stop=True).then_inc(s_3["z"], 1)
                    pe.wait_ge(s_3["same"], t + 1)
                    pe.wait_ge(s_3["h"], t + 1)
                    passed(pe, "pe")
                    pe.matmul(ps[5][:, 0:C], same, hR, start=True, stop=True).then_inc(s_3["sum"], 1)
                with pe.Fori(0, NB) as b:
                    pe.wait_ge(s_3["loaded"], 16 * (b + 1))
                    passed(pe, "pe")
                    pe.transpose(ps[0][:, 0:P], oldR[:, 0:C], ident[:, :]).then_inc(s_3["bt"], 1)
                pe.wait_ge(s_3["back"], NB + 1)
            with pe.Else():
                def edge(q, r, k):
                    g4, z, e, h, t = (later(q, lag) for lag in (4, 3, 2, 1, 0))
                    if g4 is not None:
                        pe.wait_ge(s_b["h"], g4 + 1)
                        pe.wait_ge(s_b["oh"], g4 + 1)
                        need(pe, s_b["acc"], g4)
                        for i in range(4):
                            ins = pe.matmul(ps[4][:, 0:W], hS[:, i * C:(i + 1) * C], ohB[:, i * W:(i + 1) * W],
                                            start=(i == 0), stop=(i == 3))
                        ins.then_inc(s_b["agg"], 1)
                    if z is not None:
                        pe.wait_ge(s_b["efs"], z + 1)
                        need(pe, s_b["zs"], z)
                        for i in range(4):
                            ins = pe.matmul(ps[3][:, i * C:(i + 1) * C], efS[:, i * P:(i + 1) * P], wN1[:, 1, :],
                                            start=True, stop=True)
                        ins.then_inc(s_b["z"], 1)
                    if e is not None:
                        pe.wait_ge(s_b["r1"], e + 1)
                        need(pe, s_b["efs"], e)
                        pe.matmul(ps[2][:, :], wE2[:, :], r1S, start=True, stop=True).then_inc(s_b["ef"], 1)
                    if h is not None:
                        pe.wait_ge(s_b["atc"], h + 1)
                        need(pe, s_b["r1"], h)
                        pe.matmul(ps[1][:, :], wE1[:, :], atS, start=True, stop=True).then_inc(s_b["h1"], 1)
                    if t is not None:
                        last = is_int(t) and t == NQ - 1
                        pe.wait_ge(s_at[r], 16 * (k + 1) + 16 * last)
                        need(pe, s_b["atc"], t)
                        passed(pe, "pe")
                        for i in range(4):
                            ins = pe.transpose(ps[0][0:EC, i * P:(i + 1) * P], atB[:, r, i * EC:(i + 1) * EC],
                                               ident[:, :])
                        ins.then_inc(s_b["at"], 1)
                run_edges(pe, edge)
                pe.wait_ge(s_b["acc"], NQ)

            for c in range(NC):
                need(pe, s_f["xs"], c - 1)
                for i in range(NCH):
                    n0 = (c * NCH + i) * P
                    ins = pe.matmul(bank(2 * (c % 2), i), accH[:, n0:n0 + P], wN2[:, :], start=True, stop=True)
                ins.then_inc(s_f["o"], 1)


_INS = ["x", "src", "dst", "edge_attr_64", "edge_weight", "L0_gnn_w1", "L0_gnn_w2", "L0_gnn_a", "L1_gnn_We1",
        "L1_gnn_be1", "L1_gnn_We2", "L1_gnn_be2", "L1_gnn_Wt", "L1_gnn_bt", "L1_gnn_Wn1", "L1_gnn_bn1",
        "L1_gnn_Wn2", "L1_gnn_bn2"]


def kernel(**inputs):
    import numpy as np
    import concourse.bacc as bacc
    from concourse.bass_utils import run_bass_kernel_spmd as run

    nc = bacc.Bacc("TRN2", target_bir_lowering=False, num_devices=1)
    arrays, args = {}, []
    for name in _INS:
        v = np.ascontiguousarray(inputs[name])
        arrays[f"in_{name}"] = v
        args.append(nc.dram_tensor(f"in_{name}", v.shape, mybir.dt.from_np(v.dtype), kind="ExternalInput").ap())
    hi_d = nc.dram_tensor("hi_rows", (NB * P, C), F32, kind="Internal").ap()
    y_d = nc.dram_tensor("y_rows", (NB * P, C), F32, kind="Internal").ap()
    rel_d = nc.dram_tensor("block_destinations", (NQ * QE,), BF16, kind="Internal").ap()
    scan_d = nc.dram_tensor("scan_destinations", (HALO * P + NQ * QE + 16 * P,), F32, kind="Internal").ap()
    out = nc.dram_tensor("out", (NODES, C), F32, kind="ExternalOutput").ap()
    max_d = nc.dram_tensor("segment_maxima", (NB * P, HEADS), F32, kind="Internal").ap()
    sum_d = nc.dram_tensor("attention_sums", (NB * P, C + DC), F32, kind="Internal").ap()
    agg_d = nc.dram_tensor("message_sums", (NB * P, C), F32, kind="Internal").ap()
    build(nc, *args, hi_d, y_d, rel_d, scan_d, max_d, sum_d, agg_d, out)
    r = run(nc, [arrays], core_ids=[0])
    return r.results[0]["out"]
```
